# Optimizing a Trainium2 kernel written in Bass

```python
import numpy as np
import jax
import jax.numpy as jnp

def _softmax(x, axis=-1):
    return jax.nn.softmax(x, axis=axis)

def _gelu(x):
    return jax.nn.gelu(x, approximate=True)

def _silu(x):
    return jax.nn.silu(x)

def _sigmoid(x):
    return jax.nn.sigmoid(x)

def _layernorm(x, axis=-1, eps=1e-05):
    m = jnp.mean(x, axis=axis, keepdims=True)
    v = jnp.var(x, axis=axis, keepdims=True)
    return (x - m) / jnp.sqrt(v + eps)

def _scatter_add(tgt, idx, src, axis=0):
    return tgt.at[idx].add(src)

def _segment_sum(src, seg, n):
    return jax.ops.segment_sum(src, seg, n)
kernel_name = 'mk_seq_postln_d1_jaxref_r4_7253f3'

def setup_inputs(seed: int=0):
    np.random.seed(seed)
    _w = jnp.asarray

    def _L0_attn_setup():
        import jax, jax.numpy as jnp
        import numpy as np
        B, N, C, H = (4, 2048, 256, 16)
        D = C // H
        EPS = 1e-05
        key = jax.random.key(seed)
        ks = jax.random.split(key, 10)
        s = 1.0 / np.sqrt(C)
        return {'x': jax.random.normal(ks[0], (B, N, C), jnp.float32), 'Wq': jax.random.uniform(ks[1], (C, C), jnp.float32, -s, s), 'bq': jax.random.uniform(ks[2], (C,), jnp.float32, -s, s), 'Wk': jax.random.uniform(ks[3], (C, C), jnp.float32, -s, s), 'bk': jax.random.uniform(ks[4], (C,), jnp.float32, -s, s), 'Wv': jax.random.uniform(ks[5], (C, C), jnp.float32, -s, s), 'bv': jax.random.uniform(ks[6], (C,), jnp.float32, -s, s), 'Wo': jax.random.uniform(ks[7], (C, C), jnp.float32, -s, s), 'bo': jax.random.uniform(ks[8], (C,), jnp.float32, -s, s), 'ln_g': jnp.ones((C,), jnp.float32), 'ln_b': jnp.zeros((C,), jnp.float32)}
    _L0_attn_in = _L0_attn_setup()

    def _L0_ffn_setup():
        import jax, jax.numpy as jnp
        import numpy as np
        LN_EPS = 1e-05

        def layer_norm(x, g, b):
            mu = jnp.mean(x, axis=-1, keepdims=True)
            var = jnp.mean(jnp.square(x - mu), axis=-1, keepdims=True)
            return (x - mu) * jax.lax.rsqrt(var + LN_EPS) * g + b

        def ternary_quant(w):
            scale = 1.0 / jnp.clip(jnp.mean(jnp.abs(w)), 1e-05)
            wq = jnp.clip(jnp.round(w * scale), -1.0, 1.0) / scale
            return w + jax.lax.stop_gradient(wq - w)
        key = jax.random.key(seed)
        ks = jax.random.split(key, 3)
        dim, hidden = (256, 1024)
        B, S = (8, 256)
        x = jax.random.normal(ks[0], (B, S, dim), dtype=jnp.float32)
        w1 = jax.random.normal(ks[1], (hidden, dim), dtype=jnp.float32) * 0.02
        w2 = jax.random.normal(ks[2], (dim, hidden), dtype=jnp.float32) * 0.02
        return {'x': x, 'ln1_g': jnp.ones((dim,), jnp.float32), 'ln1_b': jnp.zeros((dim,), jnp.float32), 'w1': w1, 'b1': jnp.zeros((hidden,), jnp.float32), 'ln2_g': jnp.ones((hidden,), jnp.float32), 'ln2_b': jnp.zeros((hidden,), jnp.float32), 'w2': w2, 'b2': jnp.zeros((dim,), jnp.float32)}
    _L0_ffn_in = _L0_ffn_setup()
    _d = {'L0_attn_x': _L0_attn_in['x'], 'L0_attn_Wq': _L0_attn_in['Wq'], 'L0_attn_bq': _L0_attn_in['bq'], 'L0_attn_Wk': _L0_attn_in['Wk'], 'L0_attn_bk': _L0_attn_in['bk'], 'L0_attn_Wv': _L0_attn_in['Wv'], 'L0_attn_bv': _L0_attn_in['bv'], 'L0_attn_Wo': _L0_attn_in['Wo'], 'L0_attn_bo': _L0_attn_in['bo'], 'L0_attn_ln_g': _L0_attn_in['ln_g'], 'L0_attn_ln_b': _L0_attn_in['ln_b'], 'L0_ffn_ln1_g': _L0_ffn_in['ln1_g'], 'L0_ffn_ln1_b': _L0_ffn_in['ln1_b'], 'L0_ffn_w1': _L0_ffn_in['w1'], 'L0_ffn_b1': _L0_ffn_in['b1'], 'L0_ffn_ln2_g': _L0_ffn_in['ln2_g'], 'L0_ffn_ln2_b': _L0_ffn_in['ln2_b'], 'L0_ffn_w2': _L0_ffn_in['w2'], 'L0_ffn_b2': _L0_ffn_in['b2']}
    _x0 = _d['L0_attn_x']
    _d['L0_attn_x'] = jax.random.normal(jax.random.fold_in(jax.random.key(seed), 1), (8, 1024, 256), dtype=_x0.dtype)
    del _x0
    return _d

def reference(L0_attn_x, L0_attn_Wq, L0_attn_bq, L0_attn_Wk, L0_attn_bk, L0_attn_Wv, L0_attn_bv, L0_attn_Wo, L0_attn_bo, L0_attn_ln_g, L0_attn_ln_b, L0_ffn_ln1_g, L0_ffn_ln1_b, L0_ffn_w1, L0_ffn_b1, L0_ffn_ln2_g, L0_ffn_ln2_b, L0_ffn_w2, L0_ffn_b2):

    def _L0_attn_ref(x, Wq, bq, Wk, bk, Wv, bv, Wo, bo, ln_g, ln_b):
        import jax, jax.numpy as jnp
        import numpy as np
        B, N, C, H = (4, 2048, 256, 16)
        D = C // H
        EPS = 1e-05
        b, n, c = x.shape
        q = x @ Wq.T + bq
        k = x @ Wk.T + bk
        v = x @ Wv.T + bv
        split = lambda z: z.reshape(b, n, H, D).transpose(0, 2, 1, 3)
        q, k, v = (split(q), split(k), split(v))
        q = jax.nn.softmax(q, axis=-1)
        k = jax.nn.softmax(k, axis=-2)
        state = jnp.einsum('bhnd,bhne->bhde', k, v)
        out = jnp.einsum('bhnd,bhde->bhne', q, state)
        out = out.transpose(0, 2, 1, 3).reshape(b, n, c)
        mu = out.mean(-1, keepdims=True)
        var = out.var(-1, keepdims=True)
        out = (out - mu) * jax.lax.rsqrt(var + EPS) * ln_g + ln_b
        return out @ Wo.T + bo

    def _L0_ffn_ref(x, ln1_g, ln1_b, w1, b1, ln2_g, ln2_b, w2, b2):
        import jax, jax.numpy as jnp
        import numpy as np
        LN_EPS = 1e-05

        def layer_norm(x, g, b):
            mu = jnp.mean(x, axis=-1, keepdims=True)
            var = jnp.mean(jnp.square(x - mu), axis=-1, keepdims=True)
            return (x - mu) * jax.lax.rsqrt(var + LN_EPS) * g + b

        def ternary_quant(w):
            scale = 1.0 / jnp.clip(jnp.mean(jnp.abs(w)), 1e-05)
            wq = jnp.clip(jnp.round(w * scale), -1.0, 1.0) / scale
            return w + jax.lax.stop_gradient(wq - w)
        h = layer_norm(x, ln1_g, ln1_b)
        h = jnp.einsum('bsd,hd->bsh', h, ternary_quant(w1)) + b1
        h = jax.nn.gelu(h, approximate=False)
        h = layer_norm(h, ln2_g, ln2_b)
        out = jnp.einsum('bsh,dh->bsd', h, ternary_quant(w2)) + b2
        return out
    x = L0_attn_x
    x = _layernorm(x + _L0_attn_ref(x, L0_attn_Wq, L0_attn_bq, L0_attn_Wk, L0_attn_bk, L0_attn_Wv, L0_attn_bv, L0_attn_Wo, L0_attn_bo, L0_attn_ln_g, L0_attn_ln_b), axis=-1)
    x = _layernorm(x + _L0_ffn_ref(x, L0_ffn_ln1_g, L0_ffn_ln1_b, L0_ffn_w1, L0_ffn_b1, L0_ffn_ln2_g, L0_ffn_ln2_b, L0_ffn_w2, L0_ffn_b2), axis=-1)
    return x

_drawn_inputs = setup_inputs


def setup_inputs(seed=0):
    import zlib

    import numpy as np

    out = dict(_drawn_inputs(seed))
    spreads = {'L0_attn_ln_g': (1.0, 0.2),
     'L0_attn_ln_b': (0.0, 0.1),
     'L0_ffn_ln1_g': (1.0, 0.2),
     'L0_ffn_ln1_b': (0.0, 0.1),
     'L0_ffn_b1': (0.0, 0.1),
     'L0_ffn_ln2_g': (1.0, 0.2),
     'L0_ffn_ln2_b': (0.0, 0.1),
     'L0_ffn_b2': (0.0, 0.1)}
    factors = {'L0_attn_bq': 8.0, 'L0_attn_bk': 8.0}
    for name, (base, spread) in spreads.items():
        noise = np.random.default_rng([zlib.crc32(name.encode()), seed]).standard_normal(out[name].shape)
        drawn = base * np.exp(spread * noise) if base else spread * noise
        out[name] = jnp.asarray(drawn.astype(out[name].dtype))
    for name, factor in factors.items():
        out[name] = (out[name] * factor).astype(out[name].dtype)
    return out
```

```python
from contextlib import ExitStack

import numpy as np

import concourse.bass as bass
from concourse import mybir

F32 = mybir.dt.float32
F32R = mybir.dt.float32r
ALU = mybir.AluOpType
ACT = mybir.ActivationFunctionType
AX_X = mybir.AxisListType.X

P = 128
EPS = 1e-5

VEC = {}
_at = 0
for _name, _n in (("bk", 2), ("ln_g", 2), ("ln_b", 2), ("ln1_g", 2), ("ln1_b", 2),
                  ("b1", 8), ("ln2_g", 8), ("ln2_b", 8)):
    VEC[_name] = (_at, _n)
    _at += _n
NVEC = _at
ROW = {"bq": 0, "bv": 1, "bo": 2, "b2": 3}


def wait_for(eng, semaphore, count):
    if not isinstance(count, int) or count > 0:
        eng.wait_ge(semaphore, count)


def attention_phase(nc, x_tok, x_chan, wq, wk, wv, wo, vecs_d, rows_d, ident_d, mask_d, x1_scratch):
    NB, _, T, C = x_tok.shape
    N = T * P
    CH = C // P
    D = 16
    HEADS = C // D
    PAIRS = T // 2
    GROUP = 4
    NG = T // GROUP
    RW = C + P
    assert NB % 2 == 0 and CH == 2 and T == 8

    with ExitStack() as ctx:
        def sb(name, shape, dt=F32):
            return ctx.enter_context(nc.sbuf_tensor(name, shape, dt))

        def sem(name):
            return ctx.enter_context(nc.semaphore(name))

        ring = ctx.enter_context(nc.psum_tensor("ring", [P, 4, 512], F32))
        qps = ctx.enter_context(nc.psum_tensor("qps", [P, 2, 512], F32))
        stA = ctx.enter_context(nc.psum_tensor("stA", [P, 512], F32))
        stB = ctx.enter_context(nc.psum_tensor("stB", [P, 512], F32))

        xt = sb("xt", [P, 2, T, C])
        xc = sb("xc", [P, 2, CH, N])
        xt_hi, xt_lo = sb("xt_hi", [P, T, C], F32R), sb("xt_lo", [P, T, C], F32R)
        xc_hi, xc_lo = sb("xc_hi", [P, CH, N], F32R), sb("xc_lo", [P, CH, N], F32R)
        ek = sb("ek", [P, CH, N])
        et_hi, et_lo = sb("et_hi", [P, T, C], F32R), sb("et_lo", [P, T, C], F32R)
        qw = sb("qw", [P, T, C])
        pt_hi, pt_lo = sb("pt_hi", [P, CH, N], F32R), sb("pt_lo", [P, CH, N], F32R)
        z = sb("z", [P, T, C])
        w_raw = sb("w_raw", [P, 4, CH, C])
        w_hi, w_lo = sb("w_hi", [P, 4, CH, C], F32R), sb("w_lo", [P, 4, CH, C], F32R)
        lnb_wo = sb("lnb_wo", [P, CH, C])
        vecs = sb("vecs", [P, NVEC])
        rows = sb("rows", [P, 4, C])
        bq_hi, bq_lo = sb("bq_hi", [P, C], F32R), sb("bq_lo", [P, C], F32R)
        ident = sb("ident", [P, P])
        mask = sb("mask", [P, P])
        ones = sb("ones", [P, P])
        part = sb("part", [P, P], F32R)
        u_row = sb("u_row", [P, C])
        c_row = sb("c_row", [P, C])
        xe_hi, xe_lo = sb("xe_hi", [P, CH, C], F32R), sb("xe_lo", [P, CH, C], F32R)
        s_f = sb("s_f", [P, CH, P])
        st_hi, st_lo = sb("st_hi", [P, CH, P], F32R), sb("st_lo", [P, CH, P], F32R)
        r_f = sb("r_f", [P, CH, RW])
        r_hi, r_lo = sb("r_hi", [P, CH, RW], F32R), sb("r_lo", [P, CH, RW], F32R)
        kmx = sb("kmx", [P, CH])
        kbm = sb("kbm", [P, CH])
        kbias = sb("kbias", [P, CH])
        esum = sb("esum", [P, CH])
        einv = sb("einv", [P, CH])
        srow = sb("srow", [P, CH])
        nmean = sb("nmean", [P, CH])
        qmx = sb("qmx", [P, 2, 2 * HEADS])
        qsum = sb("qsum", [P, NG, GROUP * HEADS])
        qinv = sb("qinv", [P, NG, GROUP * HEADS])
        bnA = sb("bnA", [P, T, 6])
        mvA = sb("mvA", [P, T, 2])
        veA = sb("veA", [P, T])
        rsA = sb("rsA", [P, T])
        bnZ = sb("bnZ", [P, T, 6])
        mvZ = sb("mvZ", [P, T, 2])
        veZ = sb("veZ", [P, T])
        rsZ = sb("rsZ", [P, T])
        nmr = sb("nmr", [P, T])
        nhalf = sb("nhalf", [P, T])

        fence = sb("fence", [P, 1])

        xt_in = [sem(f"xt_in{n}") for n in range(2)]
        xc_in = [sem(f"xc_in{n}") for n in range(2)]
        w_in = sem("w_in")
        v_in = sem("v_in")
        consts, half_ok = sem("consts"), sem("half_ok")
        w_scaled = sem("w_scaled")
        w_split_hi = sem("w_split_hi")
        w_split = sem("w_split")
        rows_mm = sem("rows_mm")
        rows_ok = sem("rows_ok")
        xc_hi_ok, xc_lo_ok = sem("xc_hi_ok"), sem("xc_lo_ok")
        xt_hi_ok, xt_lo_ok, xt_c_ok = sem("xt_hi_ok"), sem("xt_lo_ok"), sem("xt_c_ok")
        k_mm, k_max, k_maxb, k_bias, k_exp = (sem(s) for s in ("k_mm", "k_max", "k_maxb", "k_bias", "k_exp"))
        q_mm, q_max, q_sub, q_exp = (sem(s) for s in ("q_mm", "q_max", "q_sub", "q_exp"))
        q_sum, q_inv, q_norm = (sem(s) for s in ("q_sum", "q_inv", "q_norm"))
        pt_tr, pt_hi_ok, pt_lo_ok = (sem(s) for s in ("pt_tr", "pt_hi_ok", "pt_lo_ok"))
        et_tr, et_hi_ok, et_lo_ok = (sem(s) for s in ("et_tr", "et_hi_ok", "et_lo_ok"))
        xe_mm, xe_hi_ok, xe_lo_ok = (sem(s) for s in ("xe_mm", "xe_hi_ok", "xe_lo_ok"))
        e_inv, s_mm, s_norm, s_mask, s_sum, s_mean = (
            sem(s) for s in ("e_inv", "s_mm", "s_norm", "s_mask", "s_sum", "s_mean"))
        st_tr, st_hi_ok, st_lo_ok = (sem(s) for s in ("st_tr", "st_hi_ok", "st_lo_ok"))
        m_mm, m_cent, r_hi_ok, r_lo_ok = (sem(s) for s in ("m_mm", "m_cent", "r_hi_ok", "r_lo_ok"))
        ap_mm, a_stat, a_var, a_eps, a_rstd = (sem(s) for s in ("ap_mm", "a_stat", "a_var", "a_eps", "a_rstd"))
        z_ok, z_stat, z_var, z_eps, z_rstd, z_nmr, x1_ok = (
            sem(s) for s in ("z_ok", "z_stat", "z_var", "z_eps", "z_rstd", "z_nmr", "x1_ok"))
        x1_out = sem("x1_out")
        Z_CREDIT = T

        def vec(name, c):
            return vecs[:, VEC[name][0] + c:VEC[name][0] + c + 1]

        def s_cols(c):
            return (0, P) if c == 0 else (C, RW)

        def m_cols(c):
            return (P, RW) if c == 0 else (0, C)

        def split3(a_hi, a_lo, b_hi, b_lo):
            return ((a_hi, b_hi), (a_lo, b_hi), (a_hi, b_lo))

        def batches(eng, body):
            for par in range(2):
                body(par, 0, par, True)
            with eng.Fori(1, NB // 2 - 1) as i:
                for par in range(2):
                    body(2 * i + par, i, par, True)
            for par in range(2):
                body(NB - 2 + par, NB // 2 - 1, par, par == 0)

        def nxt(i, par):
            return (i, 1) if par == 0 else (i + 1, 0)

        block = ctx.enter_context(nc.Block())

        @block.sync
        def _(sp):
            sp.dma_start(w_raw[:, 0], wq).then_inc(w_in, 16)
            sp.dma_start(vecs[:], vecs_d).then_inc(v_in, 16)
            sp.dma_start(rows[:], rows_d).then_inc(v_in, 16)
            sp.dma_start(xc[:, 0], x_chan[0]).then_inc(xc_in[0], 16)
            for n, w in ((1, wk), (2, wv), (3, wo)):
                sp.dma_start(w_raw[:, n], w).then_inc(w_in, 16)
            sp.dma_start(ident[:], ident_d).then_inc(v_in, 16)
            sp.dma_start(mask[:], mask_d).then_inc(v_in, 16)
            sp.dma_start(xt[:, 0], x_tok[0]).then_inc(xt_in[0], 16)

            def step(b, i, par, has_next):
                if has_next:
                    ni, npar = nxt(i, par)
                    nb = b + 1 if isinstance(b, int) else sp.snap(b + 1)
                    wait_for(sp, xc_lo_ok, b)
                    sp.dma_start(xc[:, npar], x_chan[bass.ds(nb, 1)].rearrange("o p c n -> (o p) c n")
                                 ).then_inc(xc_in[npar], 16)
                    sp.wait_ge(z_ok, Z_CREDIT + T * b)
                    sp.dma_start(xt[:, npar], x_tok[bass.ds(nb, 1)].rearrange("o p t c -> (o p) t c")
                                 ).then_inc(xt_in[npar], 16)
                for g in range(NG):
                    sp.wait_ge(x1_ok, T * b + GROUP * (g + 1))
                    sp.dma_start(x1_scratch[bass.ds(b, 1), :, g * GROUP:(g + 1) * GROUP].rearrange(
                        "o p t c -> (o p) t c"), z[:, g * GROUP:(g + 1) * GROUP]).then_inc(x1_out, 16)
            batches(sp, step)
            sp.wait_ge(x1_out, 16 * NG * NB)

        @block.gpsimd
        def _(pool):
            nc.gpsimd.memset(nhalf[:], -0.5).then_inc(half_ok, 1)

            def chan_lo(b, par, n):
                pool.wait_ge(xc_in[par], 16 * n)
                pool.wait_ge(xc_hi_ok, b + 1)
                nc.gpsimd.tensor_tensor(xc_lo[:], xc[:, par], xc_hi[:].bitcast(F32), ALU.subtract
                                        ).then_inc(xc_lo_ok, 1)

            def tok_lo(b, par, n):
                pool.wait_ge(xt_in[par], 16 * n)
                pool.wait_ge(xt_hi_ok, b + 1)
                nc.gpsimd.tensor_tensor(xt_lo[:], xt[:, par], xt_hi[:].bitcast(F32), ALU.subtract
                                        ).then_inc(xt_lo_ok, 1)

            def tok_c(b, par):
                pool.wait_ge(xt_lo_ok, b + 1)
                if isinstance(b, int) and b == 0:
                    pool.wait_ge(rows_ok, 2)
                nc.gpsimd.tensor_tensor(xt[:, par], xt[:, par],
                                        c_row[:].rearrange("p (o c) -> p o c", o=1).to_broadcast([P, T, C]),
                                        ALU.add).then_inc(xt_c_ok, 1)

            def q_normalise(b, g):
                pool.wait_ge(q_inv, NG * b + g + 1)
                v = qw[:, g * GROUP:(g + 1) * GROUP].rearrange("p t (h d) -> p (t h) d", d=D)
                nc.gpsimd.tensor_tensor(
                    v, v, qinv[:, g].rearrange("p (h o) -> p h o", o=1).to_broadcast([P, GROUP * HEADS, D]),
                    ALU.mult).then_inc(q_norm, 1)

            def rstd(out, var, ready, n, done, g):
                pool.wait_ge(ready, n)
                gs = slice(g * GROUP, (g + 1) * GROUP)
                nc.gpsimd.tensor_tensor(out[:, gs], var[:, gs], nhalf[:, gs], ALU.pow).then_inc(done, 1)

            pool.wait_ge(half_ok, 1)
            chan_lo(0, 0, 1)
            tok_lo(0, 0, 1)
            tok_c(0, 0)
            for g in range(NG):
                q_normalise(0, g)

            def step(b, i, par, has_next):
                ni, npar = nxt(i, par)
                if has_next:
                    pool.wait_ge(k_mm, CH * (b + 1))
                    chan_lo(b + 1, npar, ni + 1)
                    pool.wait_ge(xe_mm, b + 1)
                    tok_lo(b + 1, npar, ni + 1)
                rstd(rsA, veA, a_eps, NG * b + 1, a_rstd, 0)
                if has_next:
                    q_normalise(b + 1, 0)
                rstd(rsZ, veZ, z_eps, NG * b + 1, z_rstd, 0)
                if has_next:
                    tok_c(b + 1, npar)
                rstd(rsA, veA, a_eps, NG * b + 2, a_rstd, 1)
                rstd(rsZ, veZ, z_eps, NG * b + 2, z_rstd, 1)
                if has_next:
                    q_normalise(b + 1, 1)
            batches(pool, step)

        @block.scalar
        def _(act):
            def chan_hi(b, par, n):
                act.wait_ge(xc_in[par], 16 * n)
                nc.scalar.copy(xc_hi[:], xc[:, par]).then_inc(xc_hi_ok, 1)

            def tok_hi(b, par, n):
                act.wait_ge(xt_in[par], 16 * n)
                nc.scalar.copy(xt_hi[:], xt[:, par]).then_inc(xt_hi_ok, 1)

            def q_exponent(b, g):
                act.wait_ge(q_sub, PAIRS * b + 2 * (g + 1))
                v = qw[:, g * GROUP:(g + 1) * GROUP]
                nc.scalar.activation(v, v, ACT.Exp).then_inc(q_exp, 1)

            chan_hi(0, 0, 1)
            tok_hi(0, 0, 1)
            for g in range(NG):
                q_exponent(0, g)

            def step(b, i, par, has_next):
                ni, npar = nxt(i, par)
                for c in range(CH):
                    act.wait_ge(k_bias, CH * b + c + 1)
                    wait_for(act, et_tr, PAIRS * b)
                    wait_for(act, e_inv, CH * b)
                    nc.scalar.activation(ek[:, c], ring[:, 2 * c:2 * c + 2].rearrange("p a n -> p (a n)"),
                                         ACT.Exp, bias=kbias[:, c:c + 1], accum_out=esum[:, c:c + 1]
                                         ).then_inc(k_exp, 1)
                if has_next:
                    chan_hi(b + 1, npar, ni + 1)
                wait_for(act, ap_mm, T * b)
                for n in range(PAIRS):
                    act.wait_ge(pt_tr, PAIRS * b + n + 1)
                    c, g = n // NG, n % NG
                    nc.scalar.copy(pt_hi[:, c, g * 512:(g + 1) * 512], ring[:, n]).then_inc(pt_hi_ok, 1)
                wait_for(act, xe_mm, b)
                for n in range(PAIRS):
                    act.wait_ge(et_tr, PAIRS * b + n + 1)
                    nc.scalar.copy(et_hi[:, 2 * n:2 * n + 2].rearrange("p t c -> p (t c)"), ring[:, n]
                                   ).then_inc(et_hi_ok, 1)
                act.wait_ge(xe_mm, b + 1)
                wait_for(act, s_mm, b)
                nc.scalar.copy(xe_hi[:].rearrange("p a c -> p (a c)"), stA[:]).then_inc(xe_hi_ok, 1)
                act.wait_ge(st_tr, b + 1)
                wait_for(act, m_mm, b)
                nc.scalar.copy(st_hi[:].rearrange("p a c -> p (a c)"), stA[:, 0:C]).then_inc(st_hi_ok, 1)
                act.wait_ge(m_cent, CH * (b + 1))
                nc.scalar.copy(r_hi[:], r_f[:]).then_inc(r_hi_ok, 1)
                if has_next:
                    tok_hi(b + 1, npar, ni + 1)
                    q_exponent(b + 1, 0)
                for g in range(NG):
                    act.wait_ge(z_nmr, NG * b + g + 1)
                    act.wait_ge(z_rstd, NG * b + g + 1)
                    for t in range(g * GROUP, (g + 1) * GROUP):
                        nc.scalar.activation(z[:, t], z[:, t], ACT.Identity, bias=nmr[:, t:t + 1],
                                             scale=rsZ[:, t:t + 1]).then_inc(x1_ok, 1)
                    if g == 0 and has_next:
                        q_exponent(b + 1, 1)
            batches(act, step)

        @block.vector
        def _(dve):
            nc.vector.memset(ones[:], 1.0).then_inc(consts, 1)
            nc.vector.memset(part[:].bitcast(F32), 1.0 / P).then_inc(consts, 1)
            nc.vector.memset(veZ[:], 1.0).then_inc(z_ok, Z_CREDIT)

            def split_lo(out, full, hi):
                return nc.vector.tensor_tensor(out, full, hi.bitcast(F32), ALU.subtract)

            dve.wait_ge(w_in, 64)
            dve.wait_ge(v_in, 64)
            for c in range(CH):
                nc.vector.tensor_scalar(lnb_wo[:, c], w_raw[:, 3, c], vec("ln_b", c), None, ALU.mult
                                        ).then_inc(w_scaled, 1)
            dve.wait_ge(w_scaled, CH)
            for c in range(CH):
                nc.vector.tensor_scalar(w_raw[:, 3, c], w_raw[:, 3, c], vec("ln_g", c), None, ALU.mult
                                        ).then_inc(w_scaled, 1)
            nc.vector.tensor_copy(bq_hi[:], rows[:, ROW["bq"]]).then_inc(w_split_hi, 1)
            dve.wait_ge(w_scaled, 2 * CH)
            nc.vector.tensor_copy(w_hi[:].rearrange("p w a c -> p (w a c)"),
                                  w_raw[:].rearrange("p w a c -> p (w a c)")).then_inc(w_split_hi, 1)
            dve.wait_ge(w_split_hi, 2)
            split_lo(bq_lo[:], rows[:, ROW["bq"]], bq_hi[:]).then_inc(w_split, 1)
            split_lo(w_lo[:].rearrange("p w a c -> p (w a c)"), w_raw[:].rearrange("p w a c -> p (w a c)"),
                     w_hi[:].rearrange("p w a c -> p (w a c)")).then_inc(w_split, 1)
            dve.wait_ge(rows_mm, 1)
            nc.vector.tensor_copy(u_row[:], stA[:, 0:C]).then_inc(rows_ok, 1)
            nc.vector.tensor_tensor(c_row[:], stB[:, 0:C], rows[:, ROW["bo"]], ALU.add).then_inc(rows_ok, 1)

            def q_centre(b, v):
                dve.wait_ge(q_mm, PAIRS * b + v + 1)
                src = qps[:, v % 2].rearrange("p (h d) -> p h d", d=D)
                nc.vector.tensor_reduce(qmx[:, v % 2], src, AX_X, ALU.max).then_inc(q_max, 1)
                dve.wait_ge(q_max, PAIRS * b + v + 1)
                nc.vector.tensor_tensor(
                    qw[:, 2 * v:2 * v + 2].rearrange("p t (h d) -> p (t h) d", d=D), src,
                    qmx[:, v % 2].rearrange("p (h o) -> p h o", o=1).to_broadcast([P, 2 * HEADS, D]),
                    ALU.subtract).then_inc(q_sub, 1)

            def q_denominator(b, g):
                dve.wait_ge(q_exp, NG * b + g + 1)
                nc.vector.tensor_reduce(qsum[:, g], qw[:, g * GROUP:(g + 1) * GROUP].rearrange(
                    "p t (h d) -> p (t h) d", d=D), AX_X, ALU.add).then_inc(q_sum, 1)
                dve.wait_ge(q_sum, NG * b + g + 1)
                nc.vector.reciprocal(qinv[:, g], qsum[:, g]).then_inc(q_inv, 1)

            for v in range(PAIRS):
                q_centre(0, v)
            for g in range(NG):
                q_denominator(0, g)

            def step(b, i, par, has_next):
                for c in range(CH):
                    dve.wait_ge(k_mm, CH * b + c + 1)
                    wait_for(dve, k_exp, CH * b)
                    nc.vector.tensor_reduce(kmx[:, c:c + 1], ring[:, 2 * c:2 * c + 2].rearrange(
                        "p a n -> p (a n)"), AX_X, ALU.max).then_inc(k_max, 1)
                    dve.wait_ge(k_max, CH * b + c + 1)
                    nc.vector.tensor_tensor(kbm[:, c:c + 1], kmx[:, c:c + 1], vec("bk", c), ALU.add
                                            ).then_inc(k_maxb, 1)
                    dve.wait_ge(k_maxb, CH * b + c + 1)
                    nc.vector.tensor_tensor(kbias[:, c:c + 1], vec("bk", c), kbm[:, c:c + 1], ALU.subtract
                                            ).then_inc(k_bias, 1)
                for n in range(PAIRS):
                    dve.wait_ge(pt_hi_ok, PAIRS * b + n + 1)
                    c, g = n // NG, n % NG
                    seg = slice(g * 512, (g + 1) * 512)
                    split_lo(pt_lo[:, c, seg], ring[:, n], pt_hi[:, c, seg]).then_inc(pt_lo_ok, 1)
                for c in range(CH):
                    dve.wait_ge(k_exp, CH * b + c + 1)
                    nc.vector.reciprocal(einv[:, c:c + 1], esum[:, c:c + 1]).then_inc(e_inv, 1)
                for n in range(PAIRS):
                    dve.wait_ge(et_hi_ok, PAIRS * b + n + 1)
                    split_lo(et_lo[:, 2 * n:2 * n + 2].rearrange("p t c -> p (t c)"), ring[:, n],
                             et_hi[:, 2 * n:2 * n + 2].rearrange("p t c -> p (t c)")).then_inc(et_lo_ok, 1)
                dve.wait_ge(xe_hi_ok, b + 1)
                split_lo(xe_lo[:].rearrange("p a c -> p (a c)"), stA[:],
                         xe_hi[:].rearrange("p a c -> p (a c)")).then_inc(xe_lo_ok, 1)
                if has_next:
                    q_centre(b + 1, 0)
                dve.wait_ge(s_mm, b + 1)
                dve.wait_ge(e_inv, CH * (b + 1))
                for c in range(CH):
                    nc.vector.scalar_tensor_tensor(
                        out=s_f[:, c], in0=stB[:, c * C + c * P:c * C + (c + 1) * P], scalar=einv[:, c:c + 1],
                        in1=rows[:, ROW["bv"], c * P:(c + 1) * P], op0=ALU.mult, op1=ALU.add).then_inc(s_norm, 1)
                dve.wait_ge(s_norm, CH * (b + 1))
                wait_for(dve, r_lo_ok, b)
                for c in range(CH):
                    s0, s1 = s_cols(c)
                    nc.vector.tensor_tensor(r_f[:, c, s0:s1], s_f[:, c], mask[:], ALU.mult).then_inc(s_mask, 1)
                dve.wait_ge(s_mask, CH * (b + 1))
                for c in range(CH):
                    s0, s1 = s_cols(c)
                    nc.vector.tensor_reduce(srow[:, c:c + 1], r_f[:, c, s0:s1], AX_X, ALU.add).then_inc(s_sum, 1)
                dve.wait_ge(s_sum, CH * (b + 1))
                nc.vector.tensor_scalar(nmean[:], srow[:], -1.0 / C, None, ALU.mult).then_inc(s_mean, 1)
                if has_next:
                    q_centre(b + 1, 1)
                dve.wait_ge(st_hi_ok, b + 1)
                split_lo(st_lo[:].rearrange("p a c -> p (a c)"), stA[:, 0:C],
                         st_hi[:].rearrange("p a c -> p (a c)")).then_inc(st_lo_ok, 1)
                dve.wait_ge(m_mm, b + 1)
                dve.wait_ge(s_mean, b + 1)
                for c in range(CH):
                    m0, m1 = m_cols(c)
                    nc.vector.scalar_tensor_tensor(
                        out=r_f[:, c, m0:m1], in0=u_row[:], scalar=nmean[:, c:c + 1],
                        in1=stB[:, c * C:(c + 1) * C], op0=ALU.mult, op1=ALU.add).then_inc(m_cent, 1)
                dve.wait_ge(r_hi_ok, b + 1)
                split_lo(r_lo[:], r_f[:], r_hi[:]).then_inc(r_lo_ok, 1)
                if has_next:
                    q_centre(b + 1, 2)
                    q_denominator(b + 1, 0)
                for g in range(NG):
                    ts = range(g * GROUP, (g + 1) * GROUP)
                    gs = slice(g * GROUP, (g + 1) * GROUP)
                    for t in ts:
                        dve.wait_ge(ap_mm, T * b + t + 1)
                        nc.vector.bn_stats(bnA[:, t], ring[:, t % 4].rearrange("p (a c) -> p a c", c=P)[:, 0:4:3]
                                           ).then_inc(a_stat, 1)
                    dve.wait_ge(a_stat, T * b + GROUP * (g + 1))
                    nc.vector.memset(fence[:], 0.0)
                    for t in ts:
                        nc.vector.bn_aggr(mvA[:, t], bnA[:, t]).then_inc(a_var, 1)
                    dve.wait_ge(a_var, T * b + GROUP * (g + 1))
                    nc.vector.tensor_scalar(veA[:, gs], mvA[:, gs, 1], EPS, None, ALU.add).then_inc(a_eps, 1)
                    if g == 0 and has_next:
                        q_centre(b + 1, 3)
                    dve.wait_ge(a_rstd, NG * b + g + 1)
                    dve.wait_ge(xt_c_ok, b + 1)
                    wait_for(dve, x1_out, 16 * NG * b)
                    for t in ts:
                        nc.vector.scalar_tensor_tensor(
                            out=z[:, t], in0=ring[:, t % 4, P:P + C], scalar=rsA[:, t:t + 1],
                            in1=xt[:, par, t], op0=ALU.mult, op1=ALU.add).then_inc(z_ok, 1)
                    for t in ts:
                        dve.wait_ge(z_ok, Z_CREDIT + T * b + t + 1)
                        nc.vector.bn_stats(bnZ[:, t], z[:, t]).then_inc(z_stat, 1)
                    dve.wait_ge(z_stat, T * b + GROUP * (g + 1))
                    nc.vector.memset(fence[:], 0.0)
                    for t in ts:
                        nc.vector.bn_aggr(mvZ[:, t], bnZ[:, t]).then_inc(z_var, 1)
                    dve.wait_ge(z_var, T * b + GROUP * (g + 1))
                    nc.vector.tensor_scalar(veZ[:, gs], mvZ[:, gs, 1], EPS, None, ALU.add).then_inc(z_eps, 1)
                    dve.wait_ge(z_rstd, NG * b + g + 1)
                    nc.vector.scalar_tensor_tensor(
                        out=nmr[:, gs], in0=mvZ[:, gs, 0], scalar=-1.0, in1=rsZ[:, gs],
                        op0=ALU.mult, op1=ALU.mult).then_inc(z_nmr, 1)
                if has_next:
                    q_denominator(b + 1, 1)
            batches(dve, step)

        @block.tensor
        def _(pe):
            pe.wait_ge(consts, 2)
            pe.wait_ge(w_scaled, 2 * CH)
            pe.wait_ge(v_in, 64)
            for dst, src in ((stA, w_raw[:, 3]), (stB, lnb_wo[:])):
                for c in range(CH):
                    last = nc.tensor.matmul(dst[:, 0:C], ones[:], src[:, c], start=(c == 0), stop=(c == CH - 1))
            last.then_inc(rows_mm, 1)
            pe.wait_ge(w_split, 2)

            def q_product(b, v):
                pe.wait_ge(xc_hi_ok, b + 1)
                pe.wait_ge(xc_lo_ok, b + 1)
                if True:
                    wait_for(pe, q_sub, PAIRS * b + v - 1)
                for h in range(2):
                    t = 2 * v + h
                    out = qps[:, v % 2, h * C:(h + 1) * C]
                    nc.tensor.matmul(out, part[:], bq_hi[:], start=(h == 0), stop=False, skip_group_check=True)
                    nc.tensor.matmul(out, part[:], bq_lo[:], start=False, stop=False, skip_group_check=True)
                    for c in range(CH):
                        ts = slice(t * P, (t + 1) * P)
                        for k, (a, w) in enumerate(split3(xc_hi[:, c, ts], xc_lo[:, c, ts],
                                                          w_hi[:, 0, c], w_lo[:, 0, c])):
                            last = nc.tensor.matmul(out, a, w, start=False, stop=(c == CH - 1 and k == 2),
                                                    skip_group_check=True)
                last.then_inc(q_mm, 1)

            for v in range(PAIRS):
                q_product(0, v)

            def step(b, i, par, has_next):
                for m in range(CH):
                    pe.wait_ge(z_ok, T * b + GROUP + 2 * (m + 1))
                    for h in range(2):
                        n = 0
                        for c in range(CH):
                            ms, ns = slice(m * P, (m + 1) * P), slice(h * 512, (h + 1) * 512)
                            for w, a in split3(w_hi[:, 1, c, ms], w_lo[:, 1, c, ms],
                                               xc_hi[:, c, ns], xc_lo[:, c, ns]):
                                last = nc.tensor.matmul(ring[:, 2 * m + h], w, a, start=(n == 0), stop=(n == 5))
                                n += 1
                    last.then_inc(k_mm, 1)
                for n in range(PAIRS):
                    c, g = n // NG, n % NG
                    pe.wait_ge(k_exp, CH * b + n // 2 + 1)
                    pe.wait_ge(q_norm, NG * b + g + 1)
                    for j in range(GROUP):
                        last = nc.tensor.transpose(ring[:, n, j * P:(j + 1) * P],
                                                   qw[:, g * GROUP + j, c * P:(c + 1) * P], ident[:])
                    last.then_inc(pt_tr, 1)

                def state_product(n):
                    pe.wait_ge(et_lo_ok, PAIRS * b + n + 1)
                    for t in (2 * n, 2 * n + 1):
                        for a in range(CH):
                            as_ = slice(a * P, (a + 1) * P)
                            for k, (x, e) in enumerate(split3(xt_hi[:, t, as_], xt_lo[:, t, as_],
                                                              et_hi[:, t], et_lo[:, t])):
                                last = nc.tensor.matmul(
                                    stA[:, a * C:(a + 1) * C], x, e, start=(t == 0 and a == 0 and k == 0),
                                    stop=(t == T - 1 and k == 2), skip_group_check=True)
                    return last
                for n in range(PAIRS):
                    pe.wait_ge(pt_lo_ok, PAIRS * b + n + 1)
                    for h in range(2):
                        for c in range(CH):
                            t = 2 * n + h
                            last = nc.tensor.transpose(ring[:, n, h * C + c * P:h * C + (c + 1) * P],
                                                       ek[:, c, t * P:(t + 1) * P], ident[:])
                    last.then_inc(et_tr, 1)
                    if n == 0:
                        pe.wait_ge(xt_lo_ok, b + 1)
                        wait_for(pe, st_lo_ok, b)
                    if n >= 1:
                        state_product(n - 1)
                state_product(PAIRS - 1).then_inc(xe_mm, 1)
                if has_next:
                    q_product(b + 1, 0)
                pe.wait_ge(xe_lo_ok, b + 1)
                wait_for(pe, m_cent, CH * b)
                for d in range(CH):
                    for a in range(CH):
                        ds = slice(d * P, (d + 1) * P)
                        for k, (l, r) in enumerate(split3(xe_hi[:, a, ds], xe_lo[:, a, ds],
                                                          w_hi[:, 2, a], w_lo[:, 2, a])):
                            last = nc.tensor.matmul(stB[:, d * C:(d + 1) * C], l, r,
                                                    start=(d == 0 and a == 0 and k == 0),
                                                    stop=(a == CH - 1 and k == 2), skip_group_check=True)
                last.then_inc(s_mm, 1)
                if has_next:
                    q_product(b + 1, 1)
                pe.wait_ge(s_mask, CH * (b + 1))
                for c in range(CH):
                    s0, s1 = s_cols(c)
                    last = nc.tensor.transpose(stA[:, c * P:(c + 1) * P], r_f[:, c, s0:s1], ident[:])
                last.then_inc(st_tr, 1)
                pe.wait_ge(st_lo_ok, b + 1)
                for c in range(CH):
                    for k, (l, r) in enumerate(split3(st_hi[:, c], st_lo[:, c], w_hi[:, 3, c], w_lo[:, 3, c])):
                        last = nc.tensor.matmul(stB[:, c * C:(c + 1) * C], l, r, start=(c == 0 and k == 0),
                                                stop=(k == 2), skip_group_check=True)
                last.then_inc(m_mm, 1)
                if has_next:
                    q_product(b + 1, 2)
                pe.wait_ge(r_hi_ok, b + 1)
                pe.wait_ge(r_lo_ok, b + 1)
                for t in range(T):
                    if t >= GROUP:
                        pe.wait_ge(z_ok, Z_CREDIT + T * b + t - GROUP + 1)
                    ts = slice(t * P, (t + 1) * P)
                    for c in range(CH):
                        out = ring[:, t % 4, c * P:c * P + RW]
                        for k, (l, r) in enumerate(split3(pt_hi[:, c, ts], pt_lo[:, c, ts],
                                                          r_hi[:, c], r_lo[:, c])):
                            last = nc.tensor.matmul(out, l, r, start=(c == 0 and k == 0),
                                                    stop=(c == CH - 1 and k == 2), skip_group_check=True)
                    last.then_inc(ap_mm, 1)
                    if t == GROUP - 1 and has_next:
                        q_product(b + 1, 3)
            batches(pe, step)


def feed_forward_phase(nc, x1_scratch, w1, w2, vecs_d, rows_d, ident_d, out):
    NB, _, T, C = x1_scratch.shape
    CH = C // P
    F = w1.shape[2]
    FC = F // P
    TB = 4
    TOK = TB * P
    NK = NB * T // TB
    DEPTH = 4
    LAG = 3
    POOL_SQ = 3
    assert NK % 2 == 0 and T == 2 * TB

    with ExitStack() as ctx:
        def sb(name, shape, dt=F32):
            return ctx.enter_context(nc.sbuf_tensor("ff_" + name, shape, dt))

        def sem(name):
            return ctx.enter_context(nc.semaphore("ff_" + name))

        hps = ctx.enter_context(nc.psum_tensor("hps", [P, 2, TOK], F32))
        tps = ctx.enter_context(nc.psum_tensor("tps", [P, 2, TOK], F32))
        yps = ctx.enter_context(nc.psum_tensor("yps", [P, 2, TB, C], F32))

        x1 = sb("x1", [P, 2, TB, C])
        x1c = sb("x1c", [P, 2, TB, C])
        xn = sb("xn", [P, TB, C])
        ht_hi, ht_lo = sb("ht_hi", [P, 2, CH, TOK], F32R), sb("ht_lo", [P, 2, CH, TOK], F32R)
        gel = sb("gel", [P, FC, TOK])
        sq = sb("sq", [P, FC, TOK])
        a_hi, a_lo = sb("a_hi", [P, DEPTH, TOK], F32R), sb("a_lo", [P, DEPTH, TOK], F32R)
        acc = sb("acc", [P, 2, 2, TOK])
        accp = sb("accp", [P, TOK])
        z = sb("z", [P, 2, TB, C])
        w1f = sb("w1f", [P, CH, F])
        w2f = sb("w2f", [P, FC, C])
        wm = sb("wm", [P, CH * F])
        t1 = sb("t1", [P, CH, F], F32R)
        t2 = sb("t2", [P, FC, C], F32R)
        vecs = sb("vecs", [P, NVEC])
        rows = sb("rows", [P, 4, C])
        ident = sb("ident", [P, P])
        ones = sb("ones", [P, P])
        wabs = sb("wabs", [P, 2])
        wmean = sb("wmean", [P, 2])
        wscale = sb("wscale", [P, 2])
        wstep = sb("wstep", [P, 2])
        bias1 = sb("bias1", [P, FC])
        u_row = sb("u_row", [P, C])
        c_row = sb("c_row", [P, C])
        bn1, mv1, ve1, rs1 = sb("bn1", [P, TB, 6]), sb("mv1", [P, TB, 2]), sb("ve1", [P, TB]), sb("rs1", [P, TB])
        bnZ, mvZ, veZ, rsZ = sb("bnZ", [P, TB, 6]), sb("mvZ", [P, TB, 2]), sb("veZ", [P, TB]), sb("rsZ", [P, TB])
        nmr = sb("nmr", [P, TB])
        sums = sb("sums", [P, 2 * TB])
        nmu = sb("nmu", [P, TB])
        msq = sb("msq", [P, TB])
        var = sb("var", [P, TB])
        rsH = sb("rsH", [P, TB])
        gain = sb("gain", [P, TB])
        yc = sb("yc", [P, TB, C])
        nhalf = sb("nhalf", [P, TB])

        fence = sb("fence", [P, 1])

        x1_in = [sem(f"x1_in{n}") for n in range(2)]
        w_in, v_in, consts, half_ok = sem("w_in"), sem("v_in"), sem("consts"), sem("half_ok")
        w_abs, w_sum, w_mean, w_scale, w_step = (sem(s) for s in ("w_abs", "w_sum", "w_mean", "w_scale", "w_step"))
        w_neg, w_pos, w_tern, w_sc2 = (sem(s) for s in ("w_neg", "w_pos", "w_tern", "w_sc2"))
        fold_mm, fold_t, fold_ok = sem("fold_mm"), sem("fold_t"), sem("fold_ok")
        n_stat, n_var, n_eps, n_rstd, n_ok = (sem(s) for s in ("n_stat", "n_var", "n_eps", "n_rstd", "n_ok"))
        x1c_ok = sem("x1c_ok")
        ht_tr, ht_hi_ok, ht_lo_ok = (sem(s) for s in ("ht_tr", "ht_hi_ok", "ht_lo_ok"))
        h_mm, gelu_ok, hi_ok, lo_ok, sq_ok = (sem(s) for s in ("h_mm", "gelu_ok", "hi_ok", "lo_ok", "sq_ok"))
        y_mm = sem("y_mm")
        sum_g, sum_p, sum_q = sem("sum_g"), sem("sum_p"), sem("sum_q")
        r_tr, r_sum, r_mean, r_sq, r_var, r_eps, r_rstd, r_gain = (
            sem(s) for s in ("r_tr", "r_sum", "r_mean", "r_sq", "r_var", "r_eps", "r_rstd", "r_gain"))
        yc_ok, z_ok, z_stat, z_var, z_eps, z_rstd, z_nmr, o_ok = (
            sem(s) for s in ("yc_ok", "z_ok", "z_stat", "z_var", "z_eps", "z_rstd", "z_nmr", "o_ok"))
        o_out = [sem(f"o_out{n}") for n in range(2)]
        Q_ADDS = FC - POOL_SQ
        P_ADDS = POOL_SQ - 1

        def vec(name, c):
            return vecs[:, VEC[name][0] + c:VEC[name][0] + c + 1]

        def blocks(eng, body):
            for par in range(2):
                body(par, 0, par, par == 0, False)
            with eng.Fori(1, NK // 2 - 1) as i:
                for par in range(2):
                    body(2 * i + par, i, par, False, False)
            for par in range(2):
                body(NK - 2 + par, NK // 2 - 1, par, False, par == 1)

        block = ctx.enter_context(nc.Block())

        @block.sync
        def _(sp):
            sp.dma_start(w1f[:], w1).then_inc(w_in, 16)
            sp.dma_start(w2f[:], w2).then_inc(w_in, 16)
            sp.dma_start(x1[:, 0], x1_scratch[0, :, 0:TB]).then_inc(x1_in[0], 16)
            sp.dma_start(vecs[:], vecs_d).then_inc(v_in, 16)
            sp.dma_start(rows[:], rows_d).then_inc(v_in, 16)
            sp.dma_start(ident[:], ident_d).then_inc(v_in, 16)

            def step(k, i, par, first, last):
                if not last:
                    if not first:
                        sp.wait_ge(n_ok, TB * k)
                        sp.wait_ge(x1c_ok, k)
                    src = x1_scratch[bass.ds(i, 1), :, TB:T] if par == 0 else x1_scratch[bass.ds(i + 1, 1), :, 0:TB]
                    sp.dma_start(x1[:, 1 - par], src.rearrange("o p t c -> (o p) t c")).then_inc(x1_in[1 - par], 16)
                if not first:
                    store(sp, k - 1, i if par == 1 else i - 1, 1 - par)

            def store(sp, k, i, par):
                dst = out.rearrange("b p t c -> (b p) t c")[bass.ds(i * P, P), par * TB:(par + 1) * TB]
                sp.wait_ge(o_ok, TB * (k + 1))
                sp.dma_start(dst, z[:, par]).then_inc(o_out[par], 16)
            blocks(sp, step)
            store(sp, NK - 1, NK // 2 - 1, 1)
            for par in range(2):
                sp.wait_ge(o_out[par], 8 * NK)

        @block.gpsimd
        def _(pool):
            nc.gpsimd.memset(nhalf[:], -0.5).then_inc(half_ok, 1)
            pool.wait_ge(half_ok, 1)

            def pow_half(o, v, ready, n, done):
                pool.wait_ge(ready, n)
                nc.gpsimd.tensor_tensor(o[:], v[:], nhalf[:], ALU.pow).then_inc(done, 1)

            def keep_residual(k, par, n):
                pool.wait_ge(x1_in[par], 16 * n)
                if isinstance(k, int) and k == 0:
                    pool.wait_ge(fold_ok, 3)
                if not (isinstance(k, int) and k < 2):
                    pool.wait_ge(z_ok, TB * (k - 1))
                nc.gpsimd.tensor_tensor(x1c[:, par], x1[:, par],
                                        c_row[:].rearrange("p (o c) -> p o c", o=1).to_broadcast([P, TB, C]),
                                        ALU.add).then_inc(x1c_ok, 1)

            pow_half(rs1, ve1, n_eps, 1, n_rstd)

            def step(k, i, par, first, last):
                keep_residual(k, par, i + 1)
                if not first:
                    tail_rstd(k - 1, 0)
                for m in range(1, FC):
                    pool.wait_ge(gelu_ok, FC * k + m + 1)
                    if m > 1:
                        pool.wait_ge(sum_g, (FC - 1) * k + m - 1)
                    elif not (isinstance(k, int) and k < 2):
                        pool.wait_ge(r_tr, k - 1)
                    a = gel[:, 0] if m == 1 else acc[:, par, 0]
                    nc.gpsimd.tensor_tensor(acc[:, par, 0], a, gel[:, m], ALU.add).then_inc(sum_g, 1)
                    if 1 <= m < POOL_SQ:
                        pool.wait_ge(sq_ok, FC * k + m + 1)
                        if m > 1:
                            pool.wait_ge(sum_p, P_ADDS * k + m - 1)
                        elif not first:
                            pool.wait_ge(sum_q, Q_ADDS * k)
                        a = sq[:, 0] if m == 1 else accp[:]
                        nc.gpsimd.tensor_tensor(accp[:], a, sq[:, m], ALU.add).then_inc(sum_p, 1)
                    if m == 3 and not first:
                        tail_rstd(k - 1, 1)
                    if m == 5 and not last:
                        pow_half(rs1, ve1, n_eps, k + 2, n_rstd)

            def tail_rstd(k, part):
                if part == 0:
                    return
                pow_half(rsH, var, r_eps, k + 1, r_rstd)
                pow_half(rsZ, veZ, z_eps, k + 1, z_rstd)
            blocks(pool, step)
            tail_rstd(NK - 1, 1)

        @block.scalar
        def _(act):
            def ht_high(k, par):
                for c in range(CH):
                    act.wait_ge(ht_tr, CH * k + c + 1)
                    nc.scalar.activation(ht_hi[:, par, c], tps[:, c], ACT.Copy, scale=vec("ln1_g", c)
                                         ).then_inc(ht_hi_ok, 1)

            def normalise_out(k, par):
                act.wait_ge(z_nmr, k + 1)
                for t in range(TB):
                    nc.scalar.activation(z[:, par, t], z[:, par, t], ACT.Identity, bias=nmr[:, t:t + 1],
                                         scale=rsZ[:, t:t + 1]).then_inc(o_ok, 1)

            act.wait_ge(v_in, 48)
            ht_high(0, 0)
            act.wait_ge(w_step, 1)
            act.wait_ge(fold_ok, 1)

            def step(k, i, par, first, last):
                for m in range(FC):
                    act.wait_ge(h_mm, FC * k + m + 1)
                    if not first:
                        act.wait_ge(lo_ok, FC * (k - 1) + m + 1)
                        if m < FC and m >= 1:
                            act.wait_ge(sum_g, (FC - 1) * (k - 1) + m)
                        else:
                            act.wait_ge(sum_g, (FC - 1) * (k - 1) + 1)
                    nc.scalar.activation(gel[:, m], hps[:, m % 2], ACT.Gelu, bias=bias1[:, m:m + 1],
                                         scale=wstep[:, 0:1]).then_inc(gelu_ok, 1)
                    act.wait_ge(gelu_ok, FC * k + m + 1)
                    n = m - DEPTH
                    if n >= 0 or not first:
                        act.wait_ge(y_mm, FC * k + n + 1)
                    nc.scalar.activation(a_hi[:, m % DEPTH], gel[:, m], ACT.Copy, scale=vec("ln2_g", m)
                                         ).then_inc(hi_ok, 1)
                    if not first:
                        act.wait_ge(sum_q, Q_ADDS * k)
                        act.wait_ge(sum_p, P_ADDS * k)
                    nc.scalar.activation(sq[:, m], gel[:, m], ACT.Square).then_inc(sq_ok, 1)
                    if m == 6 and not last:
                        ht_high(k + 1, 1 - par)
                    if m == 5 and not first:
                        normalise_out(k - 1, 1 - par)
            blocks(act, step)
            normalise_out(NK - 1, 1)

        @block.vector
        def _(dve):
            nc.vector.memset(ones[:], 1.0).then_inc(consts, 1)

            dve.wait_ge(w_in, 32)
            flat = (w1f[:].rearrange("p a f -> p (a f)"), w2f[:].rearrange("p a f -> p (a f)"))
            tern = (t1[:].rearrange("p a f -> p (a f)"), t2[:].rearrange("p a f -> p (a f)"))
            for n in range(2):
                nc.vector.tensor_reduce(wabs[:, n:n + 1], flat[n], AX_X, ALU.add, apply_absolute_value=True
                                        ).then_inc(w_abs, 1)
            dve.wait_ge(w_sum, 1)
            nc.vector.tensor_scalar(wmean[:], hps[:, 0, 0:2], 1.0 / (C * F), 1e-5, ALU.mult, ALU.max
                                    ).then_inc(w_mean, 1)
            dve.wait_ge(w_mean, 1)
            nc.vector.reciprocal(wscale[:], wmean[:]).then_inc(w_scale, 1)
            dve.wait_ge(w_scale, 1)
            nc.vector.reciprocal(wstep[:], wscale[:]).then_inc(w_step, 1)
            for n in range(2):
                if n:
                    dve.wait_ge(w_tern, n)
                nc.vector.tensor_scalar(wm[:], flat[n], wscale[:, n:n + 1], -0.5, ALU.mult, ALU.is_lt
                                        ).then_inc(w_neg, 1)
                nc.vector.tensor_scalar(flat[n], flat[n], wscale[:, n:n + 1], 0.5, ALU.mult, ALU.is_gt
                                        ).then_inc(w_pos, 1)
                dve.wait_ge(w_neg, n + 1)
                dve.wait_ge(w_pos, n + 1)
                nc.vector.tensor_tensor(tern[n], flat[n], wm[:], ALU.subtract).then_inc(w_tern, 1)
            dve.wait_ge(w_tern, 2)
            dve.wait_ge(v_in, 48)
            for m in range(FC):
                nc.vector.tensor_scalar(w2f[:, m], t2[:, m].bitcast(F32), vec("ln2_g", m), None, ALU.mult
                                        ).then_inc(w_sc2, 1)
                nc.vector.tensor_scalar(wm[:, m * C:(m + 1) * C], t2[:, m].bitcast(F32), vec("ln2_b", m), None,
                                        ALU.mult).then_inc(w_sc2, 1)
            dve.wait_ge(fold_mm, 1)
            nc.vector.scalar_tensor_tensor(
                out=bias1[:], in0=hps[:, 1, 0:FC], scalar=wstep[:, 0:1],
                in1=vecs[:, VEC["b1"][0]:VEC["b1"][0] + FC], op0=ALU.mult, op1=ALU.add).then_inc(fold_ok, 1)
            nc.vector.tensor_copy(u_row[:], yps[:, 0, 0]).then_inc(fold_ok, 1)
            nc.vector.scalar_tensor_tensor(
                out=c_row[:], in0=yps[:, 1, 0], scalar=wstep[:, 1:2], in1=rows[:, ROW["b2"]],
                op0=ALU.mult, op1=ALU.add).then_inc(fold_ok, 1)

            def norm_stats(k, par, n):
                dve.wait_ge(x1_in[par], 16 * n)
                for t in range(TB):
                    nc.vector.bn_stats(bn1[:, t], x1[:, par, t]).then_inc(n_stat, 1)
                dve.wait_ge(n_stat, TB * (k + 1))
                nc.vector.memset(fence[:], 0.0)
                for t in range(TB):
                    nc.vector.bn_aggr(mv1[:, t], bn1[:, t]).then_inc(n_var, 1)
                dve.wait_ge(n_var, TB * (k + 1))
                nc.vector.tensor_scalar(ve1[:], mv1[:, :, 1], EPS, None, ALU.add).then_inc(n_eps, 1)

            def norm_apply(k, par):
                dve.wait_ge(n_rstd, k + 1)
                if not (isinstance(k, int) and k == 0):
                    dve.wait_ge(ht_tr, CH * k)
                for t in range(TB):
                    nc.vector.tensor_scalar(xn[:, t], x1[:, par, t], mv1[:, t, 0:1], rs1[:, t:t + 1],
                                            ALU.subtract, ALU.mult).then_inc(n_ok, 1)

            def ht_low(k, par):
                for c in range(CH):
                    dve.wait_ge(ht_hi_ok, CH * k + c + 1)
                    nc.vector.scalar_tensor_tensor(
                        out=ht_lo[:, par, c], in0=tps[:, c], scalar=vec("ln1_g", c),
                        in1=ht_hi[:, par, c].bitcast(F32), op0=ALU.mult, op1=ALU.subtract).then_inc(ht_lo_ok, 1)

            def hidden_stats(k):
                dve.wait_ge(r_tr, k + 1)
                nc.vector.tensor_reduce(sums[:], tps[:].rearrange("p a (t n) -> p (a t) n", n=P), AX_X, ALU.add
                                        ).then_inc(r_sum, 1)
                dve.wait_ge(r_sum, k + 1)
                nc.vector.tensor_scalar(nmu[:], sums[:, 0:TB], -1.0 / F, None, ALU.mult).then_inc(r_mean, 1)
                dve.wait_ge(r_mean, k + 1)
                nc.vector.tensor_tensor(msq[:], nmu[:], nmu[:], ALU.mult).then_inc(r_sq, 1)
                dve.wait_ge(r_sq, k + 1)
                nc.vector.scalar_tensor_tensor(out=var[:], in0=sums[:, TB:2 * TB], scalar=1.0 / F, in1=msq[:],
                                               op0=ALU.mult, op1=ALU.subtract).then_inc(r_var, 1)
                dve.wait_ge(r_var, k + 1)
                nc.vector.tensor_scalar(var[:], var[:], 0.0, EPS, ALU.max, ALU.add).then_inc(r_eps, 1)

            def centre_y(k, par):
                dve.wait_ge(y_mm, FC * (k + 1))
                for t in range(TB):
                    nc.vector.scalar_tensor_tensor(
                        out=yc[:, t], in0=u_row[:], scalar=nmu[:, t:t + 1], in1=yps[:, par, t],
                        op0=ALU.mult, op1=ALU.add).then_inc(yc_ok, 1)

            def residual(k, par, uses):
                dve.wait_ge(r_rstd, k + 1)
                nc.vector.tensor_scalar(gain[:], rsH[:], wstep[:, 1:2], None, ALU.mult).then_inc(r_gain, 1)
                dve.wait_ge(r_gain, k + 1)
                dve.wait_ge(yc_ok, TB * (k + 1))
                dve.wait_ge(x1c_ok, k + 1)
                if not (isinstance(uses, int) and uses == 0):
                    dve.wait_ge(o_out[par], 16 * uses)
                for t in range(TB):
                    nc.vector.scalar_tensor_tensor(
                        out=z[:, par, t], in0=yc[:, t], scalar=gain[:, t:t + 1], in1=x1c[:, par, t],
                        op0=ALU.mult, op1=ALU.add).then_inc(z_ok, 1)
                for t in range(TB):
                    dve.wait_ge(z_ok, TB * k + t + 1)
                    nc.vector.bn_stats(bnZ[:, t], z[:, par, t]).then_inc(z_stat, 1)
                dve.wait_ge(z_stat, TB * (k + 1))
                nc.vector.memset(fence[:], 0.0)
                for t in range(TB):
                    nc.vector.bn_aggr(mvZ[:, t], bnZ[:, t]).then_inc(z_var, 1)
                dve.wait_ge(z_var, TB * (k + 1))
                nc.vector.tensor_scalar(veZ[:], mvZ[:, :, 1], EPS, None, ALU.add).then_inc(z_eps, 1)

            def out_bias(k):
                dve.wait_ge(z_rstd, k + 1)
                if not (isinstance(k, int) and k == 0):
                    dve.wait_ge(o_ok, TB * k)
                nc.vector.scalar_tensor_tensor(out=nmr[:], in0=mvZ[:, :, 0], scalar=-1.0, in1=rsZ[:],
                                               op0=ALU.mult, op1=ALU.mult).then_inc(z_nmr, 1)

            norm_stats(0, 0, 1)
            norm_apply(0, 0)
            ht_low(0, 0)

            def step(k, i, par, first, last):
                ni = i if par == 0 else i + 1
                for m in range(FC):
                    dve.wait_ge(hi_ok, FC * k + m + 1)
                    nc.vector.scalar_tensor_tensor(
                        out=a_lo[:, m % DEPTH], in0=gel[:, m], scalar=vec("ln2_g", m),
                        in1=a_hi[:, m % DEPTH].bitcast(F32), op0=ALU.mult, op1=ALU.subtract).then_inc(lo_ok, 1)
                    if m > POOL_SQ:
                        j = m - POOL_SQ
                        dve.wait_ge(sq_ok, FC * k + m + 1)
                        if j > 1:
                            dve.wait_ge(sum_q, Q_ADDS * k + j - 1)
                        a = sq[:, POOL_SQ] if j == 1 else acc[:, par, 1]
                        nc.vector.tensor_tensor(acc[:, par, 1], a, sq[:, m], ALU.add).then_inc(sum_q, 1)
                    if m == 0 and not last:
                        norm_stats(k + 1, 1 - par, ni + 1)
                    if m == 3 and not first:
                        hidden_stats(k - 1)
                        centre_y(k - 1, 1 - par)
                        residual(k - 1, 1 - par, i if par == 1 else i - 1)
                        out_bias(k - 1)
                    if m == 5 and not last:
                        norm_apply(k + 1, 1 - par)
                    if m == 6 and not last:
                        ht_low(k + 1, 1 - par)
                dve.wait_ge(sum_q, Q_ADDS * (k + 1) - 1)
                dve.wait_ge(sum_p, P_ADDS * (k + 1))
                nc.vector.tensor_tensor(acc[:, par, 1], acc[:, par, 1], accp[:], ALU.add).then_inc(sum_q, 1)
            blocks(dve, step)
            hidden_stats(NK - 1)
            centre_y(NK - 1, 1)
            residual(NK - 1, 1, NK // 2 - 1)
            out_bias(NK - 1)

        @block.tensor
        def _(pe):
            pe.wait_ge(consts, 1)
            pe.wait_ge(w_abs, 2)
            nc.tensor.matmul(hps[:, 0, 0:2], ones[:], wabs[:], start=True, stop=True).then_inc(w_sum, 1)
            pe.wait_ge(w_tern, 2)
            pe.wait_ge(v_in, 48)
            for m in range(FC):
                for c in range(CH):
                    nc.tensor.matmul(hps[:, 1, m:m + 1], t1[:, c, m * P:(m + 1) * P].bitcast(F32), vec("ln1_b", c),
                                     start=(m == 0 and c == 0), stop=(c == CH - 1), skip_group_check=True)
            pe.wait_ge(w_sc2, 2 * FC)
            for slot, src in ((0, w2f[:]), (1, wm[:].rearrange("p (m c) -> p m c", c=C))):
                for m in range(FC):
                    last = nc.tensor.matmul(yps[:, slot, 0], ones[:], src[:, m], start=(m == 0), stop=(m == FC - 1))
            last.then_inc(fold_mm, 1)

            def transposes(k):
                pe.wait_ge(n_ok, TB * (k + 1))
                for c in range(CH):
                    for t in range(TB):
                        last = nc.tensor.transpose(tps[:, c, t * P:(t + 1) * P], xn[:, t, c * P:(c + 1) * P],
                                                   ident[:])
                    last.then_inc(ht_tr, 1)

            def sum_transposes(k, par):
                pe.wait_ge(sum_g, (FC - 1) * (k + 1))
                pe.wait_ge(sum_q, Q_ADDS * (k + 1))
                for a in range(2):
                    for t in range(TB):
                        last = nc.tensor.transpose(tps[:, a, t * P:(t + 1) * P], acc[:, par, a, t * P:(t + 1) * P],
                                                   ident[:])
                last.then_inc(r_tr, 1)

            def second(k, m, par):
                pe.wait_ge(hi_ok, FC * k + m + 1)
                pe.wait_ge(lo_ok, FC * k + m + 1)
                if m == 0 and not (isinstance(k, int) and k < 2):
                    pe.wait_ge(yc_ok, TB * (k - 1))
                for t in range(TB):
                    for n, a in enumerate((a_hi, a_lo)):
                        last = nc.tensor.matmul(yps[:, par, t], a[:, m % DEPTH, t * P:(t + 1) * P], t2[:, m],
                                                start=(m == 0 and n == 0 and t % 2 == 0),
                                                stop=(m == FC - 1 and n == 1), skip_group_check=True)
                last.then_inc(y_mm, 1)

            transposes(0)
            pe.wait_ge(fold_ok, 3)

            def step(k, i, par, first, last):
                for m in range(FC):
                    if m == 0:
                        pe.wait_ge(ht_hi_ok, CH * (k + 1))
                        pe.wait_ge(ht_lo_ok, CH * (k + 1))
                    if m >= 2 or not first:
                        pe.wait_ge(gelu_ok, FC * k + m - 1)
                    for c in range(CH):
                        for n, h in enumerate((ht_hi, ht_lo)):
                            mm = nc.tensor.matmul(hps[:, m % 2], t1[:, c, m * P:(m + 1) * P], h[:, par, c],
                                                  start=(c == 0 and n == 0), stop=(c == CH - 1 and n == 1))
                    mm.then_inc(h_mm, 1)
                    if m >= LAG:
                        second(k, m - LAG, par)
                    elif not first:
                        second(k - 1, FC + m - LAG, 1 - par)
                    if m == 2 and not first:
                        sum_transposes(k - 1, 1 - par)
                    if m == 6 and not last:
                        if not first:
                            pe.wait_ge(r_sum, k)
                        transposes(k + 1)
            blocks(pe, step)
            for m in range(FC - LAG, FC):
                second(NK - 1, m, 1)
            sum_transposes(NK - 1, 1)


_INS = ["x_tok", "x_chan", "wq", "wk", "wv", "wo", "w1", "w2", "vecs", "rows", "ident", "mask"]


def program(nc, a, out):
    NB, _, T, C = a["x_tok"].shape
    x1 = nc.dram_tensor("x1_scratch", (NB, P, T, C), F32, kind="Internal").ap()
    attention_phase(nc, a["x_tok"], a["x_chan"], a["wq"], a["wk"], a["wv"], a["wo"], a["vecs"], a["rows"],
                    a["ident"], a["mask"], x1)
    feed_forward_phase(nc, x1, a["w1"], a["w2"], a["vecs"], a["rows"], a["ident"], out)


def kernel(**inputs):
    import concourse.bacc as _bacc
    from concourse.bass_utils import run_bass_kernel_spmd as _run

    g = {k: np.asarray(v) for k, v in inputs.items()}
    x = g["L0_attn_x"]
    B, N, C = x.shape
    T = N // P
    x_tok = x.reshape(B, P, T, C)

    def kxn(w):
        wt = w.T
        return np.ascontiguousarray(wt.reshape(wt.shape[0] // P, P, wt.shape[1]).transpose(1, 0, 2))

    def col(v):
        return v.reshape(-1, P).T

    vec_of = {"bk": "L0_attn_bk", "ln_g": "L0_attn_ln_g", "ln_b": "L0_attn_ln_b", "ln1_g": "L0_ffn_ln1_g",
              "ln1_b": "L0_ffn_ln1_b", "b1": "L0_ffn_b1", "ln2_g": "L0_ffn_ln2_g", "ln2_b": "L0_ffn_ln2_b"}
    row_of = {"bq": "L0_attn_bq", "bv": "L0_attn_bv", "bo": "L0_attn_bo", "b2": "L0_ffn_b2"}
    head = np.arange(P) // 16
    arrays = {
        "x_tok": x_tok,
        "x_chan": x_tok.transpose(0, 3, 2, 1).reshape(B, C // P, P, N).transpose(0, 2, 1, 3),
        "wq": kxn(g["L0_attn_Wq"]), "wk": kxn(g["L0_attn_Wk"]), "wv": kxn(g["L0_attn_Wv"]),
        "wo": kxn(g["L0_attn_Wo"]), "w1": kxn(g["L0_ffn_w1"]), "w2": kxn(g["L0_ffn_w2"]),
        "vecs": np.concatenate([col(g[vec_of[n]]) for n in VEC], axis=1),
        "rows": np.broadcast_to(np.stack([g[row_of[n]] for n in ROW])[None], (P, len(ROW), C)),
        "ident": np.eye(P, dtype=np.float32),
        "mask": (head[:, None] == head[None, :]).astype(np.float32),
    }
    arrays = {f"in_{k}_dram": np.ascontiguousarray(v) for k, v in arrays.items()}

    nc = _bacc.Bacc("TRN2", target_bir_lowering=False, num_devices=1)
    a = {n: nc.dram_tensor(f"in_{n}_dram", arrays[f"in_{n}_dram"].shape, F32, kind="ExternalInput").ap()
         for n in _INS}
    out = nc.dram_tensor("out_0_dram", (B, P, T, C), F32, kind="ExternalOutput").ap()
    program(nc, a, out)
    r = _run(nc, [arrays], core_ids=[0])
    return r.results[0]["out_0_dram"].reshape(B, N, C)
```

```python
from contextlib import ExitStack

import numpy as np

import concourse.bass as bass
from concourse import mybir

F32 = mybir.dt.float32
F32R = mybir.dt.float32r
ALU = mybir.AluOpType
ACT = mybir.ActivationFunctionType
AX_X = mybir.AxisListType.X

P = 128
EPS = 1e-5

VEC = {}
_at = 0
for _name, _n in (("bk", 2), ("ln_g", 2), ("ln_b", 2), ("ln1_g", 2), ("ln1_b", 2),
                  ("b1", 8), ("ln2_g", 8), ("ln2_b", 8)):
    VEC[_name] = (_at, _n)
    _at += _n
NVEC = _at
ROW = {"bq": 0, "bv": 1, "bo": 2, "b2": 3}


def wait_for(eng, semaphore, count):
    if not isinstance(count, int) or count > 0:
        eng.wait_ge(semaphore, count)


def attention_phase(nc, x_tok, x_chan, wq, wk, wv, wo, vecs_d, rows_d, ident_d, mask_d, x1_scratch):
    NB, _, T, C = x_tok.shape
    N = T * P
    CH = C // P
    D = 16
    HEADS = C // D
    PAIRS = T // 2
    GROUP = 4
    NG = T // GROUP
    RW = C + P
    assert NB % 2 == 0 and CH == 2 and T == 8

    with ExitStack() as ctx:
        def sb(name, shape, dt=F32):
            return ctx.enter_context(nc.sbuf_tensor(name, shape, dt))

        def sem(name):
            return ctx.enter_context(nc.semaphore(name))

        ring = ctx.enter_context(nc.psum_tensor("ring", [P, 4, 512], F32))
        aps = ctx.enter_context(nc.psum_tensor("aps", [P, 2, 512], F32))
        qps = ctx.enter_context(nc.psum_tensor("qps", [P, 512], F32))
        sps = ctx.enter_context(nc.psum_tensor("sps", [P, 512], F32))

        xt = sb("xt", [P, 2, T, C])
        xc = sb("xc", [P, CH, N])
        xt_hi, xt_lo = sb("xt_hi", [P, T, C], F32R), sb("xt_lo", [P, T, C], F32R)
        xc_hi, xc_lo = sb("xc_hi", [P, 2, CH, N], F32R), sb("xc_lo", [P, 2, CH, N], F32R)
        ek = sb("ek", [P, CH, N])
        et_hi, et_lo = sb("et_hi", [P, T, C], F32R), sb("et_lo", [P, T, C], F32R)
        qw = sb("qw", [P, 2, T, C])
        pt_hi, pt_lo = sb("pt_hi", [P, CH, N], F32R), sb("pt_lo", [P, CH, N], F32R)
        z = sb("z", [P, T, C + 1])
        zjunk = sb("zjunk", [P, T, C])
        qtree = sb("qtree", [P, NG, GROUP * HEADS, D // 2])
        w_raw = sb("w_raw", [P, 4, CH, C])
        w_hi, w_lo = sb("w_hi", [P, 4, CH, C], F32R), sb("w_lo", [P, 4, CH, C], F32R)
        lnb_wo = sb("lnb_wo", [P, CH, C])
        vecs = sb("vecs", [P, NVEC])
        rows = sb("rows", [P, 4, C])
        bq_hi, bq_lo = sb("bq_hi", [P, C], F32R), sb("bq_lo", [P, C], F32R)
        ident = sb("ident", [P, P])
        mask = sb("mask", [P, P])
        ones = sb("ones", [P, P])
        part = sb("part", [P, P], F32R)
        u_row = sb("u_row", [P, C])
        c_row = sb("c_row", [P, C])
        xe_hi, xe_lo = sb("xe_hi", [P, CH, C], F32R), sb("xe_lo", [P, CH, C], F32R)
        s_f = sb("s_f", [P, CH, P])
        st_hi, st_lo = sb("st_hi", [P, CH, P], F32R), sb("st_lo", [P, CH, P], F32R)
        r_f = sb("r_f", [P, CH, RW])
        r_hi, r_lo = sb("r_hi", [P, CH, RW], F32R), sb("r_lo", [P, CH, RW], F32R)
        kmx = sb("kmx", [P, CH])
        kbm = sb("kbm", [P, CH])
        kbias = sb("kbias", [P, CH])
        esum = sb("esum", [P, CH])
        einv = sb("einv", [P, CH])
        srow = sb("srow", [P, CH])
        nmean = sb("nmean", [P, CH])
        qmx = sb("qmx", [P, 2, 2 * HEADS])
        qsum = sb("qsum", [P, NG, GROUP * HEADS])
        qinv = sb("qinv", [P, NG, GROUP * HEADS])
        bnA = sb("bnA", [P, T, 6])
        mvA = sb("mvA", [P, T, 2])
        veA = sb("veA", [P, T])
        rsA = sb("rsA", [P, T])
        zsum = sb("zsum", [P, T])
        znm = sb("znm", [P, T])
        zss = sb("zss", [P, T])
        veZ = sb("veZ", [P, T])
        vaZ = sb("vaZ", [P, T])
        inv_c = sb("inv_c", [P, T])
        eps = sb("eps", [P, T])
        rsZ = sb("rsZ", [P, T])
        nmr = sb("nmr", [P, T])
        nhalf = sb("nhalf", [P, T])

        fence = sb("fence", [P, 1])

        xt_in = [sem(f"xt_in{n}") for n in range(2)]
        xc_in = sem("xc_in")
        w_in = sem("w_in")
        v_in = sem("v_in")
        consts, half_ok = sem("consts"), sem("half_ok")
        w_scaled = sem("w_scaled")
        w_split_hi = sem("w_split_hi")
        w_split = sem("w_split")
        rows_mm = sem("rows_mm")
        rows_ok = sem("rows_ok")
        xc_hi_ok, xc_lo_ok = sem("xc_hi_ok"), sem("xc_lo_ok")
        xt_hi_ok, xt_lo_ok, xt_c_ok = sem("xt_hi_ok"), sem("xt_lo_ok"), sem("xt_c_ok")
        k_mm, k_max, k_maxb, k_bias, k_exp = (sem(s) for s in ("k_mm", "k_max", "k_maxb", "k_bias", "k_exp"))
        q_mm, q_max, q_sub, q_exp = (sem(s) for s in ("q_mm", "q_max", "q_sub", "q_exp"))
        q_sum, q_inv, q_norm = (sem(s) for s in ("q_sum", "q_inv", "q_norm"))
        pt_tr, pt_hi_ok, pt_lo_ok = (sem(s) for s in ("pt_tr", "pt_hi_ok", "pt_lo_ok"))
        et_tr, et_hi_ok, et_lo_ok = (sem(s) for s in ("et_tr", "et_hi_ok", "et_lo_ok"))
        xe_mm, xe_hi_ok, xe_lo_ok = (sem(s) for s in ("xe_mm", "xe_hi_ok", "xe_lo_ok"))
        e_inv, s_mm, s_norm, s_mask, s_sum, s_mean = (
            sem(s) for s in ("e_inv", "s_mm", "s_norm", "s_mask", "s_sum", "s_mean"))
        st_tr, st_hi_ok, st_lo_ok = (sem(s) for s in ("st_tr", "st_hi_ok", "st_lo_ok"))
        m_mm, m_cent, r_hi_ok, r_lo_ok = (sem(s) for s in ("m_mm", "m_cent", "r_hi_ok", "r_lo_ok"))
        ap_mm, a_stat, a_var, a_eps, a_rstd = (sem(s) for s in ("ap_mm", "a_stat", "a_var", "a_eps", "a_rstd"))
        y_out = sem("y_out")
        z_ok, z_mean, z_sq, z_var, z_eps, z_rstd, z_fin, x1_ok = (
            sem(s) for s in ("z_ok", "z_mean", "z_sq", "z_var", "z_eps", "z_rstd", "z_fin", "x1_ok"))
        q_tree = sem("q_tree")
        x1_out = sem("x1_out")

        def vec(name, c):
            return vecs[:, VEC[name][0] + c:VEC[name][0] + c + 1]

        def s_cols(c):
            return (0, P) if c == 0 else (C, RW)

        def q_bank(v):
            return aps[:, 1] if v % 2 == 0 else qps[:]

        def m_cols(c):
            return (P, RW) if c == 0 else (0, C)

        def split3(a_hi, a_lo, b_hi, b_lo):
            return ((a_hi, b_hi), (a_lo, b_hi), (a_hi, b_lo))

        def batches(eng, body):
            for par in range(2):
                body(par, 0, par, False, par == 1, True, True, True)
            with eng.Fori(1, NB // 2 - 1) as i:
                for par in range(2):
                    body(2 * i + par, i, par, True, True, True, True, True)
            for par in range(2):
                body(NB - 2 + par, NB // 2 - 1, par, True, True, True, par == 0, False)
            body(NB, NB // 2, 0, True, True, False, False, False)

        block = ctx.enter_context(nc.Block())

        @block.sync
        def _(sp):
            sp.dma_start(w_raw[:, 0], wq).then_inc(w_in, 16)
            sp.dma_start(vecs[:], vecs_d).then_inc(v_in, 16)
            sp.dma_start(rows[:], rows_d).then_inc(v_in, 16)
            sp.dma_start(xc[:], x_chan[0]).then_inc(xc_in, 16)
            for n, w in ((1, wk), (2, wv), (3, wo)):
                sp.dma_start(w_raw[:, n], w).then_inc(w_in, 16)
            sp.dma_start(ident[:], ident_d).then_inc(v_in, 16)
            sp.dma_start(mask[:], mask_d).then_inc(v_in, 16)
            sp.dma_start(xt[:, 0], x_tok[0]).then_inc(xt_in[0], 16)

            sp.wait_ge(xc_lo_ok, 1)
            sp.dma_start(xc[:], x_chan[1]).then_inc(xc_in, 16)

            def step(b, i, par, has_prev2, has_prev, has_k, has_next, has_next2):
                fixed = isinstance(b, int)
                pb2, nb, nb2 = (b + d if fixed else sp.snap(b + d) for d in (-2, 1, 2))
                if has_next2:
                    sp.wait_ge(xc_lo_ok, b + 2)
                    sp.dma_start(xc[:], x_chan[bass.ds(nb2, 1)].rearrange("o p c n -> (o p) c n")
                                 ).then_inc(xc_in, 16)
                if has_prev2:
                    store(pb2, b - 2)
                if has_next:
                    if has_prev:
                        sp.wait_ge(z_ok, T * b)
                    sp.dma_start(xt[:, 1 - par], x_tok[bass.ds(nb, 1)].rearrange("o p t c -> (o p) t c")
                                 ).then_inc(xt_in[1 - par], 16)

            def store(row, b):
                for g in range(NG):
                    sp.wait_ge(x1_ok, T * b + GROUP * (g + 1))
                    sp.dma_start(x1_scratch[bass.ds(row, 1), :, g * GROUP:(g + 1) * GROUP].rearrange(
                        "o p t c -> (o p) t c"), z[:, g * GROUP:(g + 1) * GROUP]).then_inc(x1_out, 16)
            batches(sp, step)
            store(NB - 1, NB - 1)
            sp.wait_ge(x1_out, 16 * NG * NB)

        @block.gpsimd
        def _(pool):
            nc.gpsimd.memset(nhalf[:], -0.5).then_inc(half_ok, 1)

            def chan_lo(b, par):
                pool.wait_ge(xc_hi_ok, b + 1)
                wait_for(pool, k_mm, CH * (b - 1))
                nc.gpsimd.tensor_tensor(xc_lo[:, par], xc[:], xc_hi[:, par].bitcast(F32), ALU.subtract
                                        ).then_inc(xc_lo_ok, 1)

            def tok_lo(b, par):
                pool.wait_ge(xt_hi_ok, b + 1)
                wait_for(pool, xe_mm, b)
                nc.gpsimd.tensor_tensor(xt_lo[:], xt[:, par], xt_hi[:].bitcast(F32), ALU.subtract
                                        ).then_inc(xt_lo_ok, 1)

            def tok_c(b, par):
                pool.wait_ge(xt_lo_ok, b + 1)
                if isinstance(b, int) and b == 0:
                    pool.wait_ge(rows_ok, 2)
                nc.gpsimd.tensor_tensor(xt[:, par], xt[:, par],
                                        c_row[:].rearrange("p (o c) -> p o c", o=1).to_broadcast([P, T, C]),
                                        ALU.add).then_inc(xt_c_ok, 1)

            def q_normalise(b, par, g):
                pool.wait_ge(q_inv, NG * b + g + 1)
                v = qw[:, par, g * GROUP:(g + 1) * GROUP].rearrange("p t (h d) -> p (t h) d", d=D)
                nc.gpsimd.tensor_tensor(
                    v, v, qinv[:, g].rearrange("p (h o) -> p h o", o=1).to_broadcast([P, GROUP * HEADS, D]),
                    ALU.mult).then_inc(q_norm, 1)

            def attention_rstd(b, g):
                gs = slice(g * GROUP, (g + 1) * GROUP)
                pool.wait_ge(a_eps, NG * b + g + 1)
                nc.gpsimd.tensor_tensor(rsA[:, gs], veA[:, gs], nhalf[:, gs], ALU.pow).then_inc(a_rstd, 1)

            def norm_rstd(b, g):
                gs = slice(g * GROUP, (g + 1) * GROUP)
                n = NG * b + g + 1
                pool.wait_ge(z_sq, T * b + GROUP * (g + 1))
                nc.gpsimd.tensor_tensor(vaZ[:, gs], zss[:, gs], inv_c[:, gs], ALU.mult).then_inc(z_var, 1)
                pool.wait_ge(z_var, n)
                nc.gpsimd.tensor_tensor(veZ[:, gs], vaZ[:, gs], eps[:, gs], ALU.add).then_inc(z_eps, 1)
                pool.wait_ge(z_eps, n)
                nc.gpsimd.tensor_tensor(rsZ[:, gs], veZ[:, gs], nhalf[:, gs], ALU.pow).then_inc(z_rstd, 1)
                pool.wait_ge(z_rstd, n)
                nc.gpsimd.tensor_tensor(nmr[:, gs], znm[:, gs], rsZ[:, gs], ALU.mult).then_inc(z_fin, 1)
                nc.gpsimd.tensor_tensor(vaZ[:, gs], vaZ[:, gs], rsZ[:, gs], ALU.mult).then_inc(z_fin, 1)
                pool.wait_ge(z_fin, 4 * n - 2)
                nc.gpsimd.tensor_tensor(vaZ[:, gs], vaZ[:, gs], rsZ[:, gs], ALU.mult).then_inc(z_fin, 1)
                pool.wait_ge(z_fin, 4 * n - 1)
                nc.gpsimd.tensor_tensor(z[:, gs, C], vaZ[:, gs], eps[:, gs], ALU.add).then_inc(z_fin, 1)

            def q_denominator(b, par, g):
                n = NG * b + g
                pool.wait_ge(q_exp, n + 1)
                v = qw[:, par, g * GROUP:(g + 1) * GROUP].rearrange("p t (h d) -> p (t h) d", d=D)
                nc.gpsimd.tensor_tensor(qtree[:, g], v[:, :, 0:8], v[:, :, 8:16], ALU.add).then_inc(q_tree, 1)
                pool.wait_ge(q_tree, 3 * n + 1)
                nc.gpsimd.tensor_tensor(qtree[:, g, :, 0:4], qtree[:, g, :, 0:4], qtree[:, g, :, 4:8], ALU.add
                                        ).then_inc(q_tree, 1)
                pool.wait_ge(q_tree, 3 * n + 2)
                nc.gpsimd.tensor_tensor(qtree[:, g, :, 0:2], qtree[:, g, :, 0:2], qtree[:, g, :, 2:4], ALU.add
                                        ).then_inc(q_tree, 1)
                pool.wait_ge(q_tree, 3 * n + 3)
                nc.gpsimd.tensor_tensor(qsum[:, g], qtree[:, g, :, 0], qtree[:, g, :, 1], ALU.add).then_inc(q_sum, 1)

            nc.gpsimd.memset(inv_c[:], 1.0 / C).then_inc(half_ok, 1)
            nc.gpsimd.memset(eps[:], EPS).then_inc(half_ok, 1)
            pool.wait_ge(half_ok, 3)
            chan_lo(0, 0)
            chan_lo(1, 1)
            for g in range(NG):
                q_denominator(0, 0, g)
            for g in range(NG):
                q_normalise(0, 0, g)

            def step(b, i, par, has_prev2, has_prev, has_k, has_next, has_next2):
                if has_k:
                    tok_lo(b, par)
                    tok_c(b, par)
                if has_next:
                    q_denominator(b + 1, 1 - par, 0)
                if has_next2:
                    chan_lo(b + 2, par)
                if has_prev:
                    attention_rstd(b - 1, 0)
                if has_next:
                    q_denominator(b + 1, 1 - par, 1)
                if has_prev:
                    attention_rstd(b - 1, 1)
                if has_next:
                    q_normalise(b + 1, 1 - par, 0)
                    q_normalise(b + 1, 1 - par, 1)
                if has_prev:
                    norm_rstd(b - 1, 0)
                    norm_rstd(b - 1, 1)
            batches(pool, step)

        @block.scalar
        def _(act):
            def chan_hi(b, par):
                act.wait_ge(xc_in, 16 * (b + 1))
                wait_for(act, k_mm, CH * (b - 1))
                nc.scalar.copy(xc_hi[:, par], xc[:]).then_inc(xc_hi_ok, 1)

            def tok_hi(b, par, n):
                act.wait_ge(xt_in[par], 16 * n)
                wait_for(act, xe_mm, b)
                nc.scalar.copy(xt_hi[:], xt[:, par]).then_inc(xt_hi_ok, 1)

            def q_exponent(b, par, g):
                act.wait_ge(q_sub, PAIRS * b + 2 * (g + 1))
                v = qw[:, par, g * GROUP:(g + 1) * GROUP]
                nc.scalar.activation(v, v, ACT.Exp).then_inc(q_exp, 1)

            def k_exponent(b, c):
                act.wait_ge(k_bias, CH * b + c + 1)
                wait_for(act, et_tr, PAIRS * b)
                wait_for(act, e_inv, CH * b)
                nc.scalar.activation(ek[:, c], ring[:, 2 * c:2 * c + 2].rearrange("p a n -> p (a n)"),
                                     ACT.Exp, bias=kbias[:, c:c + 1], accum_out=esum[:, c:c + 1]
                                     ).then_inc(k_exp, 1)

            def state_high(b):
                act.wait_ge(xe_mm, b + 1)
                nc.scalar.copy(xe_hi[:].rearrange("p a c -> p (a c)"), sps[:]).then_inc(xe_hi_ok, 1)

            def products_out(b, ts):
                for t in ts:
                    act.wait_ge(a_stat, T * b + t + 1)
                    nc.scalar.copy(z[:, t, 0:C], aps[:, t % 2, P:P + C]).then_inc(y_out, 1)

            def pt_high(b, n):
                act.wait_ge(pt_tr, PAIRS * b + n + 1)
                g, c = n // CH, n % CH
                nc.scalar.copy(pt_hi[:, c, g * 512:(g + 1) * 512], ring[:, n]).then_inc(pt_hi_ok, 1)

            def et_high(b, n):
                act.wait_ge(et_tr, PAIRS * b + n + 1)
                nc.scalar.copy(et_hi[:, 2 * n:2 * n + 2].rearrange("p t c -> p (t c)"), ring[:, n]
                               ).then_inc(et_hi_ok, 1)

            def squares(b, g):
                act.wait_ge(z_mean, NG * b + g + 1)
                for t in range(g * GROUP, (g + 1) * GROUP):
                    nc.scalar.activation(zjunk[:, t], z[:, t, 0:C], ACT.Square, bias=znm[:, t:t + 1],
                                         accum_out=zss[:, t:t + 1]).then_inc(z_sq, 1)

            def normalise(b, g):
                act.wait_ge(z_fin, 4 * (NG * b + g + 1))
                for t in range(g * GROUP, (g + 1) * GROUP):
                    nc.scalar.activation(z[:, t, 0:C], z[:, t, 0:C], ACT.Identity, bias=nmr[:, t:t + 1],
                                         scale=rsZ[:, t:t + 1]).then_inc(x1_ok, 1)

            chan_hi(0, 0)
            q_exponent(0, 0, 0)
            chan_hi(1, 1)
            q_exponent(0, 0, 1)

            def step(b, i, par, has_prev2, has_prev, has_k, has_next, has_next2):
                if has_k:
                    k_exponent(b, 0)
                    tok_hi(b, par, i + 1)
                if has_prev2:
                    normalise(b - 2, 0)
                if has_k:
                    k_exponent(b, 1)
                if has_prev:
                    act.wait_ge(st_tr, b)
                    nc.scalar.copy(st_hi[:].rearrange("p a c -> p (a c)"), sps[:, 0:C]).then_inc(st_hi_ok, 1)
                if has_prev2:
                    normalise(b - 2, 1)
                if has_prev:
                    act.wait_ge(m_cent, CH * b)
                    nc.scalar.copy(r_hi[:], r_f[:]).then_inc(r_hi_ok, 1)
                if has_next:
                    q_exponent(b + 1, 1 - par, 0)
                if has_next2:
                    chan_hi(b + 2, par)
                if has_prev:
                    wait_for(act, x1_out, 16 * NG * (b - 1))
                    products_out(b - 1, range(0, 4))
                if has_k:
                    pt_high(b, 0)
                    pt_high(b, 1)
                if has_prev:
                    products_out(b - 1, range(4, 6))
                if has_k:
                    et_high(b, 0)
                if has_prev:
                    products_out(b - 1, range(6, 8))
                if has_k:
                    et_high(b, 1)
                    pt_high(b, 2)
                    pt_high(b, 3)
                if has_next:
                    q_exponent(b + 1, 1 - par, 1)
                if has_k:
                    et_high(b, 2)
                    et_high(b, 3)
                if has_k:
                    state_high(b)
                if has_prev:
                    squares(b - 1, 0)
                    squares(b - 1, 1)
            batches(act, step)
            normalise(NB - 1, 0)
            normalise(NB - 1, 1)

        @block.vector
        def _(dve):
            nc.vector.memset(ones[:], 1.0).then_inc(consts, 1)
            nc.vector.memset(part[:].bitcast(F32), 1.0 / P).then_inc(consts, 1)

            def split_lo(out, full, hi):
                return nc.vector.tensor_tensor(out, full, hi.bitcast(F32), ALU.subtract)

            dve.wait_ge(w_in, 64)
            dve.wait_ge(v_in, 64)
            for c in range(CH):
                nc.vector.tensor_scalar(lnb_wo[:, c], w_raw[:, 3, c], vec("ln_b", c), None, ALU.mult
                                        ).then_inc(w_scaled, 1)
            dve.wait_ge(w_scaled, CH)
            for c in range(CH):
                nc.vector.tensor_scalar(w_raw[:, 3, c], w_raw[:, 3, c], vec("ln_g", c), None, ALU.mult
                                        ).then_inc(w_scaled, 1)
            nc.vector.tensor_copy(bq_hi[:], rows[:, ROW["bq"]]).then_inc(w_split_hi, 1)
            dve.wait_ge(w_scaled, 2 * CH)
            nc.vector.tensor_copy(w_hi[:].rearrange("p w a c -> p (w a c)"),
                                  w_raw[:].rearrange("p w a c -> p (w a c)")).then_inc(w_split_hi, 1)
            dve.wait_ge(w_split_hi, 2)
            split_lo(bq_lo[:], rows[:, ROW["bq"]], bq_hi[:]).then_inc(w_split, 1)
            split_lo(w_lo[:].rearrange("p w a c -> p (w a c)"), w_raw[:].rearrange("p w a c -> p (w a c)"),
                     w_hi[:].rearrange("p w a c -> p (w a c)")).then_inc(w_split, 1)
            dve.wait_ge(rows_mm, 1)
            nc.vector.tensor_copy(u_row[:], sps[:, 0:C]).then_inc(rows_ok, 1)
            nc.vector.tensor_tensor(c_row[:], aps[:, 0, 0:C], rows[:, ROW["bo"]], ALU.add).then_inc(rows_ok, 1)

            def q_centre(b, par, v):
                dve.wait_ge(q_mm, PAIRS * b + v + 1)
                src = q_bank(v).rearrange("p (h d) -> p h d", d=D)
                nc.vector.tensor_reduce(qmx[:, v % 2], src, AX_X, ALU.max).then_inc(q_max, 1)
                dve.wait_ge(q_max, PAIRS * b + v + 1)
                nc.vector.tensor_tensor(
                    qw[:, par, 2 * v:2 * v + 2].rearrange("p t (h d) -> p (t h) d", d=D), src,
                    qmx[:, v % 2].rearrange("p (h o) -> p h o", o=1).to_broadcast([P, 2 * HEADS, D]),
                    ALU.subtract).then_inc(q_sub, 1)

            def q_inverse(b, g):
                dve.wait_ge(q_sum, NG * b + g + 1)
                nc.vector.reciprocal(qinv[:, g], qsum[:, g]).then_inc(q_inv, 1)

            def k_maximum(b, c):
                dve.wait_ge(k_mm, CH * b + c + 1)
                nc.vector.tensor_reduce(kmx[:, c:c + 1], ring[:, 2 * c:2 * c + 2].rearrange(
                    "p a n -> p (a n)"), AX_X, ALU.max).then_inc(k_max, 1)
                dve.wait_ge(k_max, CH * b + c + 1)
                nc.vector.tensor_tensor(kbm[:, c:c + 1], kmx[:, c:c + 1], vec("bk", c), ALU.add
                                        ).then_inc(k_maxb, 1)
                dve.wait_ge(k_maxb, CH * b + c + 1)
                nc.vector.tensor_tensor(kbias[:, c:c + 1], vec("bk", c), kbm[:, c:c + 1], ALU.subtract
                                        ).then_inc(k_bias, 1)

            def state(b):
                dve.wait_ge(s_mm, b + 1)
                for c in range(CH):
                    nc.vector.scalar_tensor_tensor(
                        out=s_f[:, c], in0=sps[:, c * C + c * P:c * C + (c + 1) * P], scalar=einv[:, c:c + 1],
                        in1=rows[:, ROW["bv"], c * P:(c + 1) * P], op0=ALU.mult, op1=ALU.add).then_inc(s_norm, 1)
                dve.wait_ge(s_norm, CH * (b + 1))
                for c in range(CH):
                    s0, s1 = s_cols(c)
                    nc.vector.tensor_tensor(r_f[:, c, s0:s1], s_f[:, c], mask[:], ALU.mult).then_inc(s_mask, 1)
                dve.wait_ge(s_mask, CH * (b + 1))
                for c in range(CH):
                    s0, s1 = s_cols(c)
                    nc.vector.tensor_reduce(srow[:, c:c + 1], r_f[:, c, s0:s1], AX_X, ALU.add).then_inc(s_sum, 1)
                dve.wait_ge(s_sum, CH * (b + 1))
                nc.vector.tensor_scalar(nmean[:], srow[:], -1.0 / C, None, ALU.mult).then_inc(s_mean, 1)

            def state_low(b):
                dve.wait_ge(st_hi_ok, b + 1)
                split_lo(st_lo[:].rearrange("p a c -> p (a c)"), sps[:, 0:C],
                         st_hi[:].rearrange("p a c -> p (a c)")).then_inc(st_lo_ok, 1)

            def projected(b):
                dve.wait_ge(m_mm, b + 1)
                dve.wait_ge(s_mean, b + 1)
                for c in range(CH):
                    m0, m1 = m_cols(c)
                    nc.vector.scalar_tensor_tensor(
                        out=r_f[:, c, m0:m1], in0=u_row[:], scalar=nmean[:, c:c + 1],
                        in1=sps[:, c * C:(c + 1) * C], op0=ALU.mult, op1=ALU.add).then_inc(m_cent, 1)
                dve.wait_ge(r_hi_ok, b + 1)
                split_lo(r_lo[:], r_f[:], r_hi[:]).then_inc(r_lo_ok, 1)

            def out_variance(b, g):
                ts = range(g * GROUP, (g + 1) * GROUP)
                gs = slice(g * GROUP, (g + 1) * GROUP)
                dve.wait_ge(a_stat, T * b + GROUP * (g + 1))
                nc.vector.memset(fence[:], 0.0)
                for t in ts:
                    nc.vector.bn_aggr(mvA[:, t], bnA[:, t]).then_inc(a_var, 1)
                dve.wait_ge(a_var, T * b + GROUP * (g + 1))
                nc.vector.tensor_scalar(veA[:, gs], mvA[:, gs, 1], EPS, None, ALU.add).then_inc(a_eps, 1)

            def residual(b, par, g):
                dve.wait_ge(a_rstd, NG * b + g + 1)
                dve.wait_ge(xt_c_ok, b + 1)
                dve.wait_ge(y_out, T * b + GROUP * (g + 1))
                for t in range(g * GROUP, (g + 1) * GROUP):
                    nc.vector.scalar_tensor_tensor(
                        out=z[:, t, 0:C], in0=z[:, t, 0:C], scalar=rsA[:, t:t + 1],
                        in1=xt[:, par, t], op0=ALU.mult, op1=ALU.add, accum_out=zsum[:, t:t + 1]).then_inc(z_ok, 1)
                gs = slice(g * GROUP, (g + 1) * GROUP)
                dve.wait_ge(z_ok, T * b + GROUP * (g + 1))
                nc.vector.tensor_scalar(znm[:, gs], zsum[:, gs], -1.0 / C, None, ALU.mult).then_inc(z_mean, 1)

            def products_stats(b, ts):
                for t in ts:
                    dve.wait_ge(ap_mm, T * b + t + 1)
                    nc.vector.bn_stats(bnA[:, t], aps[:, t % 2].rearrange("p (a c) -> p a c", c=P)[:, 0:4:3]
                                       ).then_inc(a_stat, 1)

            def pt_low(b, n):
                dve.wait_ge(pt_hi_ok, PAIRS * b + n + 1)
                g, c = n // CH, n % CH
                seg = slice(g * 512, (g + 1) * 512)
                split_lo(pt_lo[:, c, seg], ring[:, n], pt_hi[:, c, seg]).then_inc(pt_lo_ok, 1)

            def et_low(b, n):
                dve.wait_ge(et_hi_ok, PAIRS * b + n + 1)
                split_lo(et_lo[:, 2 * n:2 * n + 2].rearrange("p t c -> p (t c)"), ring[:, n],
                         et_hi[:, 2 * n:2 * n + 2].rearrange("p t c -> p (t c)")).then_inc(et_lo_ok, 1)

            for v in range(PAIRS):
                q_centre(0, 0, v)
            for g in range(NG):
                q_inverse(0, g)

            def step(b, i, par, has_prev2, has_prev, has_k, has_next, has_next2):
                if has_k:
                    k_maximum(b, 0)
                if has_prev:
                    state(b - 1)
                if has_k:
                    k_maximum(b, 1)
                if has_next:
                    q_centre(b + 1, 1 - par, 0)
                if has_prev:
                    state_low(b - 1)
                if has_next:
                    q_centre(b + 1, 1 - par, 1)
                if has_prev:
                    projected(b - 1)
                if has_next:
                    q_centre(b + 1, 1 - par, 2)
                if has_prev:
                    products_stats(b - 1, range(0, 1))
                if has_next:
                    q_centre(b + 1, 1 - par, 3)
                if has_prev:
                    products_stats(b - 1, range(1, 4))
                if has_k:
                    pt_low(b, 0)
                    pt_low(b, 1)
                if has_prev:
                    products_stats(b - 1, range(4, 6))
                    out_variance(b - 1, 0)
                if has_k:
                    et_low(b, 0)
                    dve.wait_ge(k_exp, CH * (b + 1))
                    nc.vector.reciprocal(einv[:], esum[:]).then_inc(e_inv, CH)
                if has_prev:
                    products_stats(b - 1, range(6, 8))
                if has_k:
                    et_low(b, 1)
                    pt_low(b, 2)
                    pt_low(b, 3)
                if has_prev:
                    out_variance(b - 1, 1)
                if has_k:
                    et_low(b, 2)
                if has_next:
                    q_inverse(b + 1, 0)
                if has_k:
                    et_low(b, 3)
                if has_prev:
                    residual(b - 1, 1 - par, 0)
                if has_k:
                    dve.wait_ge(xe_hi_ok, b + 1)
                    split_lo(xe_lo[:].rearrange("p a c -> p (a c)"), sps[:],
                             xe_hi[:].rearrange("p a c -> p (a c)")).then_inc(xe_lo_ok, 1)
                if has_prev:
                    residual(b - 1, 1 - par, 1)
                if has_next:
                    q_inverse(b + 1, 1)
            batches(dve, step)

        @block.tensor
        def _(pe):
            pe.wait_ge(consts, 2)
            pe.wait_ge(w_scaled, 2 * CH)
            pe.wait_ge(v_in, 64)
            for dst, src in ((sps[:, 0:C], w_raw[:, 3]), (aps[:, 0, 0:C], lnb_wo[:])):
                for c in range(CH):
                    last = nc.tensor.matmul(dst, ones[:], src[:, c], start=(c == 0), stop=(c == CH - 1))
            last.then_inc(rows_mm, 1)
            pe.wait_ge(w_split, 2)

            def q_product(b, par, v):
                if v == 0:
                    pe.wait_ge(xc_lo_ok, b + 1)
                wait_for(pe, q_sub, PAIRS * b + v - 1)
                if v == 0:
                    wait_for(pe, y_out, T * (b - 2))
                for h in range(2):
                    t = 2 * v + h
                    out = q_bank(v)[:, h * C:(h + 1) * C]
                    nc.tensor.matmul(out, part[:], bq_hi[:], start=(h == 0), stop=False, skip_group_check=True)
                    nc.tensor.matmul(out, part[:], bq_lo[:], start=False, stop=False, skip_group_check=True)
                    for c in range(CH):
                        ts = slice(t * P, (t + 1) * P)
                        for k, (a, w) in enumerate(split3(xc_hi[:, par, c, ts], xc_lo[:, par, c, ts],
                                                          w_hi[:, 0, c], w_lo[:, 0, c])):
                            last = nc.tensor.matmul(out, a, w, start=False, stop=(c == CH - 1 and k == 2),
                                                    skip_group_check=True)
                last.then_inc(q_mm, 1)

            for v in range(PAIRS):
                q_product(0, 0, v)

            def k_product(b, par, m, h):
                n = 0
                for c in range(CH):
                    ms, ns = slice(m * P, (m + 1) * P), slice(h * 512, (h + 1) * 512)
                    for w, a in split3(w_hi[:, 1, c, ms], w_lo[:, 1, c, ms],
                                       xc_hi[:, par, c, ns], xc_lo[:, par, c, ns]):
                        last = nc.tensor.matmul(ring[:, 2 * m + h], w, a, start=(n == 0), stop=(n == 5))
                        n += 1
                if h == 1:
                    last.then_inc(k_mm, 1)

            def state_product(b):
                pe.wait_ge(xe_lo_ok, b + 1)
                for d in range(CH):
                    for a in range(CH):
                        ds = slice(d * P, (d + 1) * P)
                        for k, (l, r) in enumerate(split3(xe_hi[:, a, ds], xe_lo[:, a, ds],
                                                          w_hi[:, 2, a], w_lo[:, 2, a])):
                            last = nc.tensor.matmul(sps[:, d * C:(d + 1) * C], l, r,
                                                    start=(d == 0 and a == 0 and k == 0),
                                                    stop=(a == CH - 1 and k == 2), skip_group_check=True)
                last.then_inc(s_mm, 1)

            def state_transpose(b):
                pe.wait_ge(s_mask, CH * (b + 1))
                for c in range(CH):
                    s0, s1 = s_cols(c)
                    last = nc.tensor.transpose(sps[:, c * P:(c + 1) * P], r_f[:, c, s0:s1], ident[:])
                last.then_inc(st_tr, 1)

            def state_project(b):
                pe.wait_ge(st_lo_ok, b + 1)
                for c in range(CH):
                    for k, (l, r) in enumerate(split3(st_hi[:, c], st_lo[:, c], w_hi[:, 3, c], w_lo[:, 3, c])):
                        last = nc.tensor.matmul(sps[:, c * C:(c + 1) * C], l, r, start=(c == 0 and k == 0),
                                                stop=(k == 2), skip_group_check=True)
                last.then_inc(m_mm, 1)

            def attend(b, t, after_q):
                if t == 0:
                    pe.wait_ge(r_lo_ok, b + 1)
                if t == 1 and after_q:
                    pe.wait_ge(q_sub, PAIRS * (b + 3) - 1)
                if t >= 2 or not (isinstance(b, int) and b == 0):
                    pe.wait_ge(y_out, T * b + t - 1)
                ts = slice(t * P, (t + 1) * P)
                for c in range(CH):
                    out = aps[:, t % 2, c * P:c * P + RW]
                    for k, (l, r) in enumerate(split3(pt_hi[:, c, ts], pt_lo[:, c, ts],
                                                      r_hi[:, c], r_lo[:, c])):
                        last = nc.tensor.matmul(out, l, r, start=(c == 0 and k == 0),
                                                stop=(c == CH - 1 and k == 2), skip_group_check=True)
                last.then_inc(ap_mm, 1)

            def state_sum(b, n):
                pe.wait_ge(et_lo_ok, PAIRS * b + n + 1)
                if n == 0:
                    pe.wait_ge(xt_lo_ok, b + 1)
                for t in (2 * n, 2 * n + 1):
                    for a in range(CH):
                        as_ = slice(a * P, (a + 1) * P)
                        for k, (x, e) in enumerate(split3(xt_hi[:, t, as_], xt_lo[:, t, as_],
                                                          et_hi[:, t], et_lo[:, t])):
                            last = nc.tensor.matmul(
                                sps[:, a * C:(a + 1) * C], x, e, start=(t == 0 and a == 0 and k == 0),
                                stop=(t == T - 1 and k == 2), skip_group_check=True)
                if n == PAIRS - 1:
                    last.then_inc(xe_mm, 1)

            def q_transposes(b, par, g):
                for c in range(CH):
                    n = g * CH + c
                    pe.wait_ge(k_exp, CH * b + n // 2 + 1)
                    pe.wait_ge(q_norm, NG * b + g + 1)
                    for j in range(GROUP):
                        last = nc.tensor.transpose(ring[:, n, j * P:(j + 1) * P],
                                                   qw[:, par, g * GROUP + j, c * P:(c + 1) * P], ident[:])
                    last.then_inc(pt_tr, 1)

            def e_transposes(b, n):
                pe.wait_ge(pt_lo_ok, PAIRS * b + n + 1)
                for h in range(2):
                    for c in range(CH):
                        t = 2 * n + h
                        last = nc.tensor.transpose(ring[:, n, h * C + c * P:h * C + (c + 1) * P],
                                                   ek[:, c, t * P:(t + 1) * P], ident[:])
                last.then_inc(et_tr, 1)

            def step(b, i, par, has_prev2, has_prev, has_k, has_next, has_next2):
                if has_k:
                    wait_for(pe, et_lo_ok, PAIRS * b)
                    k_product(b, par, 0, 0)
                    k_product(b, par, 0, 1)
                    k_product(b, par, 1, 0)
                if has_prev:
                    state_product(b - 1)
                if has_k:
                    k_product(b, par, 1, 1)
                if has_next:
                    q_product(b + 1, 1 - par, 0)
                if has_prev:
                    state_transpose(b - 1)
                if has_next:
                    q_product(b + 1, 1 - par, 1)
                if has_prev:
                    state_project(b - 1)
                if has_next:
                    q_product(b + 1, 1 - par, 2)
                    q_product(b + 1, 1 - par, 3)
                for h in range(2):
                    for j in range(2):
                        if has_prev:
                            attend(b - 1, 4 * h + 2 * j, has_next)
                            attend(b - 1, 4 * h + 2 * j + 1, has_next)
                        if h == 1 and has_k:
                            e_transposes(b, j)
                    if has_k:
                        q_transposes(b, par, h)
                if has_k:
                    state_sum(b, 0)
                    e_transposes(b, 2)
                    state_sum(b, 1)
                    e_transposes(b, 3)
                    state_sum(b, 2)
                    state_sum(b, 3)
            batches(pe, step)


def feed_forward_phase(nc, x1_scratch, w1, w2, vecs_d, rows_d, ident_d, out):
    NB, _, T, _ = x1_scratch.shape
    C = w2.shape[2]
    CH = C // P
    F = w1.shape[2]
    FC = F // P
    TB = 4
    TOK = TB * P
    NK = NB * T // TB
    DEPTH = 4
    LAG = 3
    POOL_SQ = 3
    assert NK % 2 == 0 and T == 2 * TB

    with ExitStack() as ctx:
        def sb(name, shape, dt=F32):
            return ctx.enter_context(nc.sbuf_tensor("ff_" + name, shape, dt))

        def sem(name):
            return ctx.enter_context(nc.semaphore("ff_" + name))

        hps = ctx.enter_context(nc.psum_tensor("hps", [P, 2, TOK], F32))
        tps = ctx.enter_context(nc.psum_tensor("tps", [P, 2, TOK], F32))
        yps = ctx.enter_context(nc.psum_tensor("yps", [P, 2, TB, C], F32))

        x1 = sb("x1", [P, 2, TB, C + 1])
        x1c = sb("x1c", [P, 2, TB, C])
        xn = sb("xn", [P, TB, C])
        ht_hi, ht_lo = sb("ht_hi", [P, 2, CH, TOK], F32R), sb("ht_lo", [P, 2, CH, TOK], F32R)
        gel = sb("gel", [P, FC, TOK])
        sq = sb("sq", [P, FC, TOK])
        a_hi, a_lo = sb("a_hi", [P, DEPTH, TOK], F32R), sb("a_lo", [P, DEPTH, TOK], F32R)
        acc = sb("acc", [P, 2, 2, TOK])
        accp = sb("accp", [P, TOK])
        z = sb("z", [P, 2, TB, C])
        w1f = sb("w1f", [P, CH, F])
        w2f = sb("w2f", [P, FC, C])
        wm = sb("wm", [P, CH * F])
        t1 = sb("t1", [P, CH, F], F32R)
        t2 = sb("t2", [P, FC, C], F32R)
        vecs = sb("vecs", [P, NVEC])
        rows = sb("rows", [P, 4, C])
        ident = sb("ident", [P, P])
        ones = sb("ones", [P, P])
        wabs = sb("wabs", [P, 2])
        wmean = sb("wmean", [P, 2])
        wscale = sb("wscale", [P, 2])
        wstep = sb("wstep", [P, 2])
        bias1 = sb("bias1", [P, FC])
        u_row = sb("u_row", [P, C])
        c_row = sb("c_row", [P, C])
        rs1 = sb("rs1", [P, TB])
        bnZ, mvZ, veZ, rsZ = sb("bnZ", [P, TB, 6]), sb("mvZ", [P, TB, 2]), sb("veZ", [P, TB]), sb("rsZ", [P, TB])
        nmr = sb("nmr", [P, TB])
        sums = sb("sums", [P, 2 * TB])
        nmu = sb("nmu", [P, TB])
        msq = sb("msq", [P, TB])
        var = sb("var", [P, TB])
        rsH = sb("rsH", [P, TB])
        gain = sb("gain", [P, TB])
        yc = sb("yc", [P, TB, C])
        nhalf = sb("nhalf", [P, TB])

        fence = sb("fence", [P, 1])

        x1_in = [sem(f"x1_in{n}") for n in range(2)]
        w_in, v_in, consts, half_ok = sem("w_in"), sem("v_in"), sem("consts"), sem("half_ok")
        w_abs, w_sum, w_mean, w_scale, w_step = (sem(s) for s in ("w_abs", "w_sum", "w_mean", "w_scale", "w_step"))
        w_neg, w_pos, w_tern, w_sc2 = (sem(s) for s in ("w_neg", "w_pos", "w_tern", "w_sc2"))
        fold_mm, fold_t, fold_ok = sem("fold_mm"), sem("fold_t"), sem("fold_ok")
        n_rstd, n_ok = sem("n_rstd"), sem("n_ok")
        x1c_ok = sem("x1c_ok")
        ht_tr, ht_hi_ok, ht_lo_ok = (sem(s) for s in ("ht_tr", "ht_hi_ok", "ht_lo_ok"))
        h_mm, gelu_ok, hi_ok, lo_ok, sq_ok = (sem(s) for s in ("h_mm", "gelu_ok", "hi_ok", "lo_ok", "sq_ok"))
        y_mm = sem("y_mm")
        sum_g, sum_p, sum_q = sem("sum_g"), sem("sum_p"), sem("sum_q")
        r_tr, r_sum, r_mean, r_sq, r_var, r_eps, r_rstd, r_gain = (
            sem(s) for s in ("r_tr", "r_sum", "r_mean", "r_sq", "r_var", "r_eps", "r_rstd", "r_gain"))
        yc_ok, z_ok, z_stat, z_var, z_eps, z_rstd, z_nmr, o_ok = (
            sem(s) for s in ("yc_ok", "z_ok", "z_stat", "z_var", "z_eps", "z_rstd", "z_nmr", "o_ok"))
        o_out = [sem(f"o_out{n}") for n in range(2)]
        Q_ADDS = FC - POOL_SQ
        P_ADDS = POOL_SQ - 1

        def vec(name, c):
            return vecs[:, VEC[name][0] + c:VEC[name][0] + c + 1]

        def blocks(eng, body):
            for par in range(2):
                body(par, 0, par, par == 0, False)
            with eng.Fori(1, NK // 2 - 1) as i:
                for par in range(2):
                    body(2 * i + par, i, par, False, False)
            for par in range(2):
                body(NK - 2 + par, NK // 2 - 1, par, False, par == 1)

        def before2(k):
            return not isinstance(k, int) or k >= 2

        block = ctx.enter_context(nc.Block())

        @block.sync
        def _(sp):
            sp.dma_start(w1f[:], w1).then_inc(w_in, 16)
            sp.dma_start(w2f[:], w2).then_inc(w_in, 16)
            sp.dma_start(x1[:, 0], x1_scratch[0, :, 0:TB]).then_inc(x1_in[0], 16)
            sp.dma_start(vecs[:], vecs_d).then_inc(v_in, 16)
            sp.dma_start(rows[:], rows_d).then_inc(v_in, 16)
            sp.dma_start(ident[:], ident_d).then_inc(v_in, 16)

            def step(k, i, par, first, last):
                if not last:
                    if not first:
                        sp.wait_ge(n_ok, TB * k)
                        sp.wait_ge(x1c_ok, k)
                    src = x1_scratch[bass.ds(i, 1), :, TB:T] if par == 0 else x1_scratch[bass.ds(i + 1, 1), :, 0:TB]
                    sp.dma_start(x1[:, 1 - par], src.rearrange("o p t c -> (o p) t c")).then_inc(x1_in[1 - par], 16)
                if before2(k):
                    store(sp, k - 2, i - 1, par)

            def store(sp, k, i, par):
                dst = out.rearrange("b p t c -> (b p) t c")[bass.ds(i * P, P), par * TB:(par + 1) * TB]
                sp.wait_ge(o_ok, TB * (k + 1))
                sp.dma_start(dst, z[:, par]).then_inc(o_out[par], 16)
            blocks(sp, step)
            for par in range(2):
                store(sp, NK - 2 + par, NK // 2 - 1, par)
            for par in range(2):
                sp.wait_ge(o_out[par], 8 * NK)

        @block.gpsimd
        def _(pool):
            nc.gpsimd.memset(nhalf[:], -0.5).then_inc(half_ok, 1)
            pool.wait_ge(half_ok, 1)

            def pow_half(o, v, ready, n, done):
                pool.wait_ge(ready, n)
                nc.gpsimd.tensor_tensor(o[:], v[:], nhalf[:], ALU.pow).then_inc(done, 1)

            def keep_residual(k, par, n):
                pool.wait_ge(x1_in[par], 16 * n)
                if isinstance(k, int) and k == 0:
                    pool.wait_ge(fold_ok, 3)
                if not (isinstance(k, int) and k < 2):
                    pool.wait_ge(z_ok, TB * (k - 1))
                nc.gpsimd.tensor_tensor(x1c[:, par], x1[:, par, :, 0:C],
                                        c_row[:].rearrange("p (o c) -> p o c", o=1).to_broadcast([P, TB, C]),
                                        ALU.add).then_inc(x1c_ok, 1)

            def norm_rstd(k, par, n):
                pool.wait_ge(x1_in[par], 16 * n)
                wait_for(pool, n_ok, TB * k)
                nc.gpsimd.tensor_tensor(rs1[:], x1[:, par, :, C], nhalf[:], ALU.pow).then_inc(n_rstd, 1)

            norm_rstd(0, 0, 1)

            def step(k, i, par, first, last):
                if not last:
                    norm_rstd(k + 1, 1 - par, i + 1 + par)
                for m in range(1, FC):
                    pool.wait_ge(gelu_ok, FC * k + m + 1)
                    if m > 1:
                        pool.wait_ge(sum_g, (FC - 1) * k + m - 1)
                    elif not (isinstance(k, int) and k < 2):
                        pool.wait_ge(r_tr, k - 1)
                    a = gel[:, 0] if m == 1 else acc[:, par, 0]
                    nc.gpsimd.tensor_tensor(acc[:, par, 0], a, gel[:, m], ALU.add).then_inc(sum_g, 1)
                    if 1 <= m < POOL_SQ:
                        pool.wait_ge(sq_ok, FC * k + m + 1)
                        if m > 1:
                            pool.wait_ge(sum_p, P_ADDS * k + m - 1)
                        elif not first:
                            pool.wait_ge(sum_q, Q_ADDS * k)
                        a = sq[:, 0] if m == 1 else accp[:]
                        nc.gpsimd.tensor_tensor(accp[:], a, sq[:, m], ALU.add).then_inc(sum_p, 1)
                    if m == 3 and not first:
                        pow_half(rsH, var, r_eps, k, r_rstd)
                    if m == 5:
                        keep_residual(k, par, i + 1)
                    if m == 7 and not first:
                        wait_for(pool, o_ok, TB * (k - 1))
                        pow_half(rsZ, veZ, z_eps, k, z_rstd)

            blocks(pool, step)
            pow_half(rsH, var, r_eps, NK, r_rstd)
            pool.wait_ge(o_ok, TB * (NK - 1))
            pow_half(rsZ, veZ, z_eps, NK, z_rstd)

        @block.scalar
        def _(act):
            def ht_high(k, par):
                for c in range(CH):
                    act.wait_ge(ht_tr, CH * k + c + 1)
                    nc.scalar.activation(ht_hi[:, par, c], tps[:, c], ACT.Copy, scale=vec("ln1_g", c)
                                         ).then_inc(ht_hi_ok, 1)

            def normalise_out(k, par, h):
                act.wait_ge(z_nmr, k + 1)
                for t in range(h * TB // 2, (h + 1) * TB // 2):
                    nc.scalar.activation(z[:, par, t], z[:, par, t], ACT.Identity, bias=nmr[:, t:t + 1],
                                         scale=rsZ[:, t:t + 1]).then_inc(o_ok, 1)

            act.wait_ge(v_in, 48)
            ht_high(0, 0)
            act.wait_ge(w_step, 1)
            act.wait_ge(fold_ok, 1)

            def gelu(k, m, first):
                act.wait_ge(h_mm, FC * k + m + 1)
                if not first:
                    act.wait_ge(lo_ok, FC * (k - 1) + m + 1)
                    act.wait_ge(sum_g, (FC - 1) * (k - 1) + max(m, 1))
                nc.scalar.activation(gel[:, m], hps[:, m % 2], ACT.Gelu, bias=bias1[:, m:m + 1],
                                     scale=wstep[:, 0:1]).then_inc(gelu_ok, 1)

            def high_and_square(k, m, first):
                act.wait_ge(gelu_ok, FC * k + m + 1)
                if m >= DEPTH or not first:
                    act.wait_ge(y_mm, FC * k + m - DEPTH + 1)
                nc.scalar.activation(a_hi[:, m % DEPTH], gel[:, m], ACT.Copy, scale=vec("ln2_g", m)
                                     ).then_inc(hi_ok, 1)
                if not first:
                    if m < POOL_SQ:
                        act.wait_ge(sum_p, P_ADDS * (k - 1) + max(m, 1))
                    else:
                        act.wait_ge(sum_q, Q_ADDS * (k - 1) + max(m - POOL_SQ, 1))
                nc.scalar.activation(sq[:, m], gel[:, m], ACT.Square).then_inc(sq_ok, 1)

            def step(k, i, par, first, last):
                for m in range(FC):
                    gelu(k, m, first)
                    if m > 0:
                        high_and_square(k, m - 1, first)
                    elif not first:
                        high_and_square(k - 1, FC - 1, isinstance(k, int) and k == 1)
                    if m in (1, 2) and before2(k):
                        normalise_out(k - 2, par, m - 1)
                    if m == 4 and not last:
                        ht_high(k + 1, 1 - par)
            blocks(act, step)
            high_and_square(NK - 1, FC - 1, False)
            for par in range(2):
                for h in range(2):
                    normalise_out(NK - 2 + par, par, h)

        @block.vector
        def _(dve):
            nc.vector.memset(ones[:], 1.0).then_inc(consts, 1)

            dve.wait_ge(w_in, 32)
            flat = (w1f[:].rearrange("p a f -> p (a f)"), w2f[:].rearrange("p a f -> p (a f)"))
            tern = (t1[:].rearrange("p a f -> p (a f)"), t2[:].rearrange("p a f -> p (a f)"))
            for n in range(2):
                nc.vector.tensor_reduce(wabs[:, n:n + 1], flat[n], AX_X, ALU.add, apply_absolute_value=True
                                        ).then_inc(w_abs, 1)
            dve.wait_ge(w_sum, 1)
            nc.vector.tensor_scalar(wmean[:], hps[:, 0, 0:2], 1.0 / (C * F), 1e-5, ALU.mult, ALU.max
                                    ).then_inc(w_mean, 1)
            dve.wait_ge(w_mean, 1)
            nc.vector.reciprocal(wscale[:], wmean[:]).then_inc(w_scale, 1)
            dve.wait_ge(w_scale, 1)
            nc.vector.reciprocal(wstep[:], wscale[:]).then_inc(w_step, 1)
            for n in range(2):
                if n:
                    dve.wait_ge(w_tern, n)
                nc.vector.tensor_scalar(wm[:], flat[n], wscale[:, n:n + 1], -0.5, ALU.mult, ALU.is_lt
                                        ).then_inc(w_neg, 1)
                nc.vector.tensor_scalar(flat[n], flat[n], wscale[:, n:n + 1], 0.5, ALU.mult, ALU.is_gt
                                        ).then_inc(w_pos, 1)
                dve.wait_ge(w_neg, n + 1)
                dve.wait_ge(w_pos, n + 1)
                nc.vector.tensor_tensor(tern[n], flat[n], wm[:], ALU.subtract).then_inc(w_tern, 1)
            dve.wait_ge(w_tern, 2)
            dve.wait_ge(v_in, 48)
            for m in range(FC):
                nc.vector.tensor_scalar(w2f[:, m], t2[:, m].bitcast(F32), vec("ln2_g", m), None, ALU.mult
                                        ).then_inc(w_sc2, 1)
                nc.vector.tensor_scalar(wm[:, m * C:(m + 1) * C], t2[:, m].bitcast(F32), vec("ln2_b", m), None,
                                        ALU.mult).then_inc(w_sc2, 1)
            dve.wait_ge(fold_mm, 1)
            nc.vector.scalar_tensor_tensor(
                out=bias1[:], in0=hps[:, 1, 0:FC], scalar=wstep[:, 0:1],
                in1=vecs[:, VEC["b1"][0]:VEC["b1"][0] + FC], op0=ALU.mult, op1=ALU.add).then_inc(fold_ok, 1)
            nc.vector.tensor_copy(u_row[:], yps[:, 0, 0]).then_inc(fold_ok, 1)
            nc.vector.scalar_tensor_tensor(
                out=c_row[:], in0=yps[:, 1, 0], scalar=wstep[:, 1:2], in1=rows[:, ROW["b2"]],
                op0=ALU.mult, op1=ALU.add).then_inc(fold_ok, 1)

            def norm_apply(k, par):
                dve.wait_ge(n_rstd, k + 1)
                if not (isinstance(k, int) and k == 0):
                    dve.wait_ge(ht_tr, CH * k)
                for t in range(TB):
                    nc.vector.tensor_scalar(xn[:, t], x1[:, par, t, 0:C], rs1[:, t:t + 1], None, ALU.mult
                                            ).then_inc(n_ok, 1)

            def ht_low(k, par):
                for c in range(CH):
                    dve.wait_ge(ht_hi_ok, CH * k + c + 1)
                    nc.vector.scalar_tensor_tensor(
                        out=ht_lo[:, par, c], in0=tps[:, c], scalar=vec("ln1_g", c),
                        in1=ht_hi[:, par, c].bitcast(F32), op0=ALU.mult, op1=ALU.subtract).then_inc(ht_lo_ok, 1)

            def hidden_stats(k):
                dve.wait_ge(r_tr, k + 1)
                nc.vector.tensor_reduce(sums[:], tps[:].rearrange("p a (t n) -> p (a t) n", n=P), AX_X, ALU.add
                                        ).then_inc(r_sum, 1)
                dve.wait_ge(r_sum, k + 1)
                nc.vector.tensor_scalar(nmu[:], sums[:, 0:TB], -1.0 / F, None, ALU.mult).then_inc(r_mean, 1)
                dve.wait_ge(r_mean, k + 1)
                nc.vector.tensor_tensor(msq[:], nmu[:], nmu[:], ALU.mult).then_inc(r_sq, 1)
                dve.wait_ge(r_sq, k + 1)
                nc.vector.scalar_tensor_tensor(out=var[:], in0=sums[:, TB:2 * TB], scalar=1.0 / F, in1=msq[:],
                                               op0=ALU.mult, op1=ALU.subtract).then_inc(r_var, 1)
                dve.wait_ge(r_var, k + 1)
                nc.vector.tensor_scalar(var[:], var[:], 0.0, EPS, ALU.max, ALU.add).then_inc(r_eps, 1)

            def centre_y(k, par):
                dve.wait_ge(y_mm, FC * (k + 1))
                for t in range(TB):
                    nc.vector.scalar_tensor_tensor(
                        out=yc[:, t], in0=u_row[:], scalar=nmu[:, t:t + 1], in1=yps[:, par, t],
                        op0=ALU.mult, op1=ALU.add).then_inc(yc_ok, 1)

            def residual(k, par, uses):
                dve.wait_ge(r_rstd, k + 1)
                nc.vector.tensor_scalar(gain[:], rsH[:], wstep[:, 1:2], None, ALU.mult).then_inc(r_gain, 1)
                dve.wait_ge(r_gain, k + 1)
                dve.wait_ge(yc_ok, TB * (k + 1))
                dve.wait_ge(x1c_ok, k + 1)
                if not (isinstance(uses, int) and uses == 0):
                    dve.wait_ge(o_out[par], 16 * uses)
                for t in range(TB):
                    nc.vector.scalar_tensor_tensor(
                        out=z[:, par, t], in0=yc[:, t], scalar=gain[:, t:t + 1], in1=x1c[:, par, t],
                        op0=ALU.mult, op1=ALU.add).then_inc(z_ok, 1)

            def out_stats(k, par):
                for t in range(TB):
                    dve.wait_ge(z_ok, TB * k + t + 1)
                    nc.vector.bn_stats(bnZ[:, t], z[:, par, t]).then_inc(z_stat, 1)
                dve.wait_ge(z_stat, TB * (k + 1))
                nc.vector.memset(fence[:], 0.0)
                for t in range(TB):
                    nc.vector.bn_aggr(mvZ[:, t], bnZ[:, t]).then_inc(z_var, 1)
                dve.wait_ge(z_var, TB * (k + 1))
                nc.vector.tensor_scalar(veZ[:], mvZ[:, :, 1], EPS, None, ALU.add).then_inc(z_eps, 1)

            def out_bias(k):
                dve.wait_ge(z_rstd, k + 1)
                if not (isinstance(k, int) and k == 0):
                    dve.wait_ge(o_ok, TB * k)
                nc.vector.scalar_tensor_tensor(out=nmr[:], in0=mvZ[:, :, 0], scalar=-1.0, in1=rsZ[:],
                                               op0=ALU.mult, op1=ALU.mult).then_inc(z_nmr, 1)

            norm_apply(0, 0)
            ht_low(0, 0)

            def step(k, i, par, first, last):
                for m in range(FC):
                    dve.wait_ge(hi_ok, FC * k + m + 1)
                    nc.vector.scalar_tensor_tensor(
                        out=a_lo[:, m % DEPTH], in0=gel[:, m], scalar=vec("ln2_g", m),
                        in1=a_hi[:, m % DEPTH].bitcast(F32), op0=ALU.mult, op1=ALU.subtract).then_inc(lo_ok, 1)
                    if m > POOL_SQ:
                        j = m - POOL_SQ
                        dve.wait_ge(sq_ok, FC * k + m + 1)
                        if j > 1:
                            dve.wait_ge(sum_q, Q_ADDS * k + j - 1)
                        a = sq[:, POOL_SQ] if j == 1 else acc[:, par, 1]
                        nc.vector.tensor_tensor(acc[:, par, 1], a, sq[:, m], ALU.add).then_inc(sum_q, 1)
                    if m == 0 and before2(k):
                        out_bias(k - 2)
                    if m == 0 and not last:
                        norm_apply(k + 1, 1 - par)
                    if m == 1 and not first:
                        hidden_stats(k - 1)
                    if m == 2 and not first:
                        centre_y(k - 1, 1 - par)
                    if m == 4 and not last:
                        ht_low(k + 1, 1 - par)
                    if m == 5 and not first:
                        residual(k - 1, 1 - par, i if par == 1 else i - 1)
                    if m == 6 and not first:
                        out_stats(k - 1, 1 - par)
                dve.wait_ge(sum_q, Q_ADDS * (k + 1) - 1)
                dve.wait_ge(sum_p, P_ADDS * (k + 1))
                nc.vector.tensor_tensor(acc[:, par, 1], acc[:, par, 1], accp[:], ALU.add).then_inc(sum_q, 1)
            blocks(dve, step)
            out_bias(NK - 2)
            hidden_stats(NK - 1)
            centre_y(NK - 1, 1)
            residual(NK - 1, 1, NK // 2 - 1)
            out_stats(NK - 1, 1)
            out_bias(NK - 1)

        @block.tensor
        def _(pe):
            pe.wait_ge(consts, 1)
            pe.wait_ge(w_abs, 2)
            nc.tensor.matmul(hps[:, 0, 0:2], ones[:], wabs[:], start=True, stop=True).then_inc(w_sum, 1)
            pe.wait_ge(w_tern, 2)
            pe.wait_ge(v_in, 48)
            for m in range(FC):
                for c in range(CH):
                    nc.tensor.matmul(hps[:, 1, m:m + 1], t1[:, c, m * P:(m + 1) * P].bitcast(F32), vec("ln1_b", c),
                                     start=(m == 0 and c == 0), stop=(c == CH - 1), skip_group_check=True)
            pe.wait_ge(w_sc2, 2 * FC)
            for slot, src in ((0, w2f[:]), (1, wm[:].rearrange("p (m c) -> p m c", c=C))):
                for m in range(FC):
                    last = nc.tensor.matmul(yps[:, slot, 0], ones[:], src[:, m], start=(m == 0), stop=(m == FC - 1))
            last.then_inc(fold_mm, 1)

            def transposes(k):
                pe.wait_ge(n_ok, TB * (k + 1))
                for c in range(CH):
                    for t in range(TB):
                        last = nc.tensor.transpose(tps[:, c, t * P:(t + 1) * P], xn[:, t, c * P:(c + 1) * P],
                                                   ident[:])
                    last.then_inc(ht_tr, 1)

            def sum_transposes(k, par):
                pe.wait_ge(sum_g, (FC - 1) * (k + 1))
                pe.wait_ge(sum_q, Q_ADDS * (k + 1))
                for a in range(2):
                    for t in range(TB):
                        last = nc.tensor.transpose(tps[:, a, t * P:(t + 1) * P], acc[:, par, a, t * P:(t + 1) * P],
                                                   ident[:])
                last.then_inc(r_tr, 1)

            def second(k, m, par):
                pe.wait_ge(hi_ok, FC * k + m + 1)
                pe.wait_ge(lo_ok, FC * k + m + 1)
                if m == 0 and not (isinstance(k, int) and k < 2):
                    pe.wait_ge(yc_ok, TB * (k - 1))
                for t in range(TB):
                    for n, a in enumerate((a_hi, a_lo)):
                        last = nc.tensor.matmul(yps[:, par, t], a[:, m % DEPTH, t * P:(t + 1) * P], t2[:, m],
                                                start=(m == 0 and n == 0 and t % 2 == 0),
                                                stop=(m == FC - 1 and n == 1), skip_group_check=True)
                last.then_inc(y_mm, 1)

            transposes(0)
            pe.wait_ge(fold_ok, 3)

            def step(k, i, par, first, last):
                for m in range(FC):
                    if m == 0:
                        pe.wait_ge(ht_hi_ok, CH * (k + 1))
                        pe.wait_ge(ht_lo_ok, CH * (k + 1))
                    if m >= 2 or not first:
                        pe.wait_ge(gelu_ok, FC * k + m - 1)
                    for c in range(CH):
                        for n, h in enumerate((ht_hi, ht_lo)):
                            mm = nc.tensor.matmul(hps[:, m % 2], t1[:, c, m * P:(m + 1) * P], h[:, par, c],
                                                  start=(c == 0 and n == 0), stop=(c == CH - 1 and n == 1))
                    mm.then_inc(h_mm, 1)
                    if m >= LAG:
                        second(k, m - LAG, par)
                    elif not first:
                        second(k - 1, FC + m - LAG, 1 - par)
                    if m == 2 and not first:
                        sum_transposes(k - 1, 1 - par)
                    if m == 4 and not last:
                        if not first:
                            pe.wait_ge(r_sum, k)
                        transposes(k + 1)
            blocks(pe, step)
            for m in range(FC - LAG, FC):
                second(NK - 1, m, 1)
            sum_transposes(NK - 1, 1)


_INS = ["x_tok", "x_chan", "wq", "wk", "wv", "wo", "w1", "w2", "vecs", "rows", "ident", "mask"]


def program(nc, a, out):
    NB, _, T, C = a["x_tok"].shape
    x1 = nc.dram_tensor("x1_scratch", (NB, P, T, C + 1), F32, kind="Internal").ap()
    attention_phase(nc, a["x_tok"], a["x_chan"], a["wq"], a["wk"], a["wv"], a["wo"], a["vecs"], a["rows"],
                    a["ident"], a["mask"], x1)
    feed_forward_phase(nc, x1, a["w1"], a["w2"], a["vecs"], a["rows"], a["ident"], out)


def kernel(**inputs):
    import concourse.bacc as _bacc
    from concourse.bass_utils import run_bass_kernel_spmd as _run

    g = {k: np.asarray(v) for k, v in inputs.items()}
    x = g["L0_attn_x"]
    B, N, C = x.shape
    T = N // P
    x_tok = x.reshape(B, P, T, C)

    def kxn(w):
        wt = w.T
        return np.ascontiguousarray(wt.reshape(wt.shape[0] // P, P, wt.shape[1]).transpose(1, 0, 2))

    def col(v):
        return v.reshape(-1, P).T

    vec_of = {"bk": "L0_attn_bk", "ln_g": "L0_attn_ln_g", "ln_b": "L0_attn_ln_b", "ln1_g": "L0_ffn_ln1_g",
              "ln1_b": "L0_ffn_ln1_b", "b1": "L0_ffn_b1", "ln2_g": "L0_ffn_ln2_g", "ln2_b": "L0_ffn_ln2_b"}
    row_of = {"bq": "L0_attn_bq", "bv": "L0_attn_bv", "bo": "L0_attn_bo", "b2": "L0_ffn_b2"}
    head = np.arange(P) // 16
    arrays = {
        "x_tok": x_tok,
        "x_chan": x_tok.transpose(0, 3, 2, 1).reshape(B, C // P, P, N).transpose(0, 2, 1, 3),
        "wq": kxn(g["L0_attn_Wq"]), "wk": kxn(g["L0_attn_Wk"]), "wv": kxn(g["L0_attn_Wv"]),
        "wo": kxn(g["L0_attn_Wo"]), "w1": kxn(g["L0_ffn_w1"]), "w2": kxn(g["L0_ffn_w2"]),
        "vecs": np.concatenate([col(g[vec_of[n]]) for n in VEC], axis=1),
        "rows": np.broadcast_to(np.stack([g[row_of[n]] for n in ROW])[None], (P, len(ROW), C)),
        "ident": np.eye(P, dtype=np.float32),
        "mask": (head[:, None] == head[None, :]).astype(np.float32),
    }
    arrays = {f"in_{k}_dram": np.ascontiguousarray(v) for k, v in arrays.items()}

    nc = _bacc.Bacc("TRN2", target_bir_lowering=False, num_devices=1)
    a = {n: nc.dram_tensor(f"in_{n}_dram", arrays[f"in_{n}_dram"].shape, F32, kind="ExternalInput").ap()
         for n in _INS}
    out = nc.dram_tensor("out_0_dram", (B, P, T, C), F32, kind="ExternalOutput").ap()
    program(nc, a, out)
    r = _run(nc, [arrays], core_ids=[0])
    return r.results[0]["out_0_dram"].reshape(B, N, C)
```

```python
from contextlib import ExitStack

import numpy as np

import concourse.bass as bass
from concourse import mybir

F32 = mybir.dt.float32
F32R = mybir.dt.float32r
ALU = mybir.AluOpType
ACT = mybir.ActivationFunctionType
AX_X = mybir.AxisListType.X

P = 128
EPS = 1e-5
ROUNDER = 1.5 * 2.0 ** 23

VEC = {}
_at = 0
for _name, _n in (("bk", 2), ("ln_g", 2), ("ln_b", 2), ("ln1_g", 2), ("ln1_b", 2),
                  ("b1", 8), ("ln2_g", 8), ("ln2_b", 8)):
    VEC[_name] = (_at, _n)
    _at += _n
NVEC = _at
ROW = {"bq": 0, "bv": 1, "bo": 2, "b2": 3}


def wait_for(eng, semaphore, count):
    if not isinstance(count, int) or count > 0:
        eng.wait_ge(semaphore, count)


class Kept:

    def __init__(self, nc, ctx, C, F):
        def sb(name, shape, dt=F32):
            return ctx.enter_context(nc.sbuf_tensor(name, shape, dt))

        self.vecs = sb("vecs", [P, NVEC])
        self.rows = sb("rows", [P, len(ROW), C])
        self.ident = sb("ident", [P, P])
        self.ones = sb("ones", [P, P])
        T = F * (C // P) // C
        parts = [sb(name, [P, T * C], F32R) for name in ("x_hi_then_t1", "x_lo_then_t2")]
        self.xt_hi, self.xt_lo = (v[:].rearrange("p (t c) -> p t c", c=C) for v in parts)
        self.t1 = parts[0][:].rearrange("p (a f) -> p a f", f=F)
        self.t2 = parts[1][:].rearrange("p (m c) -> p m c", c=C)
        self.wstep = sb("wstep", [P, 2])
        self.bias1 = sb("bias1", [P, F // P])
        self.ff_u = sb("ff_u_row", [P, C])
        self.ff_c = sb("ff_c_row", [P, C])


def attention_phase(nc, kept, x_tok, x_chan, wq, wk, wv, wo, w1, w2, vecs_d, rows_d, ident_d, mask_d, x1_scratch):
    NB, _, T, C = x_tok.shape
    N = T * P
    CH = C // P
    D = 16
    HEADS = C // D
    PAIRS = T // 2
    GROUP = 4
    NG = T // GROUP
    F = w1.shape[2]
    FC = F // P
    RW = C + P
    assert NB % 2 == 0 and CH == 2 and T == 8

    with ExitStack() as ctx:
        def sb(name, shape, dt=F32):
            return ctx.enter_context(nc.sbuf_tensor(name, shape, dt))

        def sem(name):
            return ctx.enter_context(nc.semaphore(name))

        ring = ctx.enter_context(nc.psum_tensor("ring", [P, 4, 512], F32))
        aps = ctx.enter_context(nc.psum_tensor("aps", [P, 2, 512], F32))
        qps = ctx.enter_context(nc.psum_tensor("qps", [P, 512], F32))
        sps = ctx.enter_context(nc.psum_tensor("sps", [P, 512], F32))

        xt = sb("xt", [P, 2, T, C])
        xc = sb("xc", [P, CH, N])
        xt_hi, xt_lo = kept.xt_hi, kept.xt_lo
        xc_hi, xc_lo = sb("xc_hi", [P, 2, CH, N], F32R), sb("xc_lo", [P, 2, CH, N], F32R)
        ek = sb("ek", [P, CH, N])
        et_hi, et_lo = sb("et_hi", [P, T, C], F32R), sb("et_lo", [P, T, C], F32R)
        qw = sb("qw", [P, 2, T, C])
        pt_hi, pt_lo = sb("pt_hi", [P, CH, N], F32R), sb("pt_lo", [P, CH, N], F32R)
        z = sb("z", [P, T, C + 1])
        zjunk = sb("zjunk", [P, GROUP, C])
        lnb_wo = zjunk[:, 0:CH]
        qtree = sb("qtree", [P, NG, GROUP * HEADS, D // 2])
        w_hi, w_lo = sb("w_hi", [P, 4, CH, C], F32R), sb("w_lo", [P, 4, CH, C], F32R)
        vecs, rows, ident, ones = kept.vecs, kept.rows, kept.ident, kept.ones
        w_raw = sb("w_raw", [P, 4, CH, C])
        vparts = sb("vparts", [P, NVEC, 2], F32R)
        wabs = sb("wabs", [P, 2])
        wmean = sb("wmean", [P, 2])
        wscale = sb("wscale", [P, 2])
        bsum = sb("bsum", [P, F // P])
        bq_hi, bq_lo = sb("bq_hi", [P, C], F32R), sb("bq_lo", [P, C], F32R)
        mask = sb("mask", [P, P])
        part = sb("part", [P, P], F32R)
        u_row = sb("u_row", [P, C])
        c_row = sb("c_row", [P, C])
        xe_hi, xe_lo = sb("xe_hi", [P, CH, C], F32R), sb("xe_lo", [P, CH, C], F32R)
        s_f = sb("s_f", [P, CH, P])
        st_hi, st_lo = sb("st_hi", [P, CH, P], F32R), sb("st_lo", [P, CH, P], F32R)
        r_f = sb("r_f", [P, CH, RW])
        r_hi, r_lo = sb("r_hi", [P, CH, RW], F32R), sb("r_lo", [P, CH, RW], F32R)
        kmx = sb("kmx", [P, CH])
        kbm = sb("kbm", [P, CH])
        kbias = sb("kbias", [P, CH])
        esum = sb("esum", [P, CH])
        einv = sb("einv", [P, CH])
        srow = sb("srow", [P, CH])
        nmean = sb("nmean", [P, CH])
        qmx = sb("qmx", [P, 2, 2 * HEADS])
        qsum = sb("qsum", [P, NG, GROUP * HEADS])
        qinv = sb("qinv", [P, NG, GROUP * HEADS])
        bnA = sb("bnA", [P, T, 6])
        mvA = sb("mvA", [P, T, 2])
        veA = sb("veA", [P, T])
        rsA = sb("rsA", [P, T])
        zsum = sb("zsum", [P, T])
        znm = sb("znm", [P, T])
        zss = sb("zss", [P, T])
        veZ = sb("veZ", [P, T])
        vaZ = sb("vaZ", [P, T])
        inv_c = sb("inv_c", [P, T])
        eps = sb("eps", [P, T])
        rsZ = sb("rsZ", [P, T])
        nmr = sb("nmr", [P, T])
        nhalf = sb("nhalf", [P, T])

        fence = sb("fence", [P, 1])

        xt_in = [sem(f"xt_in{n}") for n in range(2)]
        xc_in = sem("xc_in")
        w_in = [sem(f"w_in{n}") for n in range(4)]
        v_in, m_in = sem("v_in"), sem("m_in")
        consts, half_ok = sem("consts"), sem("half_ok")
        w_scaled = sem("w_scaled")
        w_hi_ok = sem("w_hi_ok")
        w_ready = [sem(f"w_ready{n}") for n in range(4)]
        bq_hi_ok, bq_ready = sem("bq_hi_ok"), sem("bq_ready")
        v_hi_ok, v_ready = sem("v_hi_ok"), sem("v_ready")
        f_in, f_abs, f_sum, f_mean, f_scale, f_step = (
            sem(s) for s in ("f_in", "f_abs", "f_sum", "f_mean", "f_scale", "f_step"))
        f_round, f_top, f_tern, f_bias, f_rows, f_bsum, f_out = (
            sem(s) for s in ("f_round", "f_top", "f_tern", "f_bias", "f_rows", "f_bsum", "f_out"))
        rows_mm = sem("rows_mm")
        rows_ok = sem("rows_ok")
        xc_hi_ok, xc_lo_ok = sem("xc_hi_ok"), sem("xc_lo_ok")
        xt_hi_ok, xt_lo_ok, xt_c_ok = sem("xt_hi_ok"), sem("xt_lo_ok"), sem("xt_c_ok")
        k_mm, k_max, k_maxb, k_bias, k_exp = (sem(s) for s in ("k_mm", "k_max", "k_maxb", "k_bias", "k_exp"))
        q_mm, q_max, q_sub, q_exp = (sem(s) for s in ("q_mm", "q_max", "q_sub", "q_exp"))
        q_sum, q_inv, q_norm = (sem(s) for s in ("q_sum", "q_inv", "q_norm"))
        pt_tr, pt_hi_ok, pt_lo_ok = (sem(s) for s in ("pt_tr", "pt_hi_ok", "pt_lo_ok"))
        et_tr, et_hi_ok, et_lo_ok = (sem(s) for s in ("et_tr", "et_hi_ok", "et_lo_ok"))
        xe_mm, xe_hi_ok, xe_lo_ok = (sem(s) for s in ("xe_mm", "xe_hi_ok", "xe_lo_ok"))
        e_inv, s_mm, s_norm, s_mask, s_sum, s_mean = (
            sem(s) for s in ("e_inv", "s_mm", "s_norm", "s_mask", "s_sum", "s_mean"))
        st_tr, st_hi_ok, st_lo_ok = (sem(s) for s in ("st_tr", "st_hi_ok", "st_lo_ok"))
        m_mm, m_cent, r_hi_ok, r_lo_ok = (sem(s) for s in ("m_mm", "m_cent", "r_hi_ok", "r_lo_ok"))
        ap_mm, a_stat, a_var, a_eps, a_rstd = (sem(s) for s in ("ap_mm", "a_stat", "a_var", "a_eps", "a_rstd"))
        y_out = sem("y_out")
        z_ok, z_mean, z_sq, z_var, z_eps, z_rstd, z_fin, x1_ok = (
            sem(s) for s in ("z_ok", "z_mean", "z_sq", "z_var", "z_eps", "z_rstd", "z_fin", "x1_ok"))
        q_tree = sem("q_tree")
        x1_out = sem("x1_out")

        def vec(name, c):
            return vecs[:, VEC[name][0] + c:VEC[name][0] + c + 1]

        def s_cols(c):
            return (0, P) if c == 0 else (C, RW)

        def q_bank(v):
            return aps[:, 1] if v % 2 == 0 else qps[:]

        def m_cols(c):
            return (P, RW) if c == 0 else (0, C)

        f_raw = [xc[:].rearrange("p a n -> p (a n)"), qw[:, 0].rearrange("p t c -> p (t c)")]
        f_junk = qw[:, 1].rearrange("p t c -> p (t c)")
        f_tern_out = [kept.t1.rearrange("p a f -> p (a f)"), kept.t2.rearrange("p a f -> p (a f)")]

        def split3(a_hi, a_lo, b_hi, b_lo):
            return ((a_hi, b_hi), (a_lo, b_hi), (a_hi, b_lo))

        def batches(eng, body):
            for par in range(2):
                body(par, 0, par, False, par == 1, True, True, True)
            with eng.Fori(1, NB // 2 - 1) as i:
                for par in range(2):
                    body(2 * i + par, i, par, True, True, True, True, True)
            for par in range(2):
                body(NB - 2 + par, NB // 2 - 1, par, True, True, True, par == 0, False)
            body(NB, NB // 2, 0, True, True, False, False, False)

        block = ctx.enter_context(nc.Block())

        @block.sync
        def _(sp):
            sp.dma_start(w_raw[:, 0], wq).then_inc(w_in[0], 16)
            sp.dma_start(vecs[:], vecs_d).then_inc(v_in, 16)
            sp.dma_start(rows[:], rows_d).then_inc(v_in, 16)
            sp.dma_start(xc[:], x_chan[0]).then_inc(xc_in, 16)
            for n, w in ((1, wk), (2, wv), (3, wo)):
                sp.dma_start(w_raw[:, n], w).then_inc(w_in[n], 16)
            sp.dma_start(ident[:], ident_d).then_inc(m_in, 16)
            sp.dma_start(mask[:], mask_d).then_inc(m_in, 16)
            sp.dma_start(xt[:, 0], x_tok[0]).then_inc(xt_in[0], 16)
            sp.wait_ge(xc_lo_ok, 1)
            sp.dma_start(xc[:], x_chan[1]).then_inc(xc_in, 16)

            def step(b, i, par, has_prev2, has_prev, has_k, has_next, has_next2):
                fixed = isinstance(b, int)
                pb2, nb, nb2 = (b + d if fixed else sp.snap(b + d) for d in (-2, 1, 2))
                if has_next2:
                    sp.wait_ge(xc_lo_ok, b + 2)
                    sp.dma_start(xc[:], x_chan[bass.ds(nb2, 1)].rearrange("o p c n -> (o p) c n")
                                 ).then_inc(xc_in, 16)
                if has_prev2:
                    store(pb2, b - 2)
                if not has_next2 and has_next:
                    sp.wait_ge(pt_tr, PAIRS * (NB - 1))
                    for n, w in enumerate((w1, w2)):
                        sp.dma_start(f_raw[n], w.rearrange("p a f -> p (a f)")).then_inc(f_in, 16)
                if has_next:
                    if has_prev:
                        sp.wait_ge(z_ok, T * b)
                    sp.dma_start(xt[:, 1 - par], x_tok[bass.ds(nb, 1)].rearrange("o p t c -> (o p) t c")
                                 ).then_inc(xt_in[1 - par], 16)

            def store(row, b):
                for g in range(NG):
                    sp.wait_ge(x1_ok, T * b + GROUP * (g + 1))
                    sp.dma_start(x1_scratch[bass.ds(row, 1), :, g * GROUP:(g + 1) * GROUP].rearrange(
                        "o p t c -> (o p) t c"), z[:, g * GROUP:(g + 1) * GROUP]).then_inc(x1_out, 16)
            batches(sp, step)
            store(NB - 1, NB - 1)
            sp.wait_ge(x1_out, 16 * NG * NB)

        @block.gpsimd
        def _(pool):
            nc.gpsimd.memset(nhalf[:], -0.5).then_inc(half_ok, 1)

            def chan_lo(b, par):
                pool.wait_ge(xc_hi_ok, b + 1)
                wait_for(pool, k_mm, CH * (b - 1))
                nc.gpsimd.tensor_tensor(xc_lo[:, par], xc[:], xc_hi[:, par].bitcast(F32), ALU.subtract
                                        ).then_inc(xc_lo_ok, 1)

            def tok_lo(b, par):
                pool.wait_ge(xt_hi_ok, b + 1)
                wait_for(pool, xe_mm, b)
                nc.gpsimd.tensor_tensor(xt_lo[:], xt[:, par], xt_hi[:].bitcast(F32), ALU.subtract
                                        ).then_inc(xt_lo_ok, 1)

            def tok_c(b, par):
                pool.wait_ge(xt_lo_ok, b + 1)
                if isinstance(b, int) and b == 0:
                    pool.wait_ge(rows_ok, 2)
                nc.gpsimd.tensor_tensor(xt[:, par], xt[:, par],
                                        c_row[:].rearrange("p (o c) -> p o c", o=1).to_broadcast([P, T, C]),
                                        ALU.add).then_inc(xt_c_ok, 1)

            def q_normalise(b, par, g):
                pool.wait_ge(q_inv, NG * b + g + 1)
                v = qw[:, par, g * GROUP:(g + 1) * GROUP].rearrange("p t (h d) -> p (t h) d", d=D)
                nc.gpsimd.tensor_tensor(
                    v, v, qinv[:, g].rearrange("p (h o) -> p h o", o=1).to_broadcast([P, GROUP * HEADS, D]),
                    ALU.mult).then_inc(q_norm, 1)

            def attention_rstd(b, g):
                gs = slice(g * GROUP, (g + 1) * GROUP)
                pool.wait_ge(a_eps, NG * b + g + 1)
                nc.gpsimd.tensor_tensor(rsA[:, gs], veA[:, gs], nhalf[:, gs], ALU.pow).then_inc(a_rstd, 1)

            def norm_rstd(b, g):
                gs = slice(g * GROUP, (g + 1) * GROUP)
                n = NG * b + g + 1
                pool.wait_ge(z_sq, T * b + GROUP * (g + 1))
                nc.gpsimd.tensor_tensor(vaZ[:, gs], zss[:, gs], inv_c[:, gs], ALU.mult).then_inc(z_var, 1)
                pool.wait_ge(z_var, n)
                nc.gpsimd.tensor_tensor(veZ[:, gs], vaZ[:, gs], eps[:, gs], ALU.add).then_inc(z_eps, 1)
                pool.wait_ge(z_eps, n)
                nc.gpsimd.tensor_tensor(rsZ[:, gs], veZ[:, gs], nhalf[:, gs], ALU.pow).then_inc(z_rstd, 1)
                pool.wait_ge(z_rstd, n)
                nc.gpsimd.tensor_tensor(nmr[:, gs], znm[:, gs], rsZ[:, gs], ALU.mult).then_inc(z_fin, 1)
                nc.gpsimd.tensor_tensor(vaZ[:, gs], vaZ[:, gs], rsZ[:, gs], ALU.mult).then_inc(z_fin, 1)
                pool.wait_ge(z_fin, 4 * n - 2)
                nc.gpsimd.tensor_tensor(vaZ[:, gs], vaZ[:, gs], rsZ[:, gs], ALU.mult).then_inc(z_fin, 1)
                pool.wait_ge(z_fin, 4 * n - 1)
                nc.gpsimd.tensor_tensor(z[:, gs, C], vaZ[:, gs], eps[:, gs], ALU.add).then_inc(z_fin, 1)

            def q_denominator(b, par, g):
                n = NG * (b - 1) + g
                pool.wait_ge(q_exp, NG * b + g + 1)
                v = qw[:, par, g * GROUP:(g + 1) * GROUP].rearrange("p t (h d) -> p (t h) d", d=D)
                nc.gpsimd.tensor_tensor(qtree[:, g], v[:, :, 0:8], v[:, :, 8:16], ALU.add).then_inc(q_tree, 1)
                pool.wait_ge(q_tree, 3 * n + 1)
                nc.gpsimd.tensor_tensor(qtree[:, g, :, 0:4], qtree[:, g, :, 0:4], qtree[:, g, :, 4:8], ALU.add
                                        ).then_inc(q_tree, 1)
                pool.wait_ge(q_tree, 3 * n + 2)
                nc.gpsimd.tensor_tensor(qtree[:, g, :, 0:2], qtree[:, g, :, 0:2], qtree[:, g, :, 2:4], ALU.add
                                        ).then_inc(q_tree, 1)
                pool.wait_ge(q_tree, 3 * n + 3)
                nc.gpsimd.tensor_tensor(qsum[:, g], qtree[:, g, :, 0], qtree[:, g, :, 1], ALU.add).then_inc(q_sum, 1)

            nc.gpsimd.memset(inv_c[:], 1.0 / C).then_inc(half_ok, 1)
            nc.gpsimd.memset(eps[:], EPS).then_inc(half_ok, 1)
            pool.wait_ge(half_ok, 3)
            chan_lo(1, 1)
            for g in range(NG):
                q_normalise(0, 0, g)

            def step(b, i, par, has_prev2, has_prev, has_k, has_next, has_next2):
                if has_k:
                    tok_lo(b, par)
                    tok_c(b, par)
                if has_next:
                    q_denominator(b + 1, 1 - par, 0)
                if has_next2:
                    chan_lo(b + 2, par)
                if has_prev:
                    attention_rstd(b - 1, 0)
                if has_next:
                    q_denominator(b + 1, 1 - par, 1)
                if has_prev:
                    attention_rstd(b - 1, 1)
                if has_next:
                    q_normalise(b + 1, 1 - par, 0)
                    q_normalise(b + 1, 1 - par, 1)
                if has_prev:
                    norm_rstd(b - 1, 0)
                    norm_rstd(b - 1, 1)
            batches(pool, step)

        @block.scalar
        def _(act):
            def chan_hi(b, par):
                act.wait_ge(xc_in, 16 * (b + 1))
                wait_for(act, k_mm, CH * (b - 1))
                nc.scalar.copy(xc_hi[:, par], xc[:]).then_inc(xc_hi_ok, 1)

            def tok_hi(b, par, n):
                act.wait_ge(xt_in[par], 16 * n)
                wait_for(act, xe_mm, b)
                nc.scalar.copy(xt_hi[:], xt[:, par]).then_inc(xt_hi_ok, 1)

            def q_exponent(b, par, g):
                act.wait_ge(q_sub, PAIRS * b + 2 * (g + 1))
                v = qw[:, par, g * GROUP:(g + 1) * GROUP]
                nc.scalar.activation(v, v, ACT.Exp).then_inc(q_exp, 1)

            def k_exponent(b, c):
                act.wait_ge(k_bias, CH * b + c + 1)
                wait_for(act, et_tr, PAIRS * b)
                wait_for(act, e_inv, CH * b)
                nc.scalar.activation(ek[:, c], ring[:, 2 * c:2 * c + 2].rearrange("p a n -> p (a n)"),
                                     ACT.Exp, bias=kbias[:, c:c + 1], accum_out=esum[:, c:c + 1]
                                     ).then_inc(k_exp, 1)

            def state_high(b):
                act.wait_ge(xe_mm, b + 1)
                nc.scalar.copy(xe_hi[:].rearrange("p a c -> p (a c)"), sps[:]).then_inc(xe_hi_ok, 1)

            def products_out(b, ts):
                for t in ts:
                    act.wait_ge(a_stat, T * b + t + 1)
                    nc.scalar.copy(z[:, t, 0:C], aps[:, t % 2, P:P + C]).then_inc(y_out, 1)

            def pt_high(b, n):
                act.wait_ge(pt_tr, PAIRS * b + n + 1)
                g, c = n // CH, n % CH
                nc.scalar.copy(pt_hi[:, c, g * 512:(g + 1) * 512], ring[:, n]).then_inc(pt_hi_ok, 1)

            def et_high(b, n):
                act.wait_ge(et_tr, PAIRS * b + n + 1)
                nc.scalar.copy(et_hi[:, 2 * n:2 * n + 2].rearrange("p t c -> p (t c)"), ring[:, n]
                               ).then_inc(et_hi_ok, 1)

            def squares(b, g):
                act.wait_ge(z_mean, NG * b + g + 1)
                for t in range(g * GROUP, (g + 1) * GROUP):
                    wait_for(act, z_sq, T * b + t - GROUP + 1)
                    nc.scalar.activation(zjunk[:, t % GROUP], z[:, t, 0:C], ACT.Square, bias=znm[:, t:t + 1],
                                         accum_out=zss[:, t:t + 1]).then_inc(z_sq, 1)

            def normalise(b, g):
                act.wait_ge(z_fin, 4 * (NG * b + g + 1))
                for t in range(g * GROUP, (g + 1) * GROUP):
                    nc.scalar.activation(z[:, t, 0:C], z[:, t, 0:C], ACT.Identity, bias=nmr[:, t:t + 1],
                                         scale=rsZ[:, t:t + 1]).then_inc(x1_ok, 1)

            def absolute_sums():
                act.wait_ge(f_in, 32)
                for n in range(2):
                    wait_for(act, f_abs, n)
                    nc.scalar.activation(f_junk, f_raw[n], ACT.Abs, accum_out=wabs[:, n:n + 1]
                                         ).then_inc(f_abs, 1)

            chan_hi(0, 0)
            chan_hi(1, 1)
            q_exponent(0, 0, 0)
            q_exponent(0, 0, 1)

            def step(b, i, par, has_prev2, has_prev, has_k, has_next, has_next2):
                if has_k:
                    k_exponent(b, 0)
                if has_prev2:
                    normalise(b - 2, 0)
                if has_prev:
                    act.wait_ge(st_tr, b)
                    nc.scalar.copy(st_hi[:].rearrange("p a c -> p (a c)"), sps[:, 0:C]).then_inc(st_hi_ok, 1)
                if has_prev2:
                    normalise(b - 2, 1)
                if has_k:
                    k_exponent(b, 1)
                if has_prev:
                    act.wait_ge(m_cent, CH * b)
                    nc.scalar.copy(r_hi[:], r_f[:]).then_inc(r_hi_ok, 1)
                if has_k:
                    tok_hi(b, par, i + 1)
                if has_next:
                    q_exponent(b + 1, 1 - par, 0)
                if has_next2:
                    chan_hi(b + 2, par)
                if has_prev:
                    wait_for(act, x1_out, 16 * NG * (b - 1))
                    products_out(b - 1, range(0, 4))
                if has_k:
                    pt_high(b, 0)
                    pt_high(b, 1)
                if has_prev:
                    products_out(b - 1, range(4, 6))
                if has_k:
                    et_high(b, 0)
                if has_prev:
                    products_out(b - 1, range(6, 8))
                if has_k:
                    et_high(b, 1)
                    pt_high(b, 2)
                    pt_high(b, 3)
                if has_next:
                    q_exponent(b + 1, 1 - par, 1)
                if has_k:
                    et_high(b, 2)
                    et_high(b, 3)
                if has_k:
                    state_high(b)
                if has_prev:
                    squares(b - 1, 0)
                    squares(b - 1, 1)
                if has_k and not has_next:
                    absolute_sums()
            batches(act, step)
            normalise(NB - 1, 0)
            normalise(NB - 1, 1)

        @block.vector
        def _(dve):
            nc.vector.memset(ones[:], 1.0).then_inc(consts, 1)
            nc.vector.memset(part[:].bitcast(F32), 1.0 / P).then_inc(consts, 1)

            def split_lo(out, full, hi):
                return nc.vector.tensor_tensor(out, full, hi.bitcast(F32), ALU.subtract)

            def split_weight(n):
                if n != 3:
                    dve.wait_ge(w_in[n], 16)
                w = w_raw[:, n].rearrange("p a c -> p (a c)")
                hi, lo = (v[:, n].rearrange("p a c -> p (a c)") for v in (w_hi, w_lo))
                nc.vector.tensor_copy(hi, w).then_inc(w_hi_ok, 1)
                dve.wait_ge(w_hi_ok, n + 1)
                split_lo(lo, w, hi).then_inc(w_ready[n], 1)

            def fold_wo():
                dve.wait_ge(w_in[3], 16)
                for c in range(CH):
                    nc.vector.tensor_scalar(lnb_wo[:, c], w_raw[:, 3, c], vec("ln_b", c), None, ALU.mult
                                            ).then_inc(w_scaled, 1)
                dve.wait_ge(w_scaled, CH)
                for c in range(CH):
                    nc.vector.tensor_scalar(w_raw[:, 3, c], w_raw[:, 3, c], vec("ln_g", c), None, ALU.mult
                                            ).then_inc(w_scaled, 1)
                dve.wait_ge(w_scaled, 2 * CH)

            def split_vectors():
                nc.vector.tensor_copy(vparts[:, :, 0], vecs[:]).then_inc(v_hi_ok, 1)
                dve.wait_ge(v_hi_ok, 1)
                split_lo(vparts[:, :, 1], vecs[:], vparts[:, :, 0]).then_inc(v_ready, 1)

            def q_centre(b, par, v):
                dve.wait_ge(q_mm, PAIRS * b + v + 1)
                src = q_bank(v).rearrange("p (h d) -> p h d", d=D)
                nc.vector.tensor_reduce(qmx[:, v % 2], src, AX_X, ALU.max).then_inc(q_max, 1)
                dve.wait_ge(q_max, PAIRS * b + v + 1)
                nc.vector.tensor_tensor(
                    qw[:, par, 2 * v:2 * v + 2].rearrange("p t (h d) -> p (t h) d", d=D), src,
                    qmx[:, v % 2].rearrange("p (h o) -> p h o", o=1).to_broadcast([P, 2 * HEADS, D]),
                    ALU.subtract).then_inc(q_sub, 1)

            def q_inverse(b, g):
                dve.wait_ge(q_sum, NG * b + g + 1)
                nc.vector.reciprocal(qinv[:, g], qsum[:, g]).then_inc(q_inv, 1)

            def ternary_scales():
                dve.wait_ge(f_sum, 1)
                nc.vector.tensor_scalar(wmean[:], qps[:, 0:2], 1.0 / (C * F), 1e-5, ALU.mult, ALU.max
                                        ).then_inc(f_mean, 1)
                dve.wait_ge(f_mean, 1)
                nc.vector.reciprocal(wscale[:], wmean[:]).then_inc(f_scale, 1)
                dve.wait_ge(f_scale, 1)
                nc.vector.reciprocal(kept.wstep[:], wscale[:]).then_inc(f_step, 1)

            def ternary_round(n):
                nc.vector.tensor_scalar(f_raw[n], f_raw[n], wscale[:, n:n + 1], ROUNDER, ALU.mult, ALU.add
                                        ).then_inc(f_round, 1)

            def ternary_top(n):
                dve.wait_ge(f_round, n + 1)
                nc.vector.tensor_scalar(f_raw[n], f_raw[n], ROUNDER, 1.0, ALU.subtract, ALU.min).then_inc(f_top, 1)

            def ternary_bottom(n):
                dve.wait_ge(f_top, n + 1)
                dve.wait_ge(xe_mm, NB)
                nc.vector.tensor_scalar(f_tern_out[n], f_raw[n], -1.0, None, ALU.max).then_inc(f_tern, 1)

            def folded_rows():
                dve.wait_ge(f_bias, 1)
                nc.vector.tensor_reduce(bsum[:], sps[:, 0:2 * FC].rearrange("p (m o) -> p m o", o=2), AX_X, ALU.add
                                        ).then_inc(f_bsum, 1)
                dve.wait_ge(f_bsum, 1)
                nc.vector.scalar_tensor_tensor(
                    out=kept.bias1[:], in0=bsum[:], scalar=kept.wstep[:, 0:1],
                    in1=vecs[:, VEC["b1"][0]:VEC["b1"][0] + FC], op0=ALU.mult, op1=ALU.add).then_inc(f_out, 1)
                dve.wait_ge(f_rows, 1)
                nc.vector.tensor_copy(kept.ff_u[:], qps[:, 0:C]).then_inc(f_out, 1)
                nc.vector.scalar_tensor_tensor(
                    out=kept.ff_c[:], in0=qps[:, C:2 * C], scalar=kept.wstep[:, 1:2], in1=rows[:, ROW["b2"]],
                    op0=ALU.mult, op1=ALU.add).then_inc(f_out, 1)

            def k_maximum(b, c):
                dve.wait_ge(k_mm, CH * b + c + 1)
                nc.vector.tensor_reduce(kmx[:, c:c + 1], ring[:, 2 * c:2 * c + 2].rearrange(
                    "p a n -> p (a n)"), AX_X, ALU.max).then_inc(k_max, 1)
                dve.wait_ge(k_max, CH * b + c + 1)
                nc.vector.tensor_tensor(kbm[:, c:c + 1], kmx[:, c:c + 1], vec("bk", c), ALU.add
                                        ).then_inc(k_maxb, 1)
                dve.wait_ge(k_maxb, CH * b + c + 1)
                nc.vector.tensor_tensor(kbias[:, c:c + 1], vec("bk", c), kbm[:, c:c + 1], ALU.subtract
                                        ).then_inc(k_bias, 1)

            def state(b):
                dve.wait_ge(s_mm, b + 1)
                for c in range(CH):
                    nc.vector.scalar_tensor_tensor(
                        out=s_f[:, c], in0=sps[:, c * C + c * P:c * C + (c + 1) * P], scalar=einv[:, c:c + 1],
                        in1=rows[:, ROW["bv"], c * P:(c + 1) * P], op0=ALU.mult, op1=ALU.add).then_inc(s_norm, 1)
                dve.wait_ge(s_norm, CH * (b + 1))
                for c in range(CH):
                    s0, s1 = s_cols(c)
                    nc.vector.tensor_tensor(r_f[:, c, s0:s1], s_f[:, c], mask[:], ALU.mult).then_inc(s_mask, 1)
                dve.wait_ge(s_mask, CH * (b + 1))
                for c in range(CH):
                    s0, s1 = s_cols(c)
                    nc.vector.tensor_reduce(srow[:, c:c + 1], r_f[:, c, s0:s1], AX_X, ALU.add).then_inc(s_sum, 1)
                dve.wait_ge(s_sum, CH * (b + 1))
                nc.vector.tensor_scalar(nmean[:], srow[:], -1.0 / C, None, ALU.mult).then_inc(s_mean, 1)

            def state_low(b):
                dve.wait_ge(st_hi_ok, b + 1)
                split_lo(st_lo[:].rearrange("p a c -> p (a c)"), sps[:, 0:C],
                         st_hi[:].rearrange("p a c -> p (a c)")).then_inc(st_lo_ok, 1)

            def projected(b):
                dve.wait_ge(m_mm, b + 1)
                dve.wait_ge(s_mean, b + 1)
                for c in range(CH):
                    m0, m1 = m_cols(c)
                    nc.vector.scalar_tensor_tensor(
                        out=r_f[:, c, m0:m1], in0=u_row[:], scalar=nmean[:, c:c + 1],
                        in1=sps[:, c * C:(c + 1) * C], op0=ALU.mult, op1=ALU.add).then_inc(m_cent, 1)
                dve.wait_ge(r_hi_ok, b + 1)
                split_lo(r_lo[:], r_f[:], r_hi[:]).then_inc(r_lo_ok, 1)

            def out_variance(b, g):
                ts = range(g * GROUP, (g + 1) * GROUP)
                gs = slice(g * GROUP, (g + 1) * GROUP)
                dve.wait_ge(a_stat, T * b + GROUP * (g + 1))
                nc.vector.memset(fence[:], 0.0)
                for t in ts:
                    nc.vector.bn_aggr(mvA[:, t], bnA[:, t]).then_inc(a_var, 1)
                dve.wait_ge(a_var, T * b + GROUP * (g + 1))
                nc.vector.tensor_scalar(veA[:, gs], mvA[:, gs, 1], EPS, None, ALU.add).then_inc(a_eps, 1)

            def residual(b, par, g):
                dve.wait_ge(a_rstd, NG * b + g + 1)
                dve.wait_ge(xt_c_ok, b + 1)
                dve.wait_ge(y_out, T * b + GROUP * (g + 1))
                for t in range(g * GROUP, (g + 1) * GROUP):
                    nc.vector.scalar_tensor_tensor(
                        out=z[:, t, 0:C], in0=z[:, t, 0:C], scalar=rsA[:, t:t + 1],
                        in1=xt[:, par, t], op0=ALU.mult, op1=ALU.add, accum_out=zsum[:, t:t + 1]).then_inc(z_ok, 1)
                gs = slice(g * GROUP, (g + 1) * GROUP)
                dve.wait_ge(z_ok, T * b + GROUP * (g + 1))
                nc.vector.tensor_scalar(znm[:, gs], zsum[:, gs], -1.0 / C, None, ALU.mult).then_inc(z_mean, 1)

            def products_stats(b, ts):
                for t in ts:
                    dve.wait_ge(ap_mm, T * b + t + 1)
                    nc.vector.bn_stats(bnA[:, t], aps[:, t % 2].rearrange("p (a c) -> p a c", c=P)[:, 0:4:3]
                                       ).then_inc(a_stat, 1)

            def pt_low(b, n):
                dve.wait_ge(pt_hi_ok, PAIRS * b + n + 1)
                g, c = n // CH, n % CH
                seg = slice(g * 512, (g + 1) * 512)
                split_lo(pt_lo[:, c, seg], ring[:, n], pt_hi[:, c, seg]).then_inc(pt_lo_ok, 1)

            def et_low(b, n):
                dve.wait_ge(et_hi_ok, PAIRS * b + n + 1)
                split_lo(et_lo[:, 2 * n:2 * n + 2].rearrange("p t c -> p (t c)"), ring[:, n],
                         et_hi[:, 2 * n:2 * n + 2].rearrange("p t c -> p (t c)")).then_inc(et_lo_ok, 1)

            dve.wait_ge(v_in, 32)
            nc.vector.tensor_copy(bq_hi[:], rows[:, ROW["bq"]]).then_inc(bq_hi_ok, 1)
            dve.wait_ge(bq_hi_ok, 1)
            split_lo(bq_lo[:], rows[:, ROW["bq"]], bq_hi[:]).then_inc(bq_ready, 1)
            split_weight(0)
            dve.wait_ge(xc_hi_ok, 1)
            split_lo(xc_lo[:, 0], xc[:], xc_hi[:, 0]).then_inc(xc_lo_ok, 1)
            split_weight(1)
            q_centre(0, 0, 0)
            q_centre(0, 0, 1)
            split_vectors()
            split_weight(2)
            q_centre(0, 0, 2)
            q_centre(0, 0, 3)
            fold_wo()
            split_weight(3)
            for g in range(NG):
                dve.wait_ge(q_exp, g + 1)
                nc.vector.tensor_reduce(qsum[:, g], qw[:, 0, g * GROUP:(g + 1) * GROUP].rearrange(
                    "p t (h d) -> p (t h) d", d=D), AX_X, ALU.add).then_inc(q_sum, 1)
                q_inverse(0, g)

            def folded_rows_out():
                dve.wait_ge(rows_mm, 1)
                nc.vector.tensor_copy(u_row[:], sps[:, 0:C]).then_inc(rows_ok, 1)
                nc.vector.tensor_tensor(c_row[:], aps[:, 0, 0:C], rows[:, ROW["bo"]], ALU.add).then_inc(rows_ok, 1)

            def step(b, i, par, has_prev2, has_prev, has_k, has_next, has_next2):
                if has_k:
                    k_maximum(b, 0)
                else:
                    ternary_scales()
                    ternary_round(0)
                if has_prev:
                    state(b - 1)
                if not has_k:
                    ternary_top(0)
                if has_k:
                    k_maximum(b, 1)
                if isinstance(b, int) and b == 0:
                    folded_rows_out()
                if has_next:
                    q_centre(b + 1, 1 - par, 0)
                if has_prev:
                    state_low(b - 1)
                if not has_k:
                    ternary_bottom(0)
                if has_next:
                    q_centre(b + 1, 1 - par, 1)
                if has_prev:
                    projected(b - 1)
                if not has_k:
                    ternary_round(1)
                    ternary_top(1)
                if has_next:
                    q_centre(b + 1, 1 - par, 2)
                if has_prev:
                    products_stats(b - 1, range(0, 1))
                if has_next:
                    q_centre(b + 1, 1 - par, 3)
                if has_prev:
                    products_stats(b - 1, range(1, 4))
                if not has_k:
                    ternary_bottom(1)
                if has_k:
                    pt_low(b, 0)
                    pt_low(b, 1)
                if has_prev:
                    products_stats(b - 1, range(4, 6))
                    out_variance(b - 1, 0)
                if has_k:
                    et_low(b, 0)
                    dve.wait_ge(k_exp, CH * (b + 1))
                    nc.vector.reciprocal(einv[:], esum[:]).then_inc(e_inv, CH)
                if has_prev:
                    products_stats(b - 1, range(6, 8))
                if has_k:
                    et_low(b, 1)
                    pt_low(b, 2)
                    pt_low(b, 3)
                if has_prev:
                    out_variance(b - 1, 1)
                if has_k:
                    et_low(b, 2)
                if has_next:
                    q_inverse(b + 1, 0)
                if has_k:
                    et_low(b, 3)
                if has_prev:
                    residual(b - 1, 1 - par, 0)
                if has_k:
                    dve.wait_ge(xe_hi_ok, b + 1)
                    split_lo(xe_lo[:].rearrange("p a c -> p (a c)"), sps[:],
                             xe_hi[:].rearrange("p a c -> p (a c)")).then_inc(xe_lo_ok, 1)
                if has_prev:
                    residual(b - 1, 1 - par, 1)
                if has_next:
                    q_inverse(b + 1, 1)
            batches(dve, step)
            folded_rows()

        @block.tensor
        def _(pe):
            pe.wait_ge(consts, 2)
            pe.wait_ge(bq_ready, 1)
            pe.wait_ge(w_ready[0], 1)

            def folded_wo_rows():
                pe.wait_ge(w_ready[3], 1)
                for dst, src in ((sps[:, 0:C], w_raw[:, 3]), (aps[:, 0, 0:C], lnb_wo[:])):
                    for c in range(CH):
                        last = nc.tensor.matmul(dst, ones[:], src[:, c], start=(c == 0), stop=(c == CH - 1))
                last.then_inc(rows_mm, 1)

            def weight_sums():
                pe.wait_ge(f_abs, 2)
                nc.tensor.matmul(qps[:, 0:2], ones[:], wabs[:], start=True, stop=True).then_inc(f_sum, 1)

            def ternary_folds():
                pe.wait_ge(f_tern, 2)
                j = VEC["ln1_b"][0]
                for m in range(FC):
                    for c in range(CH):
                        last = nc.tensor.matmul(sps[:, 2 * m:2 * m + 2], kept.t1[:, c, m * P:(m + 1) * P],
                                                vparts[:, j + c], start=(m == 0 and c == 0), stop=(c == CH - 1),
                                                skip_group_check=True)
                last.then_inc(f_bias, 1)
                for h, name in enumerate(("ln2_g", "ln2_b")):
                    for m in range(FC):
                        for piece in range(2):
                            j = VEC[name][0] + m
                            last = nc.tensor.matmul(
                                qps[:, h * C:(h + 1) * C], vparts[:, j, piece:piece + 1].to_broadcast([P, P]),
                                kept.t2[:, m], start=(h == 0 and m == 0 and piece == 0),
                                stop=(m == FC - 1 and piece == 1), skip_group_check=True)
                last.then_inc(f_rows, 1)

            def q_product(b, par, v):
                if v == 0:
                    pe.wait_ge(xc_lo_ok, b + 1)
                wait_for(pe, q_sub, PAIRS * b + v - 1)
                if v == 0:
                    wait_for(pe, y_out, T * (b - 2))
                for h in range(2):
                    t = 2 * v + h
                    out = q_bank(v)[:, h * C:(h + 1) * C]
                    nc.tensor.matmul(out, part[:], bq_hi[:], start=(h == 0), stop=False, skip_group_check=True)
                    nc.tensor.matmul(out, part[:], bq_lo[:], start=False, stop=False, skip_group_check=True)
                    for c in range(CH):
                        ts = slice(t * P, (t + 1) * P)
                        for k, (a, w) in enumerate(split3(xc_hi[:, par, c, ts], xc_lo[:, par, c, ts],
                                                          w_hi[:, 0, c], w_lo[:, 0, c])):
                            last = nc.tensor.matmul(out, a, w, start=False, stop=(c == CH - 1 and k == 2),
                                                    skip_group_check=True)
                last.then_inc(q_mm, 1)

            for v in range(PAIRS):
                q_product(0, 0, v)
            pe.wait_ge(w_ready[1], 1)
            pe.wait_ge(w_ready[2], 1)
            pe.wait_ge(v_ready, 1)
            pe.wait_ge(m_in, 32)

            def k_product(b, par, m, h):
                n = 0
                for c in range(CH):
                    ms, ns = slice(m * P, (m + 1) * P), slice(h * 512, (h + 1) * 512)
                    for w, a in split3(w_hi[:, 1, c, ms], w_lo[:, 1, c, ms],
                                       xc_hi[:, par, c, ns], xc_lo[:, par, c, ns]):
                        last = nc.tensor.matmul(ring[:, 2 * m + h], w, a, start=(n == 0), stop=(n == 5))
                        n += 1
                if h == 1:
                    last.then_inc(k_mm, 1)

            def state_product(b):
                pe.wait_ge(xe_lo_ok, b + 1)
                for d in range(CH):
                    for a in range(CH):
                        ds = slice(d * P, (d + 1) * P)
                        for k, (l, r) in enumerate(split3(xe_hi[:, a, ds], xe_lo[:, a, ds],
                                                          w_hi[:, 2, a], w_lo[:, 2, a])):
                            last = nc.tensor.matmul(sps[:, d * C:(d + 1) * C], l, r,
                                                    start=(d == 0 and a == 0 and k == 0),
                                                    stop=(a == CH - 1 and k == 2), skip_group_check=True)
                last.then_inc(s_mm, 1)

            def state_transpose(b):
                pe.wait_ge(s_mask, CH * (b + 1))
                for c in range(CH):
                    s0, s1 = s_cols(c)
                    last = nc.tensor.transpose(sps[:, c * P:(c + 1) * P], r_f[:, c, s0:s1], ident[:])
                last.then_inc(st_tr, 1)

            def state_project(b):
                pe.wait_ge(st_lo_ok, b + 1)
                for c in range(CH):
                    for k, (l, r) in enumerate(split3(st_hi[:, c], st_lo[:, c], w_hi[:, 3, c], w_lo[:, 3, c])):
                        last = nc.tensor.matmul(sps[:, c * C:(c + 1) * C], l, r, start=(c == 0 and k == 0),
                                                stop=(k == 2), skip_group_check=True)
                last.then_inc(m_mm, 1)

            def attend(b, t, after_q):
                if t == 0:
                    pe.wait_ge(r_lo_ok, b + 1)
                if t == 1 and after_q:
                    pe.wait_ge(q_sub, PAIRS * (b + 3) - 1)
                if t >= 2 or not (isinstance(b, int) and b == 0):
                    pe.wait_ge(y_out, T * b + t - 1)
                ts = slice(t * P, (t + 1) * P)
                for c in range(CH):
                    out = aps[:, t % 2, c * P:c * P + RW]
                    for k, (l, r) in enumerate(split3(pt_hi[:, c, ts], pt_lo[:, c, ts],
                                                      r_hi[:, c], r_lo[:, c])):
                        last = nc.tensor.matmul(out, l, r, start=(c == 0 and k == 0),
                                                stop=(c == CH - 1 and k == 2), skip_group_check=True)
                last.then_inc(ap_mm, 1)

            def state_sum(b, n):
                pe.wait_ge(et_lo_ok, PAIRS * b + n + 1)
                if n == 0:
                    pe.wait_ge(xt_lo_ok, b + 1)
                for t in (2 * n, 2 * n + 1):
                    for a in range(CH):
                        as_ = slice(a * P, (a + 1) * P)
                        for k, (x, e) in enumerate(split3(xt_hi[:, t, as_], xt_lo[:, t, as_],
                                                          et_hi[:, t], et_lo[:, t])):
                            last = nc.tensor.matmul(
                                sps[:, a * C:(a + 1) * C], x, e, start=(t == 0 and a == 0 and k == 0),
                                stop=(t == T - 1 and k == 2), skip_group_check=True)
                if n == PAIRS - 1:
                    last.then_inc(xe_mm, 1)

            def q_transposes(b, par, g):
                for c in range(CH):
                    n = g * CH + c
                    pe.wait_ge(k_exp, CH * b + n // 2 + 1)
                    pe.wait_ge(q_norm, NG * b + g + 1)
                    for j in range(GROUP):
                        last = nc.tensor.transpose(ring[:, n, j * P:(j + 1) * P],
                                                   qw[:, par, g * GROUP + j, c * P:(c + 1) * P], ident[:])
                    last.then_inc(pt_tr, 1)

            def e_transposes(b, n):
                pe.wait_ge(pt_lo_ok, PAIRS * b + n + 1)
                for h in range(2):
                    for c in range(CH):
                        t = 2 * n + h
                        last = nc.tensor.transpose(ring[:, n, h * C + c * P:h * C + (c + 1) * P],
                                                   ek[:, c, t * P:(t + 1) * P], ident[:])
                last.then_inc(et_tr, 1)

            def step(b, i, par, has_prev2, has_prev, has_k, has_next, has_next2):
                if has_k:
                    wait_for(pe, et_lo_ok, PAIRS * b)
                    k_product(b, par, 0, 0)
                    k_product(b, par, 0, 1)
                    k_product(b, par, 1, 0)
                else:
                    weight_sums()
                if has_prev:
                    state_product(b - 1)
                if has_k:
                    k_product(b, par, 1, 1)
                if isinstance(b, int) and b == 0:
                    folded_wo_rows()
                if has_next:
                    q_product(b + 1, 1 - par, 0)
                if has_prev:
                    state_transpose(b - 1)
                if has_next:
                    q_product(b + 1, 1 - par, 1)
                if has_prev:
                    state_project(b - 1)
                if has_next:
                    q_product(b + 1, 1 - par, 2)
                    q_product(b + 1, 1 - par, 3)
                for h in range(2):
                    for j in range(2):
                        if has_prev:
                            attend(b - 1, 4 * h + 2 * j, has_next)
                            attend(b - 1, 4 * h + 2 * j + 1, has_next)
                        if h == 1 and has_k:
                            e_transposes(b, j)
                    if has_k:
                        q_transposes(b, par, h)
                if has_k:
                    state_sum(b, 0)
                    e_transposes(b, 2)
                    state_sum(b, 1)
                    e_transposes(b, 3)
                    state_sum(b, 2)
                    state_sum(b, 3)
            batches(pe, step)
            ternary_folds()


def feed_forward_phase(nc, kept, x1_scratch, out):
    NB, _, T, _ = x1_scratch.shape
    FC, C = kept.t2.shape[1:]
    CH = C // P
    F = FC * P
    TB = 4
    TOK = TB * P
    NK = NB * T // TB
    DEPTH = 4
    LAG = 3
    POOL_SQ = 3
    assert NK % 2 == 0 and T == 2 * TB

    with ExitStack() as ctx:
        def sb(name, shape, dt=F32):
            return ctx.enter_context(nc.sbuf_tensor("ff_" + name, shape, dt))

        def sem(name):
            return ctx.enter_context(nc.semaphore("ff_" + name))

        hps = ctx.enter_context(nc.psum_tensor("hps", [P, 2, TOK], F32))
        tps = ctx.enter_context(nc.psum_tensor("tps", [P, 2, TOK], F32))
        yps = ctx.enter_context(nc.psum_tensor("yps", [P, 2, TB, C], F32))

        x1 = sb("x1", [P, 2, TB, C + 1])
        x1c = sb("x1c", [P, 2, TB, C])
        xn = sb("xn", [P, TB, C])
        ht_hi, ht_lo = sb("ht_hi", [P, 2, CH, TOK], F32R), sb("ht_lo", [P, 2, CH, TOK], F32R)
        gel = sb("gel", [P, FC, TOK])
        sq = sb("sq", [P, FC, TOK])
        a_hi, a_lo = sb("a_hi", [P, DEPTH, TOK], F32R), sb("a_lo", [P, DEPTH, TOK], F32R)
        acc = sb("acc", [P, 2, 2, TOK])
        accp = sb("accp", [P, TOK])
        z = sb("z", [P, 2, TB, C])
        t1, t2, vecs, ident, wstep, bias1 = kept.t1, kept.t2, kept.vecs, kept.ident, kept.wstep, kept.bias1
        u_row, c_row = kept.ff_u, kept.ff_c
        rs1 = sb("rs1", [P, TB])
        bnZ, mvZ, veZ, rsZ = sb("bnZ", [P, TB, 6]), sb("mvZ", [P, TB, 2]), sb("veZ", [P, TB]), sb("rsZ", [P, TB])
        nmr = sb("nmr", [P, TB])
        sums = sb("sums", [P, 2 * TB])
        nmu = sb("nmu", [P, TB])
        msq = sb("msq", [P, TB])
        var = sb("var", [P, TB])
        rsH = sb("rsH", [P, TB])
        gain = sb("gain", [P, TB])
        yc = sb("yc", [P, TB, C])
        nhalf = sb("nhalf", [P, TB])

        fence = sb("fence", [P, 1])

        x1_in = [sem(f"x1_in{n}") for n in range(2)]
        half_ok = sem("half_ok")
        n_rstd, n_ok = sem("n_rstd"), sem("n_ok")
        x1c_ok = sem("x1c_ok")
        ht_tr, ht_hi_ok, ht_lo_ok = (sem(s) for s in ("ht_tr", "ht_hi_ok", "ht_lo_ok"))
        h_mm, gelu_ok, hi_ok, lo_ok, sq_ok = (sem(s) for s in ("h_mm", "gelu_ok", "hi_ok", "lo_ok", "sq_ok"))
        y_mm = sem("y_mm")
        sum_g, sum_p, sum_q = sem("sum_g"), sem("sum_p"), sem("sum_q")
        r_tr, r_sum, r_mean, r_sq, r_var, r_eps, r_rstd, r_gain = (
            sem(s) for s in ("r_tr", "r_sum", "r_mean", "r_sq", "r_var", "r_eps", "r_rstd", "r_gain"))
        yc_ok, z_ok, z_stat, z_var, z_eps, z_rstd, z_nmr, o_ok = (
            sem(s) for s in ("yc_ok", "z_ok", "z_stat", "z_var", "z_eps", "z_rstd", "z_nmr", "o_ok"))
        o_out = [sem(f"o_out{n}") for n in range(2)]
        Q_ADDS = FC - POOL_SQ
        P_ADDS = POOL_SQ - 1

        def vec(name, c):
            return vecs[:, VEC[name][0] + c:VEC[name][0] + c + 1]

        def blocks(eng, body):
            for par in range(2):
                body(par, 0, par, par == 0, False)
            with eng.Fori(1, NK // 2 - 1) as i:
                for par in range(2):
                    body(2 * i + par, i, par, False, False)
            for par in range(2):
                body(NK - 2 + par, NK // 2 - 1, par, False, par == 1)

        def before2(k):
            return not isinstance(k, int) or k >= 2

        block = ctx.enter_context(nc.Block())

        @block.sync
        def _(sp):
            sp.dma_start(x1[:, 0], x1_scratch[0, :, 0:TB]).then_inc(x1_in[0], 16)

            def step(k, i, par, first, last):
                if not last:
                    if not first:
                        sp.wait_ge(n_ok, TB * k)
                        sp.wait_ge(x1c_ok, k)
                    src = x1_scratch[bass.ds(i, 1), :, TB:T] if par == 0 else x1_scratch[bass.ds(i + 1, 1), :, 0:TB]
                    sp.dma_start(x1[:, 1 - par], src.rearrange("o p t c -> (o p) t c")).then_inc(x1_in[1 - par], 16)
                if before2(k):
                    store(sp, k - 2, i - 1, par)

            def store(sp, k, i, par):
                dst = out.rearrange("b p t c -> (b p) t c")[bass.ds(i * P, P), par * TB:(par + 1) * TB]
                sp.wait_ge(o_ok, TB * (k + 1))
                sp.dma_start(dst, z[:, par]).then_inc(o_out[par], 16)
            blocks(sp, step)
            for par in range(2):
                store(sp, NK - 2 + par, NK // 2 - 1, par)
            for par in range(2):
                sp.wait_ge(o_out[par], 8 * NK)

        @block.gpsimd
        def _(pool):
            nc.gpsimd.memset(nhalf[:], -0.5).then_inc(half_ok, 1)
            pool.wait_ge(half_ok, 1)

            def pow_half(o, v, ready, n, done):
                pool.wait_ge(ready, n)
                nc.gpsimd.tensor_tensor(o[:], v[:], nhalf[:], ALU.pow).then_inc(done, 1)

            def keep_residual(k, par, n):
                pool.wait_ge(x1_in[par], 16 * n)
                if not (isinstance(k, int) and k < 2):
                    pool.wait_ge(z_ok, TB * (k - 1))
                nc.gpsimd.tensor_tensor(x1c[:, par], x1[:, par, :, 0:C],
                                        c_row[:].rearrange("p (o c) -> p o c", o=1).to_broadcast([P, TB, C]),
                                        ALU.add).then_inc(x1c_ok, 1)

            def norm_rstd(k, par, n):
                pool.wait_ge(x1_in[par], 16 * n)
                wait_for(pool, n_ok, TB * k)
                nc.gpsimd.tensor_tensor(rs1[:], x1[:, par, :, C], nhalf[:], ALU.pow).then_inc(n_rstd, 1)

            norm_rstd(0, 0, 1)

            def step(k, i, par, first, last):
                if not last:
                    norm_rstd(k + 1, 1 - par, i + 1 + par)
                for m in range(1, FC):
                    pool.wait_ge(gelu_ok, FC * k + m + 1)
                    if m > 1:
                        pool.wait_ge(sum_g, (FC - 1) * k + m - 1)
                    elif not (isinstance(k, int) and k < 2):
                        pool.wait_ge(r_tr, k - 1)
                    a = gel[:, 0] if m == 1 else acc[:, par, 0]
                    nc.gpsimd.tensor_tensor(acc[:, par, 0], a, gel[:, m], ALU.add).then_inc(sum_g, 1)
                    if 1 <= m < POOL_SQ:
                        pool.wait_ge(sq_ok, FC * k + m + 1)
                        if m > 1:
                            pool.wait_ge(sum_p, P_ADDS * k + m - 1)
                        elif not first:
                            pool.wait_ge(sum_q, Q_ADDS * k)
                        a = sq[:, 0] if m == 1 else accp[:]
                        nc.gpsimd.tensor_tensor(accp[:], a, sq[:, m], ALU.add).then_inc(sum_p, 1)
                    if m == 3 and not first:
                        pow_half(rsH, var, r_eps, k, r_rstd)
                    if m == 5:
                        keep_residual(k, par, i + 1)
                    if m == 7 and not first:
                        wait_for(pool, o_ok, TB * (k - 1))
                        pow_half(rsZ, veZ, z_eps, k, z_rstd)

            blocks(pool, step)
            pow_half(rsH, var, r_eps, NK, r_rstd)
            pool.wait_ge(o_ok, TB * (NK - 1))
            pow_half(rsZ, veZ, z_eps, NK, z_rstd)

        @block.scalar
        def _(act):
            def ht_high(k, par):
                for c in range(CH):
                    act.wait_ge(ht_tr, CH * k + c + 1)
                    nc.scalar.activation(ht_hi[:, par, c], tps[:, c], ACT.Copy, scale=vec("ln1_g", c)
                                         ).then_inc(ht_hi_ok, 1)

            def normalise_out(k, par, h):
                act.wait_ge(z_nmr, k + 1)
                for t in range(h * TB // 2, (h + 1) * TB // 2):
                    nc.scalar.activation(z[:, par, t], z[:, par, t], ACT.Identity, bias=nmr[:, t:t + 1],
                                         scale=rsZ[:, t:t + 1]).then_inc(o_ok, 1)

            ht_high(0, 0)

            def gelu(k, m, first):
                act.wait_ge(h_mm, FC * k + m + 1)
                if not first:
                    act.wait_ge(lo_ok, FC * (k - 1) + m + 1)
                    act.wait_ge(sum_g, (FC - 1) * (k - 1) + max(m, 1))
                nc.scalar.activation(gel[:, m], hps[:, m % 2], ACT.Gelu, bias=bias1[:, m:m + 1],
                                     scale=wstep[:, 0:1]).then_inc(gelu_ok, 1)

            def high_and_square(k, m, first):
                act.wait_ge(gelu_ok, FC * k + m + 1)
                if m >= DEPTH or not first:
                    act.wait_ge(y_mm, FC * k + m - DEPTH + 1)
                nc.scalar.activation(a_hi[:, m % DEPTH], gel[:, m], ACT.Copy, scale=vec("ln2_g", m)
                                     ).then_inc(hi_ok, 1)
                if not first:
                    if m < POOL_SQ:
                        act.wait_ge(sum_p, P_ADDS * (k - 1) + max(m, 1))
                    else:
                        act.wait_ge(sum_q, Q_ADDS * (k - 1) + max(m - POOL_SQ, 1))
                nc.scalar.activation(sq[:, m], gel[:, m], ACT.Square).then_inc(sq_ok, 1)

            def step(k, i, par, first, last):
                for m in range(FC):
                    gelu(k, m, first)
                    if m > 0:
                        high_and_square(k, m - 1, first)
                    elif not first:
                        high_and_square(k - 1, FC - 1, isinstance(k, int) and k == 1)
                    if m in (3, 5) and before2(k):
                        normalise_out(k - 2, par, (m - 3) // 2)
                    if m == 4 and not last:
                        ht_high(k + 1, 1 - par)
            blocks(act, step)
            high_and_square(NK - 1, FC - 1, False)
            for par in range(2):
                for h in range(2):
                    normalise_out(NK - 2 + par, par, h)

        @block.vector
        def _(dve):
            def norm_apply(k, par):
                dve.wait_ge(n_rstd, k + 1)
                if not (isinstance(k, int) and k == 0):
                    dve.wait_ge(ht_tr, CH * k)
                for t in range(TB):
                    nc.vector.tensor_scalar(xn[:, t], x1[:, par, t, 0:C], rs1[:, t:t + 1], None, ALU.mult
                                            ).then_inc(n_ok, 1)

            def ht_low(k, par):
                for c in range(CH):
                    dve.wait_ge(ht_hi_ok, CH * k + c + 1)
                    nc.vector.scalar_tensor_tensor(
                        out=ht_lo[:, par, c], in0=tps[:, c], scalar=vec("ln1_g", c),
                        in1=ht_hi[:, par, c].bitcast(F32), op0=ALU.mult, op1=ALU.subtract).then_inc(ht_lo_ok, 1)

            def hidden_stats(k):
                dve.wait_ge(r_tr, k + 1)
                nc.vector.tensor_reduce(sums[:], tps[:].rearrange("p a (t n) -> p (a t) n", n=P), AX_X, ALU.add
                                        ).then_inc(r_sum, 1)
                dve.wait_ge(r_sum, k + 1)
                nc.vector.tensor_scalar(nmu[:], sums[:, 0:TB], -1.0 / F, None, ALU.mult).then_inc(r_mean, 1)
                dve.wait_ge(r_mean, k + 1)
                nc.vector.tensor_tensor(msq[:], nmu[:], nmu[:], ALU.mult).then_inc(r_sq, 1)
                dve.wait_ge(r_sq, k + 1)
                nc.vector.scalar_tensor_tensor(out=var[:], in0=sums[:, TB:2 * TB], scalar=1.0 / F, in1=msq[:],
                                               op0=ALU.mult, op1=ALU.subtract).then_inc(r_var, 1)
                dve.wait_ge(r_var, k + 1)
                nc.vector.tensor_scalar(var[:], var[:], 0.0, EPS, ALU.max, ALU.add).then_inc(r_eps, 1)

            def centre_y(k, par):
                dve.wait_ge(y_mm, FC * (k + 1))
                for t in range(TB):
                    nc.vector.scalar_tensor_tensor(
                        out=yc[:, t], in0=u_row[:], scalar=nmu[:, t:t + 1], in1=yps[:, par, t],
                        op0=ALU.mult, op1=ALU.add).then_inc(yc_ok, 1)

            def residual(k, par, uses):
                dve.wait_ge(r_rstd, k + 1)
                nc.vector.tensor_scalar(gain[:], rsH[:], wstep[:, 1:2], None, ALU.mult).then_inc(r_gain, 1)
                dve.wait_ge(r_gain, k + 1)
                dve.wait_ge(yc_ok, TB * (k + 1))
                dve.wait_ge(x1c_ok, k + 1)
                if not (isinstance(uses, int) and uses == 0):
                    dve.wait_ge(o_out[par], 16 * uses)
                for t in range(TB):
                    nc.vector.scalar_tensor_tensor(
                        out=z[:, par, t], in0=yc[:, t], scalar=gain[:, t:t + 1], in1=x1c[:, par, t],
                        op0=ALU.mult, op1=ALU.add).then_inc(z_ok, 1)

            def out_stats(k, par):
                for t in range(TB):
                    dve.wait_ge(z_ok, TB * k + t + 1)
                    nc.vector.bn_stats(bnZ[:, t], z[:, par, t]).then_inc(z_stat, 1)
                dve.wait_ge(z_stat, TB * (k + 1))
                nc.vector.memset(fence[:], 0.0)
                for t in range(TB):
                    nc.vector.bn_aggr(mvZ[:, t], bnZ[:, t]).then_inc(z_var, 1)
                dve.wait_ge(z_var, TB * (k + 1))
                nc.vector.tensor_scalar(veZ[:], mvZ[:, :, 1], EPS, None, ALU.add).then_inc(z_eps, 1)

            def out_bias(k):
                dve.wait_ge(z_rstd, k + 1)
                if not (isinstance(k, int) and k == 0):
                    dve.wait_ge(o_ok, TB * k)
                nc.vector.scalar_tensor_tensor(out=nmr[:], in0=mvZ[:, :, 0], scalar=-1.0, in1=rsZ[:],
                                               op0=ALU.mult, op1=ALU.mult).then_inc(z_nmr, 1)

            norm_apply(0, 0)
            ht_low(0, 0)

            def step(k, i, par, first, last):
                for m in range(FC):
                    dve.wait_ge(hi_ok, FC * k + m + 1)
                    nc.vector.scalar_tensor_tensor(
                        out=a_lo[:, m % DEPTH], in0=gel[:, m], scalar=vec("ln2_g", m),
                        in1=a_hi[:, m % DEPTH].bitcast(F32), op0=ALU.mult, op1=ALU.subtract).then_inc(lo_ok, 1)
                    if m > POOL_SQ:
                        j = m - POOL_SQ
                        dve.wait_ge(sq_ok, FC * k + m + 1)
                        if j > 1:
                            dve.wait_ge(sum_q, Q_ADDS * k + j - 1)
                        a = sq[:, POOL_SQ] if j == 1 else acc[:, par, 1]
                        nc.vector.tensor_tensor(acc[:, par, 1], a, sq[:, m], ALU.add).then_inc(sum_q, 1)
                    if m == 1 and before2(k):
                        out_bias(k - 2)
                    if m == 0 and not last:
                        norm_apply(k + 1, 1 - par)
                    if m == 1 and not first:
                        hidden_stats(k - 1)
                    if m == 2 and not first:
                        centre_y(k - 1, 1 - par)
                    if m == 3 and not first:
                        residual(k - 1, 1 - par, i if par == 1 else i - 1)
                    if m == 4 and not last:
                        ht_low(k + 1, 1 - par)
                    if m == 5 and not first:
                        out_stats(k - 1, 1 - par)
                dve.wait_ge(sum_q, Q_ADDS * (k + 1) - 1)
                dve.wait_ge(sum_p, P_ADDS * (k + 1))
                nc.vector.tensor_tensor(acc[:, par, 1], acc[:, par, 1], accp[:], ALU.add).then_inc(sum_q, 1)
            blocks(dve, step)
            out_bias(NK - 2)
            hidden_stats(NK - 1)
            centre_y(NK - 1, 1)
            residual(NK - 1, 1, NK // 2 - 1)
            out_stats(NK - 1, 1)
            out_bias(NK - 1)

        @block.tensor
        def _(pe):
            def transposes(k):
                pe.wait_ge(n_ok, TB * (k + 1))
                for c in range(CH):
                    for t in range(TB):
                        last = nc.tensor.transpose(tps[:, c, t * P:(t + 1) * P], xn[:, t, c * P:(c + 1) * P],
                                                   ident[:])
                    last.then_inc(ht_tr, 1)

            def sum_transposes(k, par):
                pe.wait_ge(sum_g, (FC - 1) * (k + 1))
                pe.wait_ge(sum_q, Q_ADDS * (k + 1))
                for a in range(2):
                    for t in range(TB):
                        last = nc.tensor.transpose(tps[:, a, t * P:(t + 1) * P], acc[:, par, a, t * P:(t + 1) * P],
                                                   ident[:])
                last.then_inc(r_tr, 1)

            def second(k, m, par):
                pe.wait_ge(hi_ok, FC * k + m + 1)
                pe.wait_ge(lo_ok, FC * k + m + 1)
                if m == 0 and not (isinstance(k, int) and k < 2):
                    pe.wait_ge(yc_ok, TB * (k - 1))
                for t in range(TB):
                    for n, a in enumerate((a_hi, a_lo)):
                        last = nc.tensor.matmul(yps[:, par, t], a[:, m % DEPTH, t * P:(t + 1) * P], t2[:, m],
                                                start=(m == 0 and n == 0 and t % 2 == 0),
                                                stop=(m == FC - 1 and n == 1), skip_group_check=True)
                last.then_inc(y_mm, 1)

            transposes(0)

            def step(k, i, par, first, last):
                for m in range(FC):
                    if m == 0:
                        pe.wait_ge(ht_hi_ok, CH * (k + 1))
                        pe.wait_ge(ht_lo_ok, CH * (k + 1))
                    if m >= 2 or not first:
                        pe.wait_ge(gelu_ok, FC * k + m - 1)
                    for c in range(CH):
                        for n, h in enumerate((ht_hi, ht_lo)):
                            mm = nc.tensor.matmul(hps[:, m % 2], t1[:, c, m * P:(m + 1) * P], h[:, par, c],
                                                  start=(c == 0 and n == 0), stop=(c == CH - 1 and n == 1))
                    mm.then_inc(h_mm, 1)
                    if m >= LAG:
                        second(k, m - LAG, par)
                    elif not first:
                        second(k - 1, FC + m - LAG, 1 - par)
                    if m == 2 and not first:
                        sum_transposes(k - 1, 1 - par)
                    if m == 4 and not last:
                        if not first:
                            pe.wait_ge(r_sum, k)
                        transposes(k + 1)
            blocks(pe, step)
            for m in range(FC - LAG, FC):
                second(NK - 1, m, 1)
            sum_transposes(NK - 1, 1)


_INS = ["x_tok", "x_chan", "wq", "wk", "wv", "wo", "w1", "w2", "vecs", "rows", "ident", "mask"]


def program(nc, a, out):
    NB, _, T, C = a["x_tok"].shape
    x1 = nc.dram_tensor("x1_scratch", (NB, P, T, C + 1), F32, kind="Internal").ap()
    with ExitStack() as ctx:
        kept = Kept(nc, ctx, C, a["w1"].shape[2])
        attention_phase(nc, kept, a["x_tok"], a["x_chan"], a["wq"], a["wk"], a["wv"], a["wo"], a["w1"], a["w2"],
                        a["vecs"], a["rows"], a["ident"], a["mask"], x1)
        feed_forward_phase(nc, kept, x1, out)


def kernel(**inputs):
    import concourse.bacc as _bacc
    from concourse.bass_utils import run_bass_kernel_spmd as _run

    g = {k: np.asarray(v) for k, v in inputs.items()}
    x = g["L0_attn_x"]
    B, N, C = x.shape
    T = N // P
    x_tok = x.reshape(B, P, T, C)

    def kxn(w):
        wt = w.T
        return np.ascontiguousarray(wt.reshape(wt.shape[0] // P, P, wt.shape[1]).transpose(1, 0, 2))

    def col(v):
        return v.reshape(-1, P).T

    vec_of = {"bk": "L0_attn_bk", "ln_g": "L0_attn_ln_g", "ln_b": "L0_attn_ln_b", "ln1_g": "L0_ffn_ln1_g",
              "ln1_b": "L0_ffn_ln1_b", "b1": "L0_ffn_b1", "ln2_g": "L0_ffn_ln2_g", "ln2_b": "L0_ffn_ln2_b"}
    row_of = {"bq": "L0_attn_bq", "bv": "L0_attn_bv", "bo": "L0_attn_bo", "b2": "L0_ffn_b2"}
    head = np.arange(P) // 16
    arrays = {
        "x_tok": x_tok,
        "x_chan": x_tok.transpose(0, 3, 2, 1).reshape(B, C // P, P, N).transpose(0, 2, 1, 3),
        "wq": kxn(g["L0_attn_Wq"]), "wk": kxn(g["L0_attn_Wk"]), "wv": kxn(g["L0_attn_Wv"]),
        "wo": kxn(g["L0_attn_Wo"]), "w1": kxn(g["L0_ffn_w1"]), "w2": kxn(g["L0_ffn_w2"]),
        "vecs": np.concatenate([col(g[vec_of[n]]) for n in VEC], axis=1),
        "rows": np.broadcast_to(np.stack([g[row_of[n]] for n in ROW])[None], (P, len(ROW), C)),
        "ident": np.eye(P, dtype=np.float32),
        "mask": (head[:, None] == head[None, :]).astype(np.float32),
    }
    arrays = {f"in_{k}_dram": np.ascontiguousarray(v) for k, v in arrays.items()}

    nc = _bacc.Bacc("TRN2", target_bir_lowering=False, num_devices=1)
    a = {n: nc.dram_tensor(f"in_{n}_dram", arrays[f"in_{n}_dram"].shape, F32, kind="ExternalInput").ap()
         for n in _INS}
    out = nc.dram_tensor("out_0_dram", (B, P, T, C), F32, kind="ExternalOutput").ap()
    program(nc, a, out)
    r = _run(nc, [arrays], core_ids=[0])
    return r.results[0]["out_0_dram"].reshape(B, N, C)
```
